# Optimizing a Trainium2 kernel written in Bass

```python
import numpy as np
import jax
import jax.numpy as jnp

def _softmax(x, axis=-1):
    return jax.nn.softmax(x, axis=axis)

def _gelu(x):
    return jax.nn.gelu(x, approximate=True)

def _silu(x):
    return jax.nn.silu(x)

def _sigmoid(x):
    return jax.nn.sigmoid(x)

def _layernorm(x, axis=-1, eps=1e-05):
    m = jnp.mean(x, axis=axis, keepdims=True)
    v = jnp.var(x, axis=axis, keepdims=True)
    return (x - m) / jnp.sqrt(v + eps)

def _scatter_add(tgt, idx, src, axis=0):
    return tgt.at[idx].add(src)

def _segment_sum(src, seg, n):
    return jax.ops.segment_sum(src, seg, n)
kernel_name = 'mk_pixart_seq_d4_seqx_r8_194ec7'

def setup_inputs(seed: int=0):
    np.random.seed(seed)
    _w = jnp.asarray

    def _rec_inputs():
        import jax
        import jax.numpy as jnp
        _rk = jax.random.key(seed)
        x = -0.0002928 + 1 * jax.random.normal(jax.random.fold_in(_rk, 1), (4, 512, 128), jnp.float32)
        _lenS = 512 - jax.random.randint(jax.random.fold_in(_rk, 7), (4,), 0, max(1, 512 // 4) + 1, jnp.int32)
        _lenS2 = 77 - jax.random.randint(jax.random.fold_in(_rk, 8), (4,), 0, max(1, 77 // 4) + 1, jnp.int32)
        cond_1024 = 0.000887014 + 1.03683 * jax.random.normal(jax.random.fold_in(_rk, 11), (4, 128), jnp.float32)
        _ctx_1024P = jax.random.normal(jax.random.fold_in(_rk, 12), (4, 16, 128), jnp.float32)
        _ctx_1024c = jax.random.dirichlet(jax.random.fold_in(_rk, 512), 0.3 * jnp.ones((16,), jnp.float32), (4, 77))
        _ctx_1024t = jnp.einsum('bsk,bkd->bsd', _ctx_1024c, _ctx_1024P)
        _ctx_1024t = _ctx_1024t * jax.lax.rsqrt(jnp.mean(jnp.square(_ctx_1024t)) + 1e-12) * 0.953939
        ctx_1024 = -0.00606593 + 0.997213 * (_ctx_1024t + 0.3 * jax.random.normal(jax.random.fold_in(_rk, 612), (4, 77, 128), jnp.float32))
        _validS = jnp.arange(512)[None, :] < _lenS[:, None]
        _validS2 = jnp.arange(77)[None, :] < _lenS2[:, None]
        _causal = jnp.tril(jnp.ones((512, 512), dtype=bool))
        mask_BxS2_bf1 = jnp.ones((4, 77), dtype=bool)
        mask_SxS_bk0 = jnp.logical_not(jnp.broadcast_to(_validS[0:1, :], (512, 512)))
        return (x, cond_1024, ctx_1024, mask_BxS2_bf1, mask_SxS_bk0)
    x, cond_1024, ctx_1024, mask_BxS2_bf1, mask_SxS_bk0 = _rec_inputs()

    def _L0_xcond_setup():
        import jax, jax.numpy as jnp
        import numpy as np
        B, N, D, H, LC = (2, 128, 128, 16, 77)
        HD = D // H
        BLOCK = 16
        ROPE_BASE = 10000.0
        EPS = 1e-05

        def _block_diff_mask(n, block_size):
            idx = np.arange(2 * n)
            q = idx[:, None]
            kv = idx[None, :]
            fq = q >= n
            fkv = kv >= n
            bq = np.where(fq, (q - n) // block_size, q // block_size)
            bkv = np.where(fkv, (kv - n) // block_size, kv // block_size)
            block_diagonal = (bq == bkv) & (fq == fkv)
            offset_block_causal = (bq > bkv) & fkv & ~fq
            block_causal = (bq >= bkv) & fq & fkv
            return jnp.asarray(block_diagonal | offset_block_causal | block_causal)

        def _rope_tables(n):
            inv_freq = 1.0 / ROPE_BASE ** (np.arange(0, HD, 2, dtype=np.float32) / HD)
            freqs = np.outer(np.arange(n, dtype=np.float32), inv_freq)
            emb = np.concatenate([freqs, freqs], axis=-1)
            cos = jnp.asarray(np.cos(emb), jnp.float32)[None, :, None, :]
            sin = jnp.asarray(np.sin(emb), jnp.float32)[None, :, None, :]
            return (cos, sin)

        def _ln(x, w):
            xf = x.astype(jnp.float32)
            mu = jnp.mean(xf, axis=-1, keepdims=True)
            var = jnp.mean(jnp.square(xf - mu), axis=-1, keepdims=True)
            y = (xf - mu) * jax.lax.rsqrt(var + EPS)
            return y * w[None, None, :]

        def _apply_rope(t, cos, sin):
            t1, t2 = jnp.split(t, 2, axis=-1)
            rot = jnp.concatenate([-t2, t1], axis=-1)
            return t * cos + rot * sin

        def _attn(q, k, v, mask):
            scale = 1.0 / np.sqrt(HD)
            s = jnp.einsum('bqhd,bkhd->bhqk', q, k) * scale
            s = jnp.where(mask, s, jnp.finfo(s.dtype).min)
            a = jax.nn.softmax(s, axis=-1)
            return jnp.einsum('bhqk,bkhd->bqhd', a, v)
        key = jax.random.key(seed)
        ks = jax.random.split(key, 16)
        w = lambda k, shp: jax.random.normal(k, shp, jnp.float32) * 0.02
        inp = {'x': jax.random.normal(ks[0], (B, 2 * N, D), jnp.float32), 'cond_global': jax.random.normal(ks[1], (B, D), jnp.float32), 'cond_tokens': jax.random.normal(ks[2], (B, LC, D), jnp.float32), 'adaLN_W': w(ks[3], (D, 9 * D)), 'adaLN_b': w(ks[4], (9 * D,)), 'norm1_w': jnp.ones((D,), jnp.float32), 'qkv_W': w(ks[5], (D, 3 * D)), 'attn_out_W': w(ks[6], (D, D)), 'normc_w': jnp.ones((D,), jnp.float32), 'cq_W': w(ks[7], (D, D)), 'ck_W': w(ks[8], (D, D)), 'cv_W': w(ks[9], (D, D)), 'co_W': w(ks[10], (D, D)), 'norm2_w': jnp.ones((D,), jnp.float32), 'mlp_W1': w(ks[11], (D, 4 * D)), 'mlp_b1': w(ks[12], (4 * D,)), 'mlp_W2': w(ks[13], (4 * D, D)), 'mlp_b2': w(ks[14], (D,)), 'cond_kv_mask': jnp.ones((B, LC), bool), 'attn_mask': _block_diff_mask(N, BLOCK)}
        return inp
    _L0_xcond_all = _L0_xcond_setup()
    _L0_xcond_in = {k: v for k, v in _L0_xcond_all.items() if k in ('adaLN_W', 'adaLN_b', 'norm1_w', 'qkv_W', 'attn_out_W', 'normc_w', 'cq_W', 'ck_W', 'cv_W', 'co_W', 'norm2_w', 'mlp_W1', 'mlp_b1', 'mlp_W2', 'mlp_b2')}
    del _L0_xcond_all

    def _L1_xcond_setup():
        import jax, jax.numpy as jnp
        import numpy as np
        H = 128
        RH = 2 * H
        E = 3
        B, T, P = (8, 256, 64)
        LN_EPS = 1e-05

        def _layer_norm(x, gamma, beta):
            mu = jnp.mean(x, axis=-1, keepdims=True)
            var = jnp.mean(jnp.square(x - mu), axis=-1, keepdims=True)
            return (x - mu) * jax.lax.rsqrt(var + LN_EPS) * gamma + beta
        key = jax.random.key(seed)
        ks = jax.random.split(key, 24)
        s = lambda fan_in: 1.0 / np.sqrt(fan_in)
        inp = {'mix_hidden_states': jax.random.normal(ks[0], (B, T, H), jnp.float32), 'global_anchor': jax.random.normal(ks[1], (B, H), jnp.float32), 'prototype_bank': jax.random.normal(ks[2], (B, P, H), jnp.float32), 'ln_gamma': jnp.ones((H,), jnp.float32), 'ln_beta': jnp.zeros((H,), jnp.float32), 'Wq': jax.random.normal(ks[3], (H, H), jnp.float32) * s(H), 'Wk': jax.random.normal(ks[4], (H, H), jnp.float32) * s(H), 'Wv': jax.random.normal(ks[5], (H, H), jnp.float32) * s(H), 'router_W': jax.random.normal(ks[6], (3 * H, E), jnp.float32) * s(3 * H), 'router_b': jnp.zeros((E,), jnp.float32), 'e_w1': jax.random.normal(ks[7], (E, 3 * H, RH), jnp.float32) * s(3 * H), 'e_b1': jnp.zeros((E, RH), jnp.float32), 'e_w2': jax.random.normal(ks[8], (E, RH, H), jnp.float32) * s(RH), 'e_b2': jnp.zeros((E, H), jnp.float32), 'gate_w1': jax.random.normal(ks[9], (3 * H, H), jnp.float32) * s(3 * H), 'gate_b1': jnp.zeros((H,), jnp.float32), 'gate_w2': jax.random.normal(ks[10], (H, H), jnp.float32) * s(H), 'gate_b2': jnp.zeros((H,), jnp.float32), 'out_w': jax.random.normal(ks[11], (H, H), jnp.float32) * s(H), 'out_b': jnp.zeros((H,), jnp.float32)}
        return inp
    _L1_xcond_all = _L1_xcond_setup()
    _L1_xcond_in = {k: v for k, v in _L1_xcond_all.items() if k in ('ln_gamma', 'ln_beta', 'Wq', 'Wk', 'Wv', 'router_W', 'router_b', 'e_w1', 'e_b1', 'e_w2', 'e_b2', 'gate_w1', 'gate_b1', 'gate_w2', 'gate_b2', 'out_w', 'out_b')}
    del _L1_xcond_all

    def _L2_xcond_setup():
        import jax, jax.numpy as jnp
        import numpy as np
        EPS = 1e-05

        def _ada_ln(x, c, W_ss, b_ss):
            mu = jnp.mean(x, axis=-1, keepdims=True)
            var = jnp.mean((x - mu) ** 2, axis=-1, keepdims=True)
            h = (x - mu) / jnp.sqrt(var + EPS)
            ss = jax.nn.silu(c) @ W_ss + b_ss
            scale, bias = jnp.split(ss, 2, axis=-1)
            return (1.0 + scale)[:, None, :] * h + bias[:, None, :]
        key = jax.random.key(seed)
        ks = jax.random.split(key, 12)
        B, Lq, Lkv, H = (8, 256, 64, 128)
        s = 0.02
        return {'x_q': jax.random.normal(ks[0], (B, Lq, H), jnp.float32), 'x_kv': jax.random.normal(ks[1], (B, Lkv, H), jnp.float32), 't_vec': jax.random.normal(ks[2], (B, H), jnp.float32), 'Wq': jax.random.normal(ks[3], (H, H), jnp.float32) * s, 'bq': jnp.zeros((H,), jnp.float32), 'Wkv': jax.random.normal(ks[4], (H, 2 * H), jnp.float32) * s, 'bkv': jnp.zeros((2 * H,), jnp.float32), 'Wp': jax.random.normal(ks[5], (H, H), jnp.float32) * s, 'bp': jnp.zeros((H,), jnp.float32), 'Wss_q': jax.random.normal(ks[6], (H, 2 * H), jnp.float32) * s, 'bss_q': jnp.zeros((2 * H,), jnp.float32), 'Wss_kv': jax.random.normal(ks[7], (H, 2 * H), jnp.float32) * s, 'bss_kv': jnp.zeros((2 * H,), jnp.float32)}
    _L2_xcond_all = _L2_xcond_setup()
    _L2_xcond_in = {k: v for k, v in _L2_xcond_all.items() if k in ('Wq', 'bq', 'Wkv', 'bkv', 'Wp', 'bp', 'Wss_q', 'bss_q', 'Wss_kv', 'bss_kv')}
    del _L2_xcond_all

    def _L3_xcond_setup():
        import jax, jax.numpy as jnp
        import numpy as np
        LN_EPS = 1e-06

        def _ln(x):
            mu = jnp.mean(x, axis=-1, keepdims=True)
            var = jnp.var(x, axis=-1, keepdims=True)
            return (x - mu) * jax.lax.rsqrt(var + LN_EPS)
        key = jax.random.key(seed)
        H, NH = (128, 16)
        B, N, S = (4, 128, 77)
        MLP = int(H * 4.0)
        ks = jax.random.split(key, 20)
        s = 1.0 / np.sqrt(H)
        return {'x': jax.random.normal(ks[0], (B, N, H), jnp.float32), 'c': jax.random.normal(ks[1], (B, H), jnp.float32), 'context': jax.random.normal(ks[2], (B, S, H), jnp.float32), 'W_mod': jax.random.normal(ks[3], (H, 6 * H), jnp.float32) * s, 'b_mod': jnp.zeros((6 * H,), jnp.float32), 'W_qkv': jax.random.normal(ks[4], (H, 3 * H), jnp.float32) * s, 'b_qkv': jnp.zeros((3 * H,), jnp.float32), 'W_proj': jax.random.normal(ks[5], (H, H), jnp.float32) * s, 'b_proj': jnp.zeros((H,), jnp.float32), 'W_qc': jax.random.normal(ks[6], (H, H), jnp.float32) * s, 'b_qc': jnp.zeros((H,), jnp.float32), 'W_kvc': jax.random.normal(ks[7], (H, 2 * H), jnp.float32) * s, 'b_kvc': jnp.zeros((2 * H,), jnp.float32), 'W_cproj': jax.random.normal(ks[8], (H, H), jnp.float32) * s, 'b_cproj': jnp.zeros((H,), jnp.float32), 'W_mlp1': jax.random.normal(ks[9], (H, MLP), jnp.float32) * s, 'b_mlp1': jnp.zeros((MLP,), jnp.float32), 'W_mlp2': jax.random.normal(ks[10], (MLP, H), jnp.float32) * (1.0 / np.sqrt(MLP)), 'b_mlp2': jnp.zeros((H,), jnp.float32)}
    _L3_xcond_all = _L3_xcond_setup()
    _L3_xcond_in = {k: v for k, v in _L3_xcond_all.items() if k in ('W_mod', 'b_mod', 'W_qkv', 'b_qkv', 'W_proj', 'b_proj', 'W_qc', 'b_qc', 'W_kvc', 'b_kvc', 'W_cproj', 'b_cproj', 'W_mlp1', 'b_mlp1', 'W_mlp2', 'b_mlp2')}
    del _L3_xcond_all
    return {'x': x, 'cond_1024': cond_1024, 'ctx_1024': ctx_1024, 'mask_BxS2_bf1': mask_BxS2_bf1, 'mask_SxS_bk0': mask_SxS_bk0, 'L0_xcond_adaLN_W': _L0_xcond_in['adaLN_W'], 'L0_xcond_adaLN_b': _L0_xcond_in['adaLN_b'], 'L0_xcond_norm1_w': _L0_xcond_in['norm1_w'], 'L0_xcond_qkv_W': _L0_xcond_in['qkv_W'], 'L0_xcond_attn_out_W': _L0_xcond_in['attn_out_W'], 'L0_xcond_normc_w': _L0_xcond_in['normc_w'], 'L0_xcond_cq_W': _L0_xcond_in['cq_W'], 'L0_xcond_ck_W': _L0_xcond_in['ck_W'], 'L0_xcond_cv_W': _L0_xcond_in['cv_W'], 'L0_xcond_co_W': _L0_xcond_in['co_W'], 'L0_xcond_norm2_w': _L0_xcond_in['norm2_w'], 'L0_xcond_mlp_W1': _L0_xcond_in['mlp_W1'], 'L0_xcond_mlp_b1': _L0_xcond_in['mlp_b1'], 'L0_xcond_mlp_W2': _L0_xcond_in['mlp_W2'], 'L0_xcond_mlp_b2': _L0_xcond_in['mlp_b2'], 'L1_xcond_ln_gamma': _L1_xcond_in['ln_gamma'], 'L1_xcond_ln_beta': _L1_xcond_in['ln_beta'], 'L1_xcond_Wq': _L1_xcond_in['Wq'], 'L1_xcond_Wk': _L1_xcond_in['Wk'], 'L1_xcond_Wv': _L1_xcond_in['Wv'], 'L1_xcond_router_W': _L1_xcond_in['router_W'], 'L1_xcond_router_b': _L1_xcond_in['router_b'], 'L1_xcond_e_w1': _L1_xcond_in['e_w1'], 'L1_xcond_e_b1': _L1_xcond_in['e_b1'], 'L1_xcond_e_w2': _L1_xcond_in['e_w2'], 'L1_xcond_e_b2': _L1_xcond_in['e_b2'], 'L1_xcond_gate_w1': _L1_xcond_in['gate_w1'], 'L1_xcond_gate_b1': _L1_xcond_in['gate_b1'], 'L1_xcond_gate_w2': _L1_xcond_in['gate_w2'], 'L1_xcond_gate_b2': _L1_xcond_in['gate_b2'], 'L1_xcond_out_w': _L1_xcond_in['out_w'], 'L1_xcond_out_b': _L1_xcond_in['out_b'], 'L2_xcond_Wq': _L2_xcond_in['Wq'], 'L2_xcond_bq': _L2_xcond_in['bq'], 'L2_xcond_Wkv': _L2_xcond_in['Wkv'], 'L2_xcond_bkv': _L2_xcond_in['bkv'], 'L2_xcond_Wp': _L2_xcond_in['Wp'], 'L2_xcond_bp': _L2_xcond_in['bp'], 'L2_xcond_Wss_q': _L2_xcond_in['Wss_q'], 'L2_xcond_bss_q': _L2_xcond_in['bss_q'], 'L2_xcond_Wss_kv': _L2_xcond_in['Wss_kv'], 'L2_xcond_bss_kv': _L2_xcond_in['bss_kv'], 'L3_xcond_W_mod': _L3_xcond_in['W_mod'], 'L3_xcond_b_mod': _L3_xcond_in['b_mod'], 'L3_xcond_W_qkv': _L3_xcond_in['W_qkv'], 'L3_xcond_b_qkv': _L3_xcond_in['b_qkv'], 'L3_xcond_W_proj': _L3_xcond_in['W_proj'], 'L3_xcond_b_proj': _L3_xcond_in['b_proj'], 'L3_xcond_W_qc': _L3_xcond_in['W_qc'], 'L3_xcond_b_qc': _L3_xcond_in['b_qc'], 'L3_xcond_W_kvc': _L3_xcond_in['W_kvc'], 'L3_xcond_b_kvc': _L3_xcond_in['b_kvc'], 'L3_xcond_W_cproj': _L3_xcond_in['W_cproj'], 'L3_xcond_b_cproj': _L3_xcond_in['b_cproj'], 'L3_xcond_W_mlp1': _L3_xcond_in['W_mlp1'], 'L3_xcond_b_mlp1': _L3_xcond_in['b_mlp1'], 'L3_xcond_W_mlp2': _L3_xcond_in['W_mlp2'], 'L3_xcond_b_mlp2': _L3_xcond_in['b_mlp2']}

def reference(x, cond_1024, ctx_1024, mask_BxS2_bf1, mask_SxS_bk0, L0_xcond_adaLN_W, L0_xcond_adaLN_b, L0_xcond_norm1_w, L0_xcond_qkv_W, L0_xcond_attn_out_W, L0_xcond_normc_w, L0_xcond_cq_W, L0_xcond_ck_W, L0_xcond_cv_W, L0_xcond_co_W, L0_xcond_norm2_w, L0_xcond_mlp_W1, L0_xcond_mlp_b1, L0_xcond_mlp_W2, L0_xcond_mlp_b2, L1_xcond_ln_gamma, L1_xcond_ln_beta, L1_xcond_Wq, L1_xcond_Wk, L1_xcond_Wv, L1_xcond_router_W, L1_xcond_router_b, L1_xcond_e_w1, L1_xcond_e_b1, L1_xcond_e_w2, L1_xcond_e_b2, L1_xcond_gate_w1, L1_xcond_gate_b1, L1_xcond_gate_w2, L1_xcond_gate_b2, L1_xcond_out_w, L1_xcond_out_b, L2_xcond_Wq, L2_xcond_bq, L2_xcond_Wkv, L2_xcond_bkv, L2_xcond_Wp, L2_xcond_bp, L2_xcond_Wss_q, L2_xcond_bss_q, L2_xcond_Wss_kv, L2_xcond_bss_kv, L3_xcond_W_mod, L3_xcond_b_mod, L3_xcond_W_qkv, L3_xcond_b_qkv, L3_xcond_W_proj, L3_xcond_b_proj, L3_xcond_W_qc, L3_xcond_b_qc, L3_xcond_W_kvc, L3_xcond_b_kvc, L3_xcond_W_cproj, L3_xcond_b_cproj, L3_xcond_W_mlp1, L3_xcond_b_mlp1, L3_xcond_W_mlp2, L3_xcond_b_mlp2):
    import jax
    import jax.numpy as jnp

    def _L0_xcond_ref(x, cond_global, cond_tokens, adaLN_W, adaLN_b, norm1_w, qkv_W, attn_out_W, normc_w, cq_W, ck_W, cv_W, co_W, norm2_w, mlp_W1, mlp_b1, mlp_W2, mlp_b2, cond_kv_mask, attn_mask):
        import jax, jax.numpy as jnp
        import numpy as np
        B, N, D, H, LC = (2, 128, 128, 16, 77)
        HD = D // H
        BLOCK = 16
        ROPE_BASE = 10000.0
        EPS = 1e-05

        def _block_diff_mask(n, block_size):
            idx = np.arange(2 * n)
            q = idx[:, None]
            kv = idx[None, :]
            fq = q >= n
            fkv = kv >= n
            bq = np.where(fq, (q - n) // block_size, q // block_size)
            bkv = np.where(fkv, (kv - n) // block_size, kv // block_size)
            block_diagonal = (bq == bkv) & (fq == fkv)
            offset_block_causal = (bq > bkv) & fkv & ~fq
            block_causal = (bq >= bkv) & fq & fkv
            return jnp.asarray(block_diagonal | offset_block_causal | block_causal)

        def _rope_tables(n):
            inv_freq = 1.0 / ROPE_BASE ** (np.arange(0, HD, 2, dtype=np.float32) / HD)
            freqs = np.outer(np.arange(n, dtype=np.float32), inv_freq)
            emb = np.concatenate([freqs, freqs], axis=-1)
            cos = jnp.asarray(np.cos(emb), jnp.float32)[None, :, None, :]
            sin = jnp.asarray(np.sin(emb), jnp.float32)[None, :, None, :]
            return (cos, sin)

        def _ln(x, w):
            xf = x.astype(jnp.float32)
            mu = jnp.mean(xf, axis=-1, keepdims=True)
            var = jnp.mean(jnp.square(xf - mu), axis=-1, keepdims=True)
            y = (xf - mu) * jax.lax.rsqrt(var + EPS)
            return y * w[None, None, :]

        def _apply_rope(t, cos, sin):
            t1, t2 = jnp.split(t, 2, axis=-1)
            rot = jnp.concatenate([-t2, t1], axis=-1)
            return t * cos + rot * sin

        def _attn(q, k, v, mask):
            scale = 1.0 / np.sqrt(HD)
            s = jnp.einsum('bqhd,bkhd->bhqk', q, k) * scale
            s = jnp.where(mask, s, jnp.finfo(s.dtype).min)
            a = jax.nn.softmax(s, axis=-1)
            return jnp.einsum('bhqk,bkhd->bqhd', a, v)
        b, s, d = x.shape
        n = s // 2
        mod = (cond_global @ adaLN_W + adaLN_b)[:, None, :]
        sh_msa, sc_msa, g_msa, sh_x, sc_x, g_x, sh_mlp, sc_mlp, g_mlp = jnp.split(mod, 9, axis=-1)
        x_norm = _ln(x, norm1_w) * (1 + sc_msa) + sh_msa
        cos, sin = _rope_tables(n)

        def qkv(h):
            t = (h @ qkv_W).reshape(b, n, 3, H, HD)
            q, k, v = (t[:, :, 0], t[:, :, 1], t[:, :, 2])
            return (_apply_rope(q, cos, sin), _apply_rope(k, cos, sin), v)
        q1, k1, v1 = qkv(x_norm[:, :n])
        q2, k2, v2 = qkv(x_norm[:, n:])
        q = jnp.concatenate([q1, q2], axis=1)
        k = jnp.concatenate([k1, k2], axis=1)
        v = jnp.concatenate([v1, v2], axis=1)
        self_out = _attn(q, k, v, attn_mask[None, None]).reshape(b, s, d) @ attn_out_W
        x = x + g_msa * self_out
        xc = _ln(x, normc_w) * (1 + sc_x) + sh_x
        qc = (xc @ cq_W).reshape(b, s, H, HD)
        kc = (cond_tokens @ ck_W).reshape(b, LC, H, HD)
        vc = (cond_tokens @ cv_W).reshape(b, LC, H, HD)
        cross = _attn(qc, kc, vc, cond_kv_mask[:, None, None, :]).reshape(b, s, d) @ co_W
        x = x + g_x * cross
        xm = _ln(x, norm2_w) * (1 + sc_mlp) + sh_mlp
        h = jax.nn.gelu(xm @ mlp_W1 + mlp_b1, approximate=True)
        mlp_out = h @ mlp_W2 + mlp_b2
        return x + g_mlp * mlp_out

    def _L1_xcond_ref(mix_hidden_states, global_anchor, prototype_bank, ln_gamma, ln_beta, Wq, Wk, Wv, router_W, router_b, e_w1, e_b1, e_w2, e_b2, gate_w1, gate_b1, gate_w2, gate_b2, out_w, out_b):
        import jax, jax.numpy as jnp
        import numpy as np
        H = 128
        RH = 2 * H
        E = 3
        B, T, P = (8, 256, 64)
        LN_EPS = 1e-05

        def _layer_norm(x, gamma, beta):
            mu = jnp.mean(x, axis=-1, keepdims=True)
            var = jnp.mean(jnp.square(x - mu), axis=-1, keepdims=True)
            return (x - mu) * jax.lax.rsqrt(var + LN_EPS) * gamma + beta
        x = mix_hidden_states
        nx = _layer_norm(x, ln_gamma, ln_beta)
        q = nx @ Wq
        k = prototype_bank @ Wk
        v = prototype_bank @ Wv
        scores = jnp.einsum('bth,bph->btp', q, k) * H ** (-0.5)
        weights = jax.nn.softmax(scores, axis=-1)
        evidence = jnp.einsum('btp,bph->bth', weights, v)
        anchor = jnp.broadcast_to(global_anchor[:, None, :], nx.shape)
        combined = jnp.concatenate([nx, evidence, anchor], axis=-1)
        router_logits = combined @ router_W + router_b
        router_probs = jax.nn.softmax(router_logits, axis=-1)
        h = jax.nn.silu(jnp.einsum('btc,ecr->bter', combined, e_w1) + e_b1)
        expert_out = jnp.einsum('bter,erh->bteh', h, e_w2) + e_b2
        routed = jnp.sum(expert_out * router_probs[..., None], axis=-2)
        g = jax.nn.sigmoid(jax.nn.silu(combined @ gate_w1 + gate_b1) @ gate_w2 + gate_b2)
        refined_delta = g * (routed @ out_w + out_b)
        return x + refined_delta

    def _L2_xcond_ref(x_q, x_kv, t_vec, Wq, bq, Wkv, bkv, Wp, bp, Wss_q, bss_q, Wss_kv, bss_kv):
        import jax, jax.numpy as jnp
        import numpy as np
        EPS = 1e-05

        def _ada_ln(x, c, W_ss, b_ss):
            mu = jnp.mean(x, axis=-1, keepdims=True)
            var = jnp.mean((x - mu) ** 2, axis=-1, keepdims=True)
            h = (x - mu) / jnp.sqrt(var + EPS)
            ss = jax.nn.silu(c) @ W_ss + b_ss
            scale, bias = jnp.split(ss, 2, axis=-1)
            return (1.0 + scale)[:, None, :] * h + bias[:, None, :]
        B, Lq, H = x_q.shape
        Lkv = x_kv.shape[1]
        nh = 16
        dh = H // nh
        xq = _ada_ln(x_q, t_vec, Wss_q, bss_q)
        xkv = _ada_ln(x_kv, t_vec, Wss_kv, bss_kv)
        q = (xq @ Wq + bq).reshape(B, Lq, nh, dh)
        kv = (xkv @ Wkv + bkv).reshape(B, Lkv, 2, nh, dh)
        k = kv[:, :, 0]
        v = kv[:, :, 1]
        scores = jnp.einsum('bqhd,bkhd->bhqk', q, k) / jnp.sqrt(jnp.float32(dh))
        attn = jax.nn.softmax(scores, axis=-1)
        out = jnp.einsum('bhqk,bkhd->bqhd', attn, v).reshape(B, Lq, H)
        return x_q + (out @ Wp + bp)

    def _L3_xcond_ref(x, c, context, W_mod, b_mod, W_qkv, b_qkv, W_proj, b_proj, W_qc, b_qc, W_kvc, b_kvc, W_cproj, b_cproj, W_mlp1, b_mlp1, W_mlp2, b_mlp2):
        import jax, jax.numpy as jnp
        import numpy as np
        LN_EPS = 1e-06

        def _ln(x):
            mu = jnp.mean(x, axis=-1, keepdims=True)
            var = jnp.var(x, axis=-1, keepdims=True)
            return (x - mu) * jax.lax.rsqrt(var + LN_EPS)
        B, N, H = x.shape
        NH = 16
        hd = H // NH
        scale = hd ** (-0.5)
        c_proj = jax.nn.silu(c) @ W_mod + b_mod
        shift_a, scale_a, gate_a, shift_m, scale_m, gate_m = jnp.split(c_proj, 6, axis=-1)

        def modulate(t, shift, sc):
            return t * (1 + sc[:, None]) + shift[:, None]
        x_norm = modulate(_ln(x), shift_a, scale_a)
        qkv = x_norm @ W_qkv + b_qkv
        q, k, v = jnp.split(qkv, 3, axis=-1)
        q = q.reshape(B, N, NH, hd).transpose(0, 2, 1, 3)
        k = k.reshape(B, N, NH, hd).transpose(0, 2, 1, 3)
        v = v.reshape(B, N, NH, hd).transpose(0, 2, 1, 3)
        attn_w = jax.nn.softmax(jnp.einsum('bhqd,bhkd->bhqk', q, k) * scale, axis=-1)
        attn_out = jnp.einsum('bhqk,bhkd->bhqd', attn_w, v)
        attn_out = attn_out.transpose(0, 2, 1, 3).reshape(B, N, H)
        attn_out = attn_out @ W_proj + b_proj
        x = x + gate_a[:, None] * attn_out
        S = context.shape[1]
        q_c = _ln(x) @ W_qc + b_qc
        kv_c = _ln(context) @ W_kvc + b_kvc
        k_c, v_c = jnp.split(kv_c, 2, axis=-1)
        q_c = q_c.reshape(B, N, NH, hd).transpose(0, 2, 1, 3)
        k_c = k_c.reshape(B, S, NH, hd).transpose(0, 2, 1, 3)
        v_c = v_c.reshape(B, S, NH, hd).transpose(0, 2, 1, 3)
        c_attn_w = jax.nn.softmax(jnp.einsum('bhqd,bhsd->bhqs', q_c, k_c) * scale, axis=-1)
        c_attn_out = jnp.einsum('bhqs,bhsd->bhqd', c_attn_w, v_c)
        c_attn_out = c_attn_out.transpose(0, 2, 1, 3).reshape(B, N, H)
        c_attn_out = c_attn_out @ W_cproj + b_cproj
        x = x + c_attn_out
        x_norm2 = modulate(_ln(x), shift_m, scale_m)
        h = jax.nn.gelu(x_norm2 @ W_mlp1 + b_mlp1)
        h = h @ W_mlp2 + b_mlp2
        x = x + gate_m[:, None] * h
        return x
    x = _L0_xcond_ref(x, cond_1024, ctx_1024, L0_xcond_adaLN_W, L0_xcond_adaLN_b, L0_xcond_norm1_w, L0_xcond_qkv_W, L0_xcond_attn_out_W, L0_xcond_normc_w, L0_xcond_cq_W, L0_xcond_ck_W, L0_xcond_cv_W, L0_xcond_co_W, L0_xcond_norm2_w, L0_xcond_mlp_W1, L0_xcond_mlp_b1, L0_xcond_mlp_W2, L0_xcond_mlp_b2, mask_BxS2_bf1, mask_SxS_bk0)
    x = _L1_xcond_ref(x, cond_1024, ctx_1024, L1_xcond_ln_gamma, L1_xcond_ln_beta, L1_xcond_Wq, L1_xcond_Wk, L1_xcond_Wv, L1_xcond_router_W, L1_xcond_router_b, L1_xcond_e_w1, L1_xcond_e_b1, L1_xcond_e_w2, L1_xcond_e_b2, L1_xcond_gate_w1, L1_xcond_gate_b1, L1_xcond_gate_w2, L1_xcond_gate_b2, L1_xcond_out_w, L1_xcond_out_b)
    x = _L2_xcond_ref(x, ctx_1024, cond_1024, L2_xcond_Wq, L2_xcond_bq, L2_xcond_Wkv, L2_xcond_bkv, L2_xcond_Wp, L2_xcond_bp, L2_xcond_Wss_q, L2_xcond_bss_q, L2_xcond_Wss_kv, L2_xcond_bss_kv)
    x = _L3_xcond_ref(x, cond_1024, ctx_1024, L3_xcond_W_mod, L3_xcond_b_mod, L3_xcond_W_qkv, L3_xcond_b_qkv, L3_xcond_W_proj, L3_xcond_b_proj, L3_xcond_W_qc, L3_xcond_b_qc, L3_xcond_W_kvc, L3_xcond_b_kvc, L3_xcond_W_cproj, L3_xcond_b_cproj, L3_xcond_W_mlp1, L3_xcond_b_mlp1, L3_xcond_W_mlp2, L3_xcond_b_mlp2)
    return x

_drawn_inputs = setup_inputs


def setup_inputs(seed=0):
    import zlib

    import numpy as np

    out = dict(_drawn_inputs(seed))
    spreads = {'L0_xcond_norm1_w': (1.0, 0.6),
     'L0_xcond_normc_w': (1.0, 0.6),
     'L0_xcond_norm2_w': (1.0, 0.6),
     'L1_xcond_ln_gamma': (1.0, 0.6),
     'L1_xcond_ln_beta': (0.0, 2.0),
     'L1_xcond_router_b': (0.0, 2.0),
     'L1_xcond_e_b1': (0.0, 2.0),
     'L1_xcond_e_b2': (0.0, 0.8),
     'L1_xcond_gate_b1': (0.0, 2.0),
     'L1_xcond_gate_b2': (0.0, 2.0),
     'L1_xcond_out_b': (0.0, 0.8),
     'L2_xcond_bq': (0.0, 2.0),
     'L2_xcond_bkv': (0.0, 2.0),
     'L2_xcond_bp': (0.0, 0.647),
     'L2_xcond_bss_q': (0.0, 2.0),
     'L2_xcond_bss_kv': (0.0, 2.0),
     'L3_xcond_b_mod': (0.0, 0.385),
     'L3_xcond_b_qkv': (0.0, 0.8),
     'L3_xcond_b_proj': (0.0, 0.8),
     'L3_xcond_b_qc': (0.0, 2.0),
     'L3_xcond_b_kvc': (0.0, 0.73),
     'L3_xcond_b_cproj': (0.0, 0.728),
     'L3_xcond_b_mlp1': (0.0, 1.578),
     'L3_xcond_b_mlp2': (0.0, 0.8)}
    factors = {'L0_xcond_adaLN_W': 3.858,
     'L0_xcond_adaLN_b': 8.0,
     'L0_xcond_qkv_W': 8.0,
     'L0_xcond_attn_out_W': 8.0,
     'L0_xcond_cq_W': 8.0,
     'L0_xcond_ck_W': 8.0,
     'L0_xcond_cv_W': 8.0,
     'L0_xcond_co_W': 8.0,
     'L0_xcond_mlp_W1': 4.964,
     'L0_xcond_mlp_b1': 8.0,
     'L0_xcond_mlp_W2': 4.837,
     'L0_xcond_mlp_b2': 27.283,
     'L2_xcond_Wq': 64.0,
     'L2_xcond_Wss_q': 64.0,
     'L2_xcond_Wss_kv': 51.488,
     'L1_xcond_Wq': 8.0,
     'L1_xcond_Wk': 8.0,
     'L1_xcond_Wv': 4.733,
     'L1_xcond_router_W': 3.095,
     'L1_xcond_gate_w1': 7.105,
     'L1_xcond_gate_w2': 5.371,
     'L2_xcond_Wkv': 5.573,
     'L2_xcond_Wp': 4.188,
     'L3_xcond_W_qc': 4.75}
    for name, (base, spread) in spreads.items():
        noise = np.random.default_rng([zlib.crc32(name.encode()), seed]).standard_normal(out[name].shape)
        drawn = base * np.exp(spread * noise) if base else spread * noise
        out[name] = jnp.asarray(drawn.astype(out[name].dtype))
    for name, factor in factors.items():
        out[name] = (out[name] * factor).astype(out[name].dtype)
    return out
```

```python
from contextlib import ExitStack

import numpy as np

import concourse.bass as bass
from concourse import mybir

F32 = mybir.dt.float32
BF16 = mybir.dt.bfloat16
U8 = mybir.dt.uint8
ALU = mybir.AluOpType
ACT = mybir.ActivationFunctionType
AX = mybir.AxisListType

P = 128
B, T, D = 4, 512, 128
H, HD = 16, 8
NK = 77
TB = T // P
G = H // 2
HG = 4
E, RH = 3, 256
FC = 4
COMBOS = 6
QSLOT = (0, 0, 1, 1, 2, 0)
STACK = 2 * HD * COMBOS
MASKROW = STACK
MROW = STACK + 1
ROWS = MROW + 6
BIG = 1e30
SCALE = float(HD) ** -0.5
SCALE1 = float(D) ** -0.5
SELF, CROSS = (0, 3), (1, 2, 4)
CL = {1: 0, 2: 1, 4: 2}
NSLOT = 3

EPS = (1e-5, 1e-5, 1e-5, 1e-5, 1e-5, 1e-6, 1e-6, 1e-6)
NMOD = 19
NLN = 9

ENGINES = ("pe", "act", "dve", "pool", "sp")

STEPS = {
    "load": ("sp",), "select": ("dve",), "ctx_stats": ("dve",), "ctx_norm": ("pool",),
    "gates": ("pe", "dve"), "gated": ("pool",), "anchor": ("pe", "dve"),
    "ctx_t": ("pe", "act"), "ctx_k": ("pe", "dve"), "ctx_v": ("pe", "act"), "ctx_split": ("dve",),
    "ctx_stack": ("sp",),
    "ln_stats": ("dve",), "ln_norm": ("pool",), "ln_t": ("pe", "act"),
    "rope": ("pe", "dve"), "proj": ("pe", "act"), "v": ("pe", "act"),
    "part1": ("act",), "parts": ("dve",), "stack": ("sp",),
    "max": ("pe", "dve"), "max_parts": ("dve",), "max_t": ("pe", "dve"), "max_rows": ("sp",),
    "exp": ("pe", "act"), "pv": ("pe",), "pv_out": ("act",),
    "heads_t": ("pe", "dve"), "attn_t": ("pe", "act"), "attn_out": ("pe", "dve"), "bias": ("pool",),
    "l1_scores": ("pe", "dve"), "l1_exp": ("act",), "l1_probs": ("dve",), "l1_probs_t": ("pe", "act"),
    "l1_evidence": ("pe", "act"), "router": ("pe", "dve"), "router_exp": ("act",),
    "router_probs": ("dve",), "expert_h": ("pe", "act"), "gate_h": ("pe", "act"),
    "gate": ("pe", "act"), "expert_out": ("pe", "dve"), "l1_add": ("dve",),
    "mlp_h": ("pe", "act"), "mlp_out": ("pe", "dve"),
    "store": ("sp",),
}
CHAIN = {k: (k, v[1]) for k, v in STEPS.items()
         if v[0] == "pe" and len(v) == 2 and k not in ("max", "max_t", "exp")}
CHAIN["l1_scores"] = ("l1_exp", "act")


def tiles(a):
    return 16 if a in SELF else 4


def attention(a):
    n = tiles(a)
    groups = [(hg, k) for hg in range(HG) for k in range(n // 4)]
    out = [("max", a, 0, t) for t in range(n)] + [("max_parts", a, 0)]
    for t in range(n):
        out.append(("max", a, 1, t))
        if t == 1:
            out += [("max_t", a, 0), ("max_rows", a, 0)]
    out.append(("max_parts", a, 1))
    done = 0

    def pv():
        nonlocal done
        hg, k = groups[done]
        out.append(("pv", a, hg, k))
        done += 1
        if k == n // 4 - 1 and hg % 2:
            out.append(("pv_out", a, hg // 2))

    for hg in range(HG):
        for t in range(n):
            if hg + 2 < HG:
                out.append(("max", a, hg + 2, t))
            out.append(("exp", a, hg, t))
            if t == 1 and hg + 1 < HG:
                out += [("max_t", a, hg + 1), ("max_rows", a, hg + 1)]
            if t % 4 == 3 and (hg, t) != (0, 3):
                pv()
        if hg + 2 < HG:
            out.append(("max_parts", a, hg + 2))
    pv()
    return out


def attention_end(a):
    return [("heads_t", a, 0), ("heads_t", a, 1), ("attn_t", a), ("attn_out", a)]


def norm(n):
    return [("ln_stats", n), ("ln_norm", n), ("ln_t", n)]


def before():
    return [("load",), ("select",), ("ctx_stats",), ("ctx_norm",), ("gates", 0), ("gates", 1), ("gated",),
            ("anchor",), ("ctx_t",), ("ctx_k",), ("ctx_v",), ("ctx_split",), ("ctx_stack",)]


def self_in(a, n):
    first = norm(n)
    if a == 0:
        qk = [("rope", w, r) for w in range(2) for r in range(2)]
        qk.insert(2, ("part1", a, 0)); qk.insert(3, ("parts", a, 0)); qk.insert(4, ("stack", a, 0))
    else:
        qk = [("proj", a, 0), ("part1", a, 0), ("parts", a, 0), ("stack", a, 0), ("proj", a, 1)]
        first.append(("bias", a))
    return first + qk + [("part1", a, 1), ("parts", a, 1), ("stack", a, 1), ("v", a)]


def cross_in(a, n):
    return norm(n) + ([("bias", a)] if a != 1 else []) + [
        ("proj", a, 0), ("part1", a, 0), ("parts", a, 0), ("stack", a, 0)]


def mlp(m, n):
    return norm(n) + [("bias", 5 + m)] + [("mlp_h", m, c) for c in range(FC)] + [("mlp_out", m)]


def layer1():
    return (norm(3) + [("proj", 5, 0), ("l1_scores",), ("l1_exp",), ("l1_probs",), ("l1_probs_t",), ("l1_evidence",),
                       ("router",), ("router_exp",), ("router_probs",), ("gate_h",)]
            + [("expert_h", i) for i in range(2 * E)] + [("gate",)]
            + [("expert_out", t) for t in range(TB)] + [("l1_add",)])


def sequence_steps():
    return (before() + self_in(0, 0) + attention(0) + attention_end(0)
            + cross_in(1, 1) + attention(1) + attention_end(1) + mlp(0, 2) + layer1()
            + cross_in(2, 4) + attention(2) + attention_end(2)
            + self_in(3, 5) + attention(3) + attention_end(3)
            + cross_in(4, 6) + attention(4) + attention_end(4) + mlp(1, 7) + [("store",)])


PLAN = [(0, *s) for s in sequence_steps()]
NS = 1

ORDER = {e: {} for e in ENGINES}
for step_ in PLAN:
    for e_ in STEPS[step_[1]]:
        assert step_ not in ORDER[e_], step_
        ORDER[e_][step_] = len(ORDER[e_]) + 1
CHAIN_STEPS = [s for s in PLAN if s[1] in CHAIN]
CHAIN_AT = {s: n for n, s in enumerate(CHAIN_STEPS)}
MAX_AT = {s: n for n, s in enumerate(s for s in PLAN if s[1] == "max")}
EXP_STEPS = [s for s in PLAN if s[1] == "exp"]
EXP_AT = {s: n for n, s in enumerate(EXP_STEPS)}
MAX_STEPS = list(MAX_AT)
PV_STEPS = [s for s in PLAN if s[1] == "pv"]
PV_OUT = [s for s in PLAN if s[1] == "pv_out"]
MAXT = [s for s in PLAN if s[1] == "max_t"]


def freed_by(step):
    kind, engine = CHAIN[step[1]]
    return engine, (step[0], kind, *step[2:])


def build(nc, io, out):
    ctx = ExitStack()
    with ctx:
        def sb(name, shape, dt=F32):
            return ctx.enter_context(nc.sbuf_tensor(name, shape, dt))

        def ps(name, shape, dt=F32):
            return ctx.enter_context(nc.psum_tensor(name, shape, dt))

        def sem(name):
            return ctx.enter_context(nc.semaphore(name))

        def per(name, shape, dt=F32):
            return [sb(f"{name}{s}", shape, dt) for s in range(NS)]

        w_ada = sb("w_ada", [P, 9 * D]); w_mod = sb("w_mod", [P, 6 * D])
        w_ssq = sb("w_ssq", [P, 2 * D]); w_sskv = sb("w_sskv", [P, 2 * D])
        w_qkv0 = sb("w_qkv0", [P, 3 * D]); w_rot = sb("w_rot", [P, 2 * D]); w_o0 = sb("w_o0", [P, D])
        w_cq = sb("w_cq", [P, D]); w_ck = sb("w_ck", [P, D]); w_cv = sb("w_cv", [P, D]); w_co = sb("w_co", [P, D])
        w_m1 = [sb(f"w_m1{m}", [P, FC * P]) for m in range(2)]
        w_m2 = [sb(f"w_m2{m}", [P, FC, D]) for m in range(2)]
        w_q1 = sb("w_q1", [P, D]); w_k1 = sb("w_k1", [P, D]); w_v1 = sb("w_v1", [P, D])
        w_rt = sb("w_rt", [P, 3, E]); w_e1 = sb("w_e1", [P, 3, E, RH]); 
        w_g1 = sb("w_g1", [P, 3, D]); w_g2 = sb("w_g2", [P, D]); w_out = sb("w_out", [P, D])
        w_q2 = sb("w_q2", [P, D]); w_kv2 = sb("w_kv2", [P, 2 * D]); w_p2 = sb("w_p2", [P, D])
        w_qkv3 = sb("w_qkv3", [P, 3 * D]); w_pr3 = sb("w_pr3", [P, D]); w_qc3 = sb("w_qc3", [P, D])
        w_kvc3 = sb("w_kvc3", [P, 2 * D]); w_cp3 = sb("w_cp3", [P, D])
        w_e2o = sb("w_e2o", [P, 2 * E, D])
        cosq = sb("cosq", [P, T]); sinq = sb("sinq", [P, T]); cosk = sb("cosk", [P, T]); sink = sb("sink", [P, T])
        ident = sb("ident", [P, P]); identb = sb("identb", [P, P], BF16); ones = sb("ones", [P, P])
        tail = sb("tail", [P, 2])
        cols = sb("cols", [P, 32])
        C_NW, C_GB, C_M1, C_E1, C_G1, C_Q2, C_K2, C_V2, C_QKV3, C_QC, C_KVC = 0, 3, (5, 9), 13, 19, 20, 21, 22, 23, 26, 27
        e_b2 = sb("e_b2", [P, E])
        mod_b = sb("mod_b", [P, NMOD]); mod = sb("mod", [P, NMOD, B])
        cond = sb("cond", [P, 2, B])
        affine = sb("affine", [P, NLN, 2, B])
        rows = sb("rows", [1, 15, D])
        R_ADA, R_MOD, R_M2, R_P2, R_PR3, R_CP3, R_OUT, R_G2 = 0, 3, (5, 6), 7, 8, 9, 10, 11
        rt_row = sb("rt_row", [1, E]); e2_row = sb("e2_row", [1, E * D])
        bvb = sb("bvb", [P, P]); bias_b = sb("bias_b", [P, 5, D])
        any_q = sb("any_q", [P, TB])
        mask_q = sb("mask_q", [P, TB, T], BF16); mask_k = sb("mask_k", [P, TB, T], BF16)
        eps_pow = sb("eps_pow", [P, 1])

        x = per("x", [P, TB, D]); xn = per("xn", [P, TB, D]); xt = per("xt", [P, T])
        stats = per("stats", [P, TB, 6]); mv = per("mv", [P, TB, 2]); var = per("var", [P, TB]); rstd = per("rstd", [P, TB])
        cx = per("cx", [NK, D]); cstats = per("cstats", [NK, 6]); cmv = per("cmv", [NK, 2])
        cvar = per("cvar", [NK, 2]); crstd = per("crstd", [NK, 2]); cxn = per("cxn", [NK, 2, D]); cxt = per("cxt", [P, 3, NK])
        cmask = per("cmask", [P, NK], U8); cmaskf = per("cmaskf", [P, NK]); cany = per("cany", [P, 1])
        cbias = per("cbias", [P, NK], BF16)
        aff = per("aff", [P, NLN, 2]); cc = per("cc", [P, 2]); cb = per("cb", [P, 2, P])
        gate_b = per("gate_b", [P, 5, D]); anc = per("anc", [P, 7]); rt_b = per("rt_b", [P, E])
        g_o0 = per("g_o0", [P, D]); g_co = per("g_co", [P, D]); g_pr = per("g_pr", [P, D])
        g_m2 = [per(f"g_m2{m}_", [P, FC, D]) for m in range(2)]; g_bias = per("g_bias", [P, 3, D])
        kc = per("kc", [P, 4, NK]); kcr = per("kcr", [P, 3, NK]); kcp = per("kcp", [P, 3, 3, NK], BF16)
        ksc = per("ksc", [P, 3, G, 2, NK], BF16); vac = per("vac", [NK, 3, 2, 2, 4, 32]); vc1 = per("vc1", [NK, D])
        hid = per("hid", [P, 2 * E, T])
        qf, r1, r2 = ([[hid[s][:, 2 * i + w, :] for s in range(NS)] for w in range(2)] for i in range(3))
        qp = [per(f"qp{w}_", [P, 3, T], BF16) for w in range(2)]
        qs = per("qs", [P, G, T], BF16); ks = per("ks", [P, 2, G, T], BF16); va = per("va", [P, 2, TB, 2, 4, 32])
        mx = per("mx", [P, 2, TB, 2, 2]); mr = per("mr", [P, TB * 2, 2]); mp = per("mp", [P, 2, TB, 2, 3, 2], BF16)
        mrow = per("mrow", [12, 2, T], BF16)
        u = per("u", [P, 2, T]); rec = per("rec", [P, 2, TB, 4, 2]); ao = per("ao", [P, TB, D]); aot = per("aot", [P, T])
        evt = per("evt", [P, T])
        m1 = per("m1", [P, TB]); nm1 = per("nm1", [P, TB]); s1 = per("s1", [P, TB]); rs1 = per("rs1", [P, TB])
        es = per("es", [P, TB, NK]); pn = per("pn", [P, TB, NK]); pt = per("pt", [NK, T])
        lg = per("lg", [P, TB, E]); lm = per("lm", [P, TB]); lsub = per("lsub", [P, TB, E]); lex = per("lex", [P, TB, E])
        lsum = per("lsum", [P, TB]); lrec = per("lrec", [P, TB]); prob = per("prob", [P, TB, E])
        gh = per("gh", [P, T])
        gt, ro = ([u[s][:, i, :].rearrange("p (t d) -> p t d", t=TB) for s in range(NS)] for i in range(2))
        ro2 = [aot[s][:, :].rearrange("p (t d) -> p t d", t=TB) for s in range(NS)]
        pr = sb("pr", [P, NSLOT * 4, T])
        mask_f = pr[:, 0, :]
        diag = pr[:, 1, :].rearrange("p (t k) -> p t k", t=TB)
        mask_u = pr[:, 2, :].bitcast(U8).rearrange("p (t k) -> p t k", t=TB)
        w_e2 = pr[:, 3:5, :].rearrange("p a n -> p (a n)")[:, 0:2 * E * D].rearrange("p (e c d) -> p e c d", e=E, c=2)
        w_e2t = pr[:, 5:7, :].rearrange("p a n -> p (a n)")[:, 0:2 * E * P].rearrange("p (e r) -> p e r", e=2 * E)

        chain = [ps(f"chain{n}", [P, T]) for n in range(2)]
        pvb = ps("pvb", [P, T]); mtb = ps("mtb", [P, 2 * T], BF16)
        mxb = [ps(f"mxb{n}", [P, T]) for n in range(2)]
        exb = [ps(f"exb{n}", [P, T]) for n in range(2)]

        q_parts = [nc.dram_tensor(f"q_parts{s}", [3, P, T], BF16).ap() for s in range(NS)]
        k_parts = [nc.dram_tensor(f"k_parts{s}", [P, COMBOS, T], BF16).ap() for s in range(NS)]
        c_parts = [nc.dram_tensor(f"c_parts{s}", [3, P, COMBOS, NK], BF16).ap() for s in range(NS)]

        loaded = sem("loaded"); tables = sem("tables")
        set_pe, set_act, set_dve = sem("set_pe"), sem("set_act"), sem("set_dve")
        in_loop0 = sem("first_loop_semaphore")
        done = {e: sem(f"{e}_done") for e in ENGINES if e != "sp"}
        dve_link, pool_link, act_link = sem("dve_link"), sem("pool_link"), sem("act_link")
        x_in = [sem(f"x_in{s}") for s in range(NS)]; ctx_in = [sem(f"ctx_in{s}") for s in range(NS)]
        cwrit = [sem(f"ctx_parts_written{s}") for s in range(NS)]; cread = [sem(f"ctx_stacked{s}") for s in range(NS)]
        qwrit = [sem(f"q_parts_written{s}") for s in range(NS)]; kwrit = [sem(f"k_parts_written{s}") for s in range(NS)]
        qread = [sem(f"q_stacked{s}") for s in range(NS)]; kread = [sem(f"k_stacked{s}") for s in range(NS)]
        mrows = [sem(f"max_rows{s}") for s in range(NS)]; stored = [sem(f"stored{s}") for s in range(NS)]
        last_sem = stored[-1]

        def link(eng, s, count, ins):
            ins.then_inc(s, 1)
            count[0] += 1
            eng.wait_ge(s, count[0])

        NLOAD = [0]

        with nc.Block() as block:
            @block.sync
            def _(sp):
                def load(dst, src):
                    sp.dma_start(dst, src).then_inc(loaded, 16)
                    NLOAD[0] += 16

                def col(c, src, n=1):
                    load(cols[:, c:c + n], src.rearrange("(c p) -> p c", p=P))

                def row(r, src, n=1):
                    load(rows[0:1, r:r + n, :], src.rearrange("(a c d) -> a c d", a=1, d=D))

                with nc.allow_non_contiguous_dma(reason="bias columns, once"):
                    load(cond[:, 0, :], io["cond_1024"].rearrange("b d -> d b"))
                    col(C_NW, io["L0_xcond_norm1_w"]); col(C_NW + 1, io["L0_xcond_normc_w"]); col(C_NW + 2, io["L0_xcond_norm2_w"])
                    col(C_GB, io["L1_xcond_ln_gamma"]); col(C_GB + 1, io["L1_xcond_ln_beta"])
                    col(C_M1[0], io["L0_xcond_mlp_b1"], 4); col(C_M1[1], io["L3_xcond_b_mlp1"], 4)
                    load(cols[:, C_E1:C_E1 + 6], io["L1_xcond_e_b1"].rearrange("e (c p) -> p (e c)", p=P))
                    col(C_G1, io["L1_xcond_gate_b1"]); col(C_Q2, io["L2_xcond_bq"]); col(C_K2, io["L2_xcond_bkv"], 2)
                    col(C_QKV3, io["L3_xcond_b_qkv"], 3); col(C_QC, io["L3_xcond_b_qc"]); col(C_KVC, io["L3_xcond_b_kvc"], 2)
                    load(e_b2[:, :], io["L1_xcond_e_b2"].rearrange("e p -> p e"))
                    for c, n, src in ((0, 9, "L0_xcond_adaLN_b"), (9, 2, "L2_xcond_bss_q"), (11, 2, "L2_xcond_bss_kv"),
                                      (13, 6, "L3_xcond_b_mod")):
                        load(mod_b[:, c:c + n], io[src].rearrange("(c p) -> p c", p=P))
                load(w_ada[:, :], io["L0_xcond_adaLN_W"]); load(w_ssq[:, :], io["L2_xcond_Wss_q"])
                load(w_sskv[:, :], io["L2_xcond_Wss_kv"]); load(w_mod[:, :], io["L3_xcond_W_mod"])
                load(mask_u[:, :, :], io["mask_SxS_bk0"].rearrange("(a p) k -> p a k", p=P))
                load(ident[:, :], io["c_ident"]); load(tail[:, :], io["c_tail"])
                load(cosk[:, :], io["c_cos"]); load(sink[:, :], io["c_sin"])
                load(w_qkv0[:, :], io["L0_xcond_qkv_W"])
                for dst, src in ((w_o0, "L0_xcond_attn_out_W"), (w_cq, "L0_xcond_cq_W"), (w_ck, "L0_xcond_ck_W"),
                                 (w_cv, "L0_xcond_cv_W"), (w_co, "L0_xcond_co_W"), (w_m1[0], "L0_xcond_mlp_W1"),
                                 (w_m1[1], "L3_xcond_W_mlp1"), (w_q1, "L1_xcond_Wq"), (w_k1, "L1_xcond_Wk"),
                                 (w_v1, "L1_xcond_Wv"), (w_g2, "L1_xcond_gate_w2"), (w_out, "L1_xcond_out_w"),
                                 (w_q2, "L2_xcond_Wq"), (w_kv2, "L2_xcond_Wkv"), (w_p2, "L2_xcond_Wp"),
                                 (w_qkv3, "L3_xcond_W_qkv"), (w_pr3, "L3_xcond_W_proj"), (w_qc3, "L3_xcond_W_qc"),
                                 (w_kvc3, "L3_xcond_W_kvc"), (w_cp3, "L3_xcond_W_cproj")):
                    load(dst[:, :], io[src])
                load(w_m2[0][:, :, :], io["L0_xcond_mlp_W2"].rearrange("(c p) d -> p c d", p=P))
                load(w_m2[1][:, :, :], io["L3_xcond_W_mlp2"].rearrange("(c p) d -> p c d", p=P))
                load(w_rt[:, :, :], io["L1_xcond_router_W"].rearrange("(c p) e -> p c e", p=P))
                for e in range(E):
                    load(w_e1[:, :, e, :], io["L1_xcond_e_w1"][e].rearrange("(c p) r -> p c r", p=P))
                    load(w_e2[:, e, :, :], io["L1_xcond_e_w2"][e].rearrange("(c p) d -> p c d", p=P))
                load(w_g1[:, :, :], io["L1_xcond_gate_w1"].rearrange("(c p) d -> p c d", p=P))
                for g in range(3):
                    row(R_ADA + g, io["L0_xcond_adaLN_b"][(3 * g + 2) * D:(3 * g + 3) * D])
                for g in range(2):
                    row(R_MOD + g, io["L3_xcond_b_mod"][(3 * g + 2) * D:(3 * g + 3) * D])
                row(R_M2[0], io["L0_xcond_mlp_b2"]); row(R_M2[1], io["L3_xcond_b_mlp2"]); row(R_P2, io["L2_xcond_bp"])
                row(R_PR3, io["L3_xcond_b_proj"]); row(R_CP3, io["L3_xcond_b_cproj"]); row(R_OUT, io["L1_xcond_out_b"])
                row(R_G2, io["L1_xcond_gate_b2"])
                load(rt_row[0:1, :], io["L1_xcond_router_b"].rearrange("(a e) -> a e", a=1))

            @block.scalar
            def _(act):
                act.wait_ge(loaded, NLOAD[0])
                act.activation(cond[:, 1, :], cond[:, 0, :], ACT.Silu).then_inc(set_act, 1)

            MODW = ([(w_ada, c, 0) for c in range(9)] + [(w_ssq, c, 1) for c in range(2)]
                    + [(w_sskv, c, 1) for c in range(2)] + [(w_mod, c, 1) for c in range(6)])

            @block.vector
            def _(dve):
                n = [0]

                def do(ins):
                    link(dve, dve_link, n, ins)

                dve.memset(ones[:, :], 1.0).then_inc(set_dve, 1)
                dve.wait_ge(loaded, NLOAD[0])
                dve.tensor_copy(identb[:, :], ident[:, :]).then_inc(set_dve, 1)
                do(dve.tensor_reduce(any_q[:, :], mask_u[:, :, :], AX.X, ALU.max))
                for t in range(TB):
                    do(dve.tensor_scalar(diag[:, t, :], ident[:, :], any_q[:, t:t + 1], None, ALU.mult))
                    do(dve.tensor_scalar(mask_f[:, :], mask_u[:, t, :], 1.0, BIG, ALU.subtract, ALU.mult))
                    do(dve.tensor_scalar(mask_q[:, t, :], mask_f[:, :], any_q[:, t:t + 1], None, ALU.mult))
                dve.memset(eps_pow[:, :], -0.5).then_inc(set_dve, 1)
                wv = w_qkv0[:, 0:2 * D].rearrange("p (h r d) -> p h r d", r=2, d=HD // 2)
                rv = w_rot[:, :].rearrange("p (h r d) -> p h r d", r=2, d=HD // 2)
                dve.tensor_scalar(rv[:, :, 0, :], wv[:, :, 1, :], -1.0, None, ALU.mult).then_inc(set_dve, 1)
                dve.tensor_copy(rv[:, :, 1, :], wv[:, :, 0, :]).then_inc(set_dve, 1)
                for s in range(NS):
                    for e in range(2):
                        dve.tensor_copy(ks[s][:, e, :, :].rearrange("p g n -> p (g n)"), tail[:, e:e + 1].to_broadcast([P, G * T]))
                        dve.tensor_copy(ksc[s][:, :, :, e, :].rearrange("p l g n -> p (l g) n"),
                                        tail[:, e:e + 1].rearrange("p (a b) -> p a b", a=1).to_broadcast([P, 3 * G, NK]))
                    dve.memset(va[s][:, :, :, :, :, :], 0.0)
                    dve.memset(vac[s][:, :, :, :, :, :], 0.0)
                    do(dve.memset(qs[s][96:128, :, :], 1.0))
                    for par in range(2):
                        dve.memset(va[s][:, par, :, :, :, 16 * par + 8:16 * par + 16], 1.0)
                        do(dve.memset(vac[s][:, :, par, :, :, 16 * par + 8:16 * par + 16], 1.0))
                dve.wait_ge(set_pe, 1)
                do(dve.tensor_tensor(mod[:, :, :], chain[0][:, 0:NMOD * B].rearrange("p (c b) -> p c b", b=B),
                                     mod_b[:, :].rearrange("p (c a) -> p c a", a=1).to_broadcast([P, NMOD, B]), ALU.add))
                for n_, (sh, sc) in ((0, (0, 1)), (1, (3, 4)), (2, (6, 7)), (4, (10, 9)), (5, (13, 14)), (7, (16, 17)), (8, (12, 11))):
                    do(dve.tensor_scalar(affine[:, n_, 0, :], mod[:, sc, :], 1.0, None, ALU.add))
                    if n_ < 3:
                        do(dve.tensor_scalar(affine[:, n_, 0, :], affine[:, n_, 0, :], cols[:, C_NW + n_:C_NW + n_ + 1], None, ALU.mult))
                    do(dve.tensor_copy(affine[:, n_, 1, :], mod[:, sh, :]))
                for k in range(2):
                    do(dve.tensor_copy(affine[:, 3, k, :], cols[:, C_GB + k:C_GB + k + 1].to_broadcast([P, B])))
                    do(dve.memset(affine[:, 6, k, :], 1.0 - k))
                dve.wait_ge(set_pe, 2)
                do(dve.tensor_tensor(cosq[:, :], chain[1][:, :], cosk[:, :], ALU.mult))
                do(dve.tensor_tensor(sinq[:, :], chain[1][:, :], sink[:, :], ALU.mult))
                dve.tensor_copy(bvb[:, :], cols[:, C_V2:C_V2 + 1].to_broadcast([P, P])).then_inc(set_dve, 1)
                for kb in range(TB):
                    dve.wait_ge(set_pe, 3 + kb)
                    dve.tensor_copy(mask_k[:, kb, :], mtb[:, 0:T]).then_inc(set_dve, 1)
                dve.wait_ge(set_pe, 7)
                dve.tensor_copy(bias_b[:, 0, :], chain[0][:, 0:D]).then_inc(set_dve, 1)
                dve.tensor_copy(bvb[:, :], cols[:, C_QKV3 + 2:C_QKV3 + 3].to_broadcast([P, P])).then_inc(set_dve, 1)
                dve.wait_ge(set_pe, 8)
                dve.tensor_copy(bias_b[:, 1, :], chain[1][:, 0:D]).then_inc(set_dve, 1)
                dve.tensor_copy(bvb[:, :], cols[:, C_KVC + 1:C_KVC + 2].to_broadcast([P, P])).then_inc(set_dve, 1)
                dve.wait_ge(set_pe, 9)
                dve.tensor_copy(bias_b[:, 2, :], chain[0][:, 0:D]).then_inc(set_dve, 1)
                dve.wait_ge(set_pe, 10)
                dve.tensor_copy(bias_b[:, 3:5, :], chain[1][:, 0:2 * D].rearrange("p (a d) -> p a d", a=2)).then_inc(set_dve, 1)
                dve.wait_ge(set_pe, 12)
                dve.tensor_copy(w_e2t[:, 0:4, :], mxb[0][:, :].rearrange("p (a r) -> p a r", a=4)).then_inc(set_dve, 1)
                dve.tensor_copy(w_e2t[:, 4:6, :], mxb[1][:, 0:2 * P].rearrange("p (a r) -> p a r", a=2)).then_inc(set_dve, 1)
                dve.wait_ge(set_pe, 15)
                do(dve.tensor_copy(w_e2o[:, 0:4, :], exb[0][:, :].rearrange("p (a r) -> p a r", a=4)))
                do(dve.tensor_copy(w_e2o[:, 4:6, :], exb[1][:, 0:2 * P].rearrange("p (a r) -> p a r", a=2)))
                do(dve.tensor_copy(e2_row[0:1, :], pvb[0:1, 0:E * D]))

            @block.tensor
            def _(pe):
                pe.wait_ge(loaded, NLOAD[0])
                pe.wait_ge(set_act, 1)
                for n, (w, c, which) in enumerate(MODW):
                    mm = pe.matmul(chain[0][:, n * B:(n + 1) * B], w[:, c * D:(c + 1) * D], cond[:, which, :], start=True, stop=True)
                mm.then_inc(set_pe, 1)
                pe.wait_ge(set_dve, 3)
                for t in range(TB):
                    mm = pe.matmul(chain[1][:, t * P:(t + 1) * P], ones[:, :], diag[:, t, :], start=True, stop=True)
                mm.then_inc(set_pe, 1)
                pe.wait_ge(set_dve, 6)
                for kb in range(TB):
                    if kb:
                        pe.wait_ge(set_dve, 6 + kb)
                    for t in range(TB):
                        mm = pe.transpose(mtb[:, t * P:(t + 1) * P],
                                          mask_q[:, t, kb * P:(kb + 1) * P], identb[:, :])
                    mm.then_inc(set_pe, 1)
                for n, (w, r) in enumerate(((w_p2[:, :], R_P2), (w_pr3[:, :], R_PR3), (w_cp3[:, :], R_CP3))):
                    if n:
                        pe.wait_ge(set_dve, 10 + 2 * n)
                    pe.matmul(chain[n % 2][:, 0:D], bvb[:, :], w, start=True, stop=False)
                    pe.matmul(chain[n % 2][:, 0:D], ones[0:1, :], rows[0:1, r, :], start=False, stop=True).then_inc(set_pe, 1)
                pe.wait_ge(set_dve, 15)
                for n in range(2):
                    mm = pe.matmul(chain[1][:, n * D:(n + 1) * D], ones[0:1, :], rows[0:1, R_M2[n], :], start=True, stop=True)
                mm.then_inc(set_pe, 1)
                for n in range(2 * E):
                    mm = pe.transpose(mxb[n // 4][:, (n % 4) * P:(n % 4 + 1) * P], w_e2[:, n // 2, n % 2, :], ident[:, :])
                    if n in (3, 5):
                        mm.then_inc(set_pe, 1)
                pe.wait_ge(set_dve, 18)
                for n in range(2 * E):
                    mm = pe.matmul(exb[n // 4][:, (n % 4) * D:(n % 4 + 1) * D], w_e2t[:, n, :], w_out[:, :], start=True, stop=True)
                    if n in (3, 5):
                        mm.then_inc(set_pe, 1)
                for e in range(E):
                    pe.matmul(pvb[0:1, e * D:(e + 1) * D], e_b2[:, e:e + 1], w_out[:, :], start=True, stop=False)
                    mm = pe.matmul(pvb[0:1, e * D:(e + 1) * D], ones[0:1, 0:1], rows[0:1, R_OUT, :], start=False, stop=True)
                mm.then_inc(set_pe, 1)

        nc.gpsimd.sem_clear(dve_link)
        nc.all_engine_barrier(sem_only=True)

        with nc.Fori(0, B // NS) as turn:
            with nc.Block(no_gpsimd_drain=True) as block:
                def after(eng, producer, step):
                    eng.wait_ge(done[producer], ORDER[producer][step])

                def chain_bank(pe, step):
                    n = CHAIN_AT[step]
                    if n >= 2:
                        after(pe, *freed_by(CHAIN_STEPS[n - 2]))
                    return chain[n % 2]

                def bank(step):
                    return chain[CHAIN_AT[step] % 2]

                def blocks(ap, n=TB):
                    return ap.rearrange("p (t d) -> p t d", t=n)

                QKIN = {0: (w_qkv0, 0), 1: (w_cq, 0), 2: (w_q2, 0), 3: (w_qkv3, 0), 4: (w_qc3, 0), 5: (w_q1, 0)}
                QBIAS = {1: None, 2: C_Q2, 3: C_QKV3, 4: C_QC, 5: None}
                LN_OF = {0: 0, 1: 1, 2: 4, 3: 5, 4: 6, 5: 3}
                LN_OF_MLP = (2, 7)

                @block.sync
                def _(sp):
                    def load(k, s):
                        seq = turn * NS + s
                        sp.dma_start(x[s][:, :, :], io["x"][bass.ds(seq, 1)].rearrange("a (t p) d -> p (a t) d", p=P)).then_inc(x_in[s], 16)
                        sp.dma_start(cx[s][:, :], io["ctx_1024"][bass.ds(seq, 1)].rearrange("a k d -> k (a d)")).then_inc(ctx_in[s], 16)
                        sp.dma_start(cmask[s][:, :], io["mask_BxS2_bf1"][bass.ds(seq, 1)].to_broadcast([P, NK])).then_inc(ctx_in[s], 16)

                    def ctx_stack(k, s):
                        after(sp, "dve", (s, "ctx_split"))
                        for c in range(3):
                            sp.dma_start(c_parts[s][c, :, 0:4, :].rearrange("p (a b) n -> p a b n", a=2)[:, 0], kcp[s][:, c, 0:2, :]).then_inc(cwrit[s], 16)
                            sp.dma_start(c_parts[s][c, :, 0:4, :].rearrange("p (a b) n -> p a b n", a=2)[:, 1], kcp[s][:, c, 0:2, :]).then_inc(cwrit[s], 16)
                            sp.dma_start(c_parts[s][c, :, 4:6, :], kcp[s][:, c, 0:3:2, :]).then_inc(cwrit[s], 16)
                        sp.wait_ge(cwrit[s], 16 * 9)
                        for c in range(3):
                            v = c_parts[s][c].rearrange("(g e d) c n -> e (d c) g n", e=2, d=HD)
                            for e in range(2):
                                sp.dma_start(ksc[s][48 * e:48 * e + 48, c, :, e, :], v[e]).then_inc(cread[s], 16)

                    def stack(k, s, a, w):
                        after(sp, "dve", (s, "parts", a, w))
                        if w == 0:
                            sp.dma_start(q_parts[s].rearrange("c p n -> p c n"), qp[0][s][:, :, :]).then_inc(qwrit[s], 16)
                            sp.wait_ge(qwrit[s], 16 * (a + 1))
                            for c in range(COMBOS):
                                sp.dma_start(qs[s][c:STACK:COMBOS, :, :],
                                             q_parts[s][QSLOT[c]].rearrange("(g ed) n -> ed g n", g=G)).then_inc(qread[s], 16)
                        else:
                            n = SELF.index(a)
                            kv = k_parts[s].rearrange("p c n -> p c n")
                            sp.dma_start(kv[:, 0:2, :], qp[1][s][:, 0:2, :]).then_inc(kwrit[s], 16)
                            sp.dma_start(kv[:, 2:4, :], qp[1][s][:, 0:2, :]).then_inc(kwrit[s], 16)
                            sp.dma_start(kv[:, 4:6, :], qp[1][s][:, 0:3:2, :]).then_inc(kwrit[s], 16)
                            sp.wait_ge(kwrit[s], 48 * (n + 1))
                            v = k_parts[s].rearrange("(g e d) c n -> e (d c) g n", e=2, d=HD)
                            for e in range(2):
                                sp.dma_start(ks[s][48 * e:48 * e + 48, e, :, :], v[e]).then_inc(kread[s], 16)

                    def max_rows(k, s, a, hg):
                        after(sp, "dve", (s, "max_t", a, hg))
                        for g in range(2):
                            sp.dma_start(qs[s][MROW:ROWS, 2 * hg + g, :], mrow[s][6 * g:6 * g + 6, hg % 2, :]).then_inc(mrows[s], 16)

                    def store(k, s):
                        after(sp, "dve", (s, "mlp_out", 1))
                        seq = turn * NS + s
                        sp.dma_start(out[bass.ds(seq, 1)].rearrange("a (t p) d -> p (a t) d", p=P), x[s][:, :, :]).then_inc(stored[s], 16)

                    parts = locals()
                    for step in PLAN:
                        if "sp" in STEPS[step[1]]:
                            parts[step[1]](step, step[0], *step[2:])
                    for s in range(NS):
                        sp.wait_ge(stored[s], 16)

                @block.gpsimd
                def _(pool):
                    n = [0]

                    def ctx_norm(k, s):
                        after(pool, "dve", (s, "ctx_stats"))
                        link(pool, pool_link, n, pool.tensor_tensor(crstd[s][:, :], cvar[s][:, :], eps_pow[0:NK, 0:1].to_broadcast([NK, 2]), ALU.pow))
                        for j in range(2):
                            ins = pool.tensor_scalar(cxn[s][:, j, :], cx[s][:, :], cmv[s][:, 0:1], crstd[s][:, j:j + 1], ALU.subtract, ALU.mult)
                        ins.then_inc(done["pool"], 1)

                    def ln_norm(k, s, m):
                        after(pool, "dve", (s, "ln_stats", m))
                        link(pool, pool_link, n, pool.tensor_tensor(rstd[s][:, :], var[s][:, :], eps_pow[:, 0:1].to_broadcast([P, TB]), ALU.pow))
                        if m:
                            after(pool, "pe", (s, "ln_t", m - 1))
                        for t in range(TB):
                            ins = pool.tensor_scalar(xn[s][:, t, :], x[s][:, t, :], mv[s][:, t, 0:1], rstd[s][:, t:t + 1], ALU.subtract, ALU.mult)
                        ins.then_inc(done["pool"], 1)

                    def gated(k, s):
                        after(pool, "dve", (s, "gates", 0))
                        after(pool, "dve", (s, "gates", 1))
                        pool.tensor_tensor(g_o0[s][:, :], w_o0[:, :], gate_b[s][:, 0, :], ALU.mult)
                        pool.tensor_tensor(g_co[s][:, :], w_co[:, :], gate_b[s][:, 1, :], ALU.mult)
                        pool.tensor_tensor(g_pr[s][:, :], w_pr3[:, :], gate_b[s][:, 3, :], ALU.mult)
                        for m, g in ((0, 2), (1, 4)):
                            pool.tensor_tensor(g_m2[m][s][:, :, :], w_m2[m][:, :, :],
                                               gate_b[s][:, g:g + 1, :].to_broadcast([P, FC, D]), ALU.mult)
                        pool.tensor_tensor(g_bias[s][:, 0, :], bias_b[:, 3, :], gate_b[s][:, 2, :], ALU.mult)
                        pool.tensor_tensor(g_bias[s][:, 1, :], bias_b[:, 1, :], gate_b[s][:, 3, :], ALU.mult)
                        pool.tensor_tensor(g_bias[s][:, 2, :], bias_b[:, 4, :], gate_b[s][:, 4, :], ALU.mult).then_inc(done["pool"], 1)

                    def bias(k, s, m):
                        b = {2: bias_b[:, 0:1, :], 3: g_bias[s][:, 1:2, :], 4: bias_b[:, 2:3, :],
                             5: g_bias[s][:, 0:1, :], 6: g_bias[s][:, 2:3, :]}[m]
                        after(pool, "pool", (s, "gated"))
                        after(pool, "pool", (s, "ln_norm", {2: 4, 3: 5, 4: 6, 5: 2, 6: 7}[m]))
                        pool.tensor_tensor(x[s][:, :, :], x[s][:, :, :], b.to_broadcast([P, TB, D]), ALU.add).then_inc(done["pool"], 1)

                    parts = locals()
                    for step in PLAN:
                        if "pool" in STEPS[step[1]]:
                            parts[step[1]](step, step[0], *step[2:])

                @block.scalar
                def _(act):
                    def ctx_t(k, s):
                        after(act, "pe", k)
                        c = blocks(bank(k)[:, 0:3 * NK], 3)
                        act.activation(cxt[s][:, 0, :], c[:, 0, :], ACT.Identity)
                        act.activation(cxt[s][:, 1, :], c[:, 1, :], ACT.Identity, scale=aff[s][:, 8, 0:1], bias=aff[s][:, 8, 1:2])
                        act.activation(cxt[s][:, 2, :], c[:, 2, :], ACT.Identity).then_inc(done["act"], 1)

                    def heads_values(dst, src):
                        for par in range(2):
                            ins = act.activation(dst[par], src[:, :, par, :, :], ACT.Identity)
                        return ins

                    def ctx_v(k, s):
                        after(act, "pe", k)
                        c = bank(k)
                        for l in range(4):
                            cv = c[0:NK, l * D:(l + 1) * D]
                            if l == 1:
                                act.activation(vc1[s][:, :], cv, ACT.Identity)
                                continue
                            m = {0: 0, 2: 1, 3: 2}[l]
                            ins = heads_values([vac[s][:, m, par, :, :, 16 * par:16 * par + 8] for par in range(2)],
                                               cv.rearrange("p (h q j d) -> p h q j d", h=2, q=2, j=4))
                        ins.then_inc(done["act"], 1)

                    def v(k, s, a):
                        after(act, "pe", k)
                        ins = heads_values([va[s][:, par, :, :, :, 16 * par:16 * par + 8].rearrange("p t h j d -> p (t h) j d") for par in range(2)],
                                           bank(k)[:, :].rearrange("p (th q j d) -> p th q j d", q=2, j=4, d=HD))
                        ins.then_inc(done["act"], 1)

                    def ln_t(k, s, m):
                        after(act, "pe", k)
                        act.activation(xt[s][:, :], bank(k)[:, :], ACT.Identity, scale=aff[s][:, m, 0:1],
                                       bias=aff[s][:, m, 1:2]).then_inc(done["act"], 1)

                    def proj(k, s, a, w):
                        after(act, "pe", k)
                        c = QBIAS[a]
                        kw = {} if c is None else {"bias": cols[:, c + w:c + w + 1]}
                        act.activation(qf[w][s][:, :], bank(k)[:, :], ACT.Identity, **kw).then_inc(done["act"], 1)

                    def part1(k, s, a, w):
                        src = (s, "rope", w, 1) if a == 0 else (s, "proj", a, w)
                        after(act, "dve" if a == 0 else "act", src)
                        act.activation(qp[w][s][:, 0, :], qf[w][s][:, :], ACT.Identity).then_inc(done["act"], 1)

                    def exp(k, s, a, hg, t):
                        n = EXP_AT[k]
                        after(act, "pe", k)
                        if n >= 4 * NSLOT:
                            after(act, "pe", PV_STEPS[n // 4 - NSLOT])
                        K = P if a in SELF else NK
                        act.activation(pr[0:K, n % (4 * NSLOT), :], exb[n % 2][0:K, :], ACT.Exp, scale=SCALE).then_inc(done["act"], 1)

                    def pv_out(k, s, a, ab):
                        after(act, "pe", (s, "pv", a, 2 * ab + 1, tiles(a) // 4 - 1))
                        act.activation(u[s][:, ab, :], pvb[:, :], ACT.Identity).then_inc(done["act"], 1)

                    def attn_t(k, s, a):
                        after(act, "pe", k)
                        act.activation(aot[s][:, :], bank(k)[:, :], ACT.Identity).then_inc(done["act"], 1)

                    def l1_exp(k, s):
                        after(act, "dve", (s, "l1_scores"))
                        c = bank((s, "l1_scores"))
                        for t in range(TB):
                            ins = act.activation(es[s][:, t, :], c[:, t * NK:(t + 1) * NK], ACT.Exp, scale=SCALE1,
                                                 bias=nm1[s][:, t:t + 1], accum_out=s1[s][:, t:t + 1])
                        ins.then_inc(done["act"], 1)

                    def l1_probs_t(k, s):
                        after(act, "pe", k)
                        act.activation(pt[s][:, :], bank(k)[0:NK, :], ACT.Identity).then_inc(done["act"], 1)

                    def l1_evidence(k, s):
                        after(act, "pe", k)
                        act.activation(evt[s][:, :], bank(k)[:, :], ACT.Identity).then_inc(done["act"], 1)

                    def router_exp(k, s):
                        after(act, "dve", (s, "router"))
                        act.activation(lex[s][:, :, :], lsub[s][:, :, :], ACT.Exp).then_inc(done["act"], 1)

                    def expert_h(k, s, i):
                        after(act, "pe", k)
                        act.activation(hid[s][:, i, :], bank(k)[:, :], ACT.Silu, bias=anc[s][:, i:i + 1]).then_inc(done["act"], 1)

                    def gate_h(k, s):
                        after(act, "pe", k)
                        act.activation(gh[s][:, :], bank(k)[:, :], ACT.Silu, bias=anc[s][:, 6:7]).then_inc(done["act"], 1)

                    def gate(k, s):
                        after(act, "pe", k)
                        act.activation(gt[s][:, :, :], blocks(bank(k)[:, :]), ACT.Tanh, scale=0.5).then_inc(done["act"], 1)

                    def mlp_h(k, s, m, c):
                        after(act, "pe", k)
                        act.activation(hid[s][:, c, :], bank(k)[:, :], ACT.Gelu_apprx_tanh,
                                       bias=cols[:, C_M1[m] + c:C_M1[m] + c + 1]).then_inc(done["act"], 1)

                    parts = locals()
                    for step in PLAN:
                        if "act" in STEPS[step[1]]:
                            parts[step[1]](step, step[0], *step[2:])

                @block.vector
                def _(dve):
                    n = [0]

                    def do(ins):
                        link(dve, dve_link, n, ins)

                    def end(ins):
                        ins.then_inc(done["dve"], 1)

                    def select(k, s):
                        seq = turn * NS + s
                        do(dve.tensor_copy(aff[s][:, :, :],
                                           affine[:, :, :, bass.ds(seq, 1)].rearrange("p n k a -> p n (k a)")))
                        do(dve.tensor_copy(cc[s][:, :], cond[:, :, bass.ds(seq, 1)].rearrange("p k a -> p (k a)")))
                        dve.tensor_copy(cb[s][:, 0, :], cc[s][:, 0:1].to_broadcast([P, P]))
                        end(dve.tensor_copy(cb[s][:, 1, :], cc[s][:, 1:2].to_broadcast([P, P])))

                    def gates(k, s, l):
                        after(dve, "pe", k)
                        m = (3, 2)[l]
                        end(dve.tensor_copy(gate_b[s][:, 3 * l:3 * l + m, :], blocks(bank(k)[:, 0:m * D], m)))

                    def anchor(k, s):
                        after(dve, "pe", k)
                        do(dve.tensor_tensor(anc[s][:, :], bank(k)[:, 0:7], cols[:, C_E1:C_E1 + 7], ALU.add))
                        end(dve.tensor_copy(rt_b[s][:, :], bank(k)[:, 8:8 + E]))

                    def ctx_stats(k, s):
                        dve.wait_ge(ctx_in[s], 32)
                        do(dve.bn_stats(cstats[s][:, :], cx[s][:, :]))
                        do(dve.bn_aggr(cmv[s][:, :], cstats[s][:, :]))
                        dve.tensor_scalar(cvar[s][:, 0:1], cmv[s][:, 1:2], EPS[4], None, ALU.add)
                        do(dve.tensor_scalar(cvar[s][:, 1:2], cmv[s][:, 1:2], EPS[6], None, ALU.add))
                        do(dve.tensor_reduce(cany[s][:, :], cmask[s][:, :], AX.X, ALU.max))
                        do(dve.tensor_scalar(cmaskf[s][:, :], cmask[s][:, :], 1.0, BIG, ALU.subtract, ALU.mult))
                        do(dve.tensor_scalar(cbias[s][:, :], cmaskf[s][:, :], cany[s][:, 0:1], None, ALU.mult))
                        end(dve.tensor_copy(ksc[s][96:97, 0, :, :, :].rearrange("p g e n -> p (g e) n"),
                                            cbias[s][96:97, :].rearrange("p (a n) -> p a n", a=1).to_broadcast([1, 2 * G, NK])))

                    def ctx_k(k, s):
                        after(dve, "pe", k)
                        c = blocks(bank(k)[:, 0:4 * NK], 4)
                        dve.tensor_scalar(kc[s][:, 0, :], c[:, 0, :], cany[s][:, 0:1], None, ALU.mult)
                        dve.tensor_copy(kc[s][:, 3, :], c[:, 1, :])
                        dve.tensor_scalar(kc[s][:, 1, :], c[:, 2, :], cols[:, C_K2:C_K2 + 1], None, ALU.add)
                        end(dve.tensor_scalar(kc[s][:, 2, :], c[:, 3, :], cols[:, C_KVC:C_KVC + 1], None, ALU.add))

                    def ctx_split(k, s):
                        after(dve, "dve", (s, "ctx_k"))
                        do(dve.tensor_copy(kcp[s][:, :, 0, :], kc[s][:, 0:3, :]))
                        do(dve.tensor_tensor(kcr[s][:, :, :], kc[s][:, 0:3, :], kcp[s][:, :, 0, :], ALU.subtract))
                        do(dve.tensor_copy(kcp[s][:, :, 1, :], kcr[s][:, :, :]))
                        end(dve.tensor_tensor(kcp[s][:, :, 2, :], kcr[s][:, :, :], kcp[s][:, :, 1, :], ALU.subtract))

                    def ln_stats(k, s, m):
                        if m == 0:
                            dve.wait_ge(x_in[s], 16)
                        else:
                            prev = {1: ("attn_out", 0), 2: ("attn_out", 1), 3: ("mlp_out", 0), 4: ("l1_add",), 5: ("attn_out", 2),
                                    6: ("attn_out", 3), 7: ("attn_out", 4)}[m]
                            after(dve, "dve", (s, *prev))
                        for t in range(TB):
                            ins = dve.bn_stats(stats[s][:, t, :], x[s][:, t, :])
                        do(ins)
                        for t in range(TB):
                            ins = dve.bn_aggr(mv[s][:, t, :], stats[s][:, t, :])
                        do(ins)
                        end(dve.tensor_scalar(var[s][:, :], mv[s][:, :, 1], EPS[m], None, ALU.add))

                    def rope(k, s, w, r):
                        after(dve, "pe", k)
                        tab = ((cosq, sinq), (cosk, sink))[w][r]
                        if r == 0:
                            end(dve.tensor_tensor(r1[w][s][:, :], bank(k)[:, :], tab[:, :], ALU.mult))
                        else:
                            do(dve.tensor_tensor(r2[w][s][:, :], bank(k)[:, :], tab[:, :], ALU.mult))
                            end(dve.tensor_tensor(qf[w][s][:, :], r1[w][s][:, :], r2[w][s][:, :], ALU.add))

                    def parts(k, s, a, w):
                        after(dve, "act", (s, "part1", a, w))
                        q, part = qf[w][s], qp[w][s]
                        do(dve.tensor_tensor(r1[w][s][:, :], q[:, :], part[:, 0, :], ALU.subtract))
                        do(dve.tensor_copy(part[:, 1, :], r1[w][s][:, :]))
                        end(dve.tensor_tensor(part[:, 2, :], r1[w][s][:, :], part[:, 1, :], ALU.subtract))

                    def max(k, s, a, hg, t):
                        after(dve, "pe", k)
                        b = mxb[MAX_AT[k] % 2]
                        dst = mx[s][:, hg % 2]
                        if a in SELF:
                            g, e, qb = t // 8, t // 4 % 2, t % 4
                            end(dve.tensor_reduce(dst[:, qb, g, e:e + 1], b[:, :], AX.X, ALU.max))
                        else:
                            end(dve.tensor_reduce(dst[:, t, :, :].rearrange("p g e -> p (g e)"),
                                                  b[:, 0:4 * NK].rearrange("p (h n) -> p h n", h=4), AX.X, ALU.max))

                    def max_parts(k, s, a, hg):
                        after(dve, "dve", (s, "max", a, hg, tiles(a) - 1))
                        m = mx[s][:, hg % 2].rearrange("p t g e -> p (t g) e")
                        part = mp[s][:, hg % 2].rearrange("p t g c e -> p (t g) c e")
                        do(dve.tensor_scalar(part[:, :, 0, :], m, -1.0, None, ALU.mult))
                        do(dve.scalar_tensor_tensor(mr[s][:, :, :], m, -1.0, part[:, :, 0, :], ALU.mult, ALU.subtract))
                        do(dve.tensor_copy(part[:, :, 1, :], mr[s][:, :, :]))
                        end(dve.tensor_tensor(part[:, :, 2, :], mr[s][:, :, :], part[:, :, 1, :], ALU.subtract))

                    def max_t(k, s, a, hg):
                        after(dve, "pe", k)
                        if (a, hg) >= (0, 2):
                            dve.wait_ge(mrows[s], 32 * (4 * a + hg - 1))
                        end(dve.tensor_copy(mrow[s][:, hg % 2, :], mtb[0:12, 0:T]))

                    def heads_t(k, s, a, ab):
                        after(dve, "pe", k)
                        c = bank(k)[:, :].rearrange("p (t j q v d) -> p t j q v d", t=TB, j=4, q=2, v=2)
                        rc = rec[s][:, ab]
                        do(dve.reciprocal(rc.rearrange("p t j q -> p (t j) q"),
                                          bank(k)[:, :].rearrange("p (tj q w) -> p tj q w", q=2, w=16)[:, :, :, 8]))
                        for par in range(2):
                            o = ao[s][:, :, 64 * ab + 32 * par:64 * ab + 32 * par + 32].rearrange("p t (j d) -> p t j d", j=4)
                            ins = dve.tensor_tensor(o, c[:, :, :, par, 0, :], rc[:, :, :, par:par + 1].to_broadcast([P, TB, 4, HD]), ALU.mult)
                        end(ins)

                    def add_residual(k, s):
                        end(dve.tensor_tensor(x[s][:, :, :], x[s][:, :, :], blocks(bank(k)[:, :]), ALU.add))

                    def attn_out(k, s, a):
                        after(dve, "pe", k)
                        after(dve, "pool", (s, "bias", a) if a >= 2 else (s, "ln_norm", a))
                        add_residual(k, s)

                    def mlp_out(k, s, m):
                        after(dve, "pe", k)
                        after(dve, "pool", (s, "bias", 5 + m))
                        add_residual(k, s)

                    def l1_scores(k, s):
                        after(dve, "pe", k)
                        do(dve.tensor_reduce(m1[s][:, :], bank(k)[:, 0:TB * NK].rearrange("p (t n) -> p t n", t=TB), AX.X, ALU.max))
                        end(dve.tensor_scalar(nm1[s][:, :], m1[s][:, :], -SCALE1, None, ALU.mult))

                    def l1_probs(k, s):
                        after(dve, "act", (s, "l1_exp"))
                        do(dve.reciprocal(rs1[s][:, :], s1[s][:, :]))
                        end(dve.tensor_tensor(pn[s][:, :, :], es[s][:, :, :],
                                              rs1[s][:, :].rearrange("p (t a) -> p t a", a=1).to_broadcast([P, TB, NK]), ALU.mult))

                    def over_e(ap):
                        return ap.rearrange("p (t a) -> p t a", a=1).to_broadcast([P, TB, E])

                    def router(k, s):
                        after(dve, "pe", k)
                        do(dve.tensor_tensor(lg[s][:, :, :], bank(k)[:, 0:TB * E].rearrange("p (t e) -> p t e", t=TB),
                                             rt_b[s][:, :].rearrange("p (a e) -> p a e", a=1).to_broadcast([P, TB, E]), ALU.add))
                        do(dve.tensor_reduce(lm[s][:, :], lg[s][:, :, :], AX.X, ALU.max))
                        end(dve.tensor_tensor(lsub[s][:, :, :], lg[s][:, :, :], over_e(lm[s][:, :]), ALU.subtract))

                    def router_probs(k, s):
                        after(dve, "act", (s, "router_exp"))
                        do(dve.tensor_reduce(lsum[s][:, :], lex[s][:, :, :], AX.X, ALU.add))
                        do(dve.reciprocal(lrec[s][:, :], lsum[s][:, :]))
                        end(dve.tensor_tensor(prob[s][:, :, :], lex[s][:, :, :], over_e(lrec[s][:, :]), ALU.mult))

                    def expert_out(k, s, t):
                        after(dve, "pe", k)
                        after(dve, "dve", (s, "router_probs"))
                        c = bank(k)
                        do(dve.tensor_scalar(ro[s][:, t, :], c[:, 0:D], prob[s][:, t, 0:1], None, ALU.mult))
                        do(dve.scalar_tensor_tensor(ro[s][:, t, :], c[:, D:2 * D], prob[s][:, t, 1:2], ro[s][:, t, :], ALU.mult, ALU.add))
                        end(dve.scalar_tensor_tensor(ro[s][:, t, :], c[:, 2 * D:3 * D], prob[s][:, t, 2:3], ro[s][:, t, :], ALU.mult, ALU.add))

                    def l1_add(k, s):
                        after(dve, "act", (s, "gate"))
                        after(dve, "dve", (s, "expert_out", TB - 1))
                        after(dve, "pool", (s, "ln_norm", 3))
                        do(dve.scalar_tensor_tensor(ro2[s][:, :, :], gt[s][:, :, :], 1.0, ro[s][:, :, :], ALU.add, ALU.mult))
                        end(dve.scalar_tensor_tensor(x[s][:, :, :], ro2[s][:, :, :], 0.5, x[s][:, :, :], ALU.mult, ALU.add))

                    parts_ = locals()
                    for step in PLAN:
                        if "dve" in STEPS[step[1]]:
                            parts_[step[1]](step, step[0], *step[2:])

                @block.tensor
                def _(pe):
                    def end(ins):
                        ins.then_inc(done["pe"], 1)

                    def gates(k, s, l):
                        b = chain_bank(pe, k)
                        after(pe, "dve", (s, "select"))
                        w, r = ((w_ada, R_ADA), (w_mod, R_MOD))[l]
                        for g in range((3, 2)[l]):
                            o = b[:, g * D:(g + 1) * D]
                            pe.matmul(o, cb[s][:, l, :], w[:, (3 * g + 2) * D:(3 * g + 3) * D], start=True, stop=False)
                            ins = pe.matmul(o, ones[0:1, :], rows[0:1, r + g, :], start=False, stop=True)
                        end(ins)

                    def anchor(k, s):
                        b = chain_bank(pe, k)
                        after(pe, "dve", (s, "select"))
                        for i in range(7):
                            w = w_e1[:, 2, i // 2, (i % 2) * P:(i % 2 + 1) * P] if i < 6 else w_g1[:, 2, :]
                            pe.matmul(b[:, i:i + 1], w, cc[s][:, 0:1], start=True, stop=True)
                        pe.matmul(b[:, 8:8 + E], cb[s][:, 0, :], w_rt[:, 2, :], start=True, stop=False)
                        end(pe.matmul(b[:, 8:8 + E], ones[0:1, :], rt_row[0:1, :], start=False, stop=True))

                    def ctx_t(k, s):
                        b = chain_bank(pe, k)
                        after(pe, "pool", (s, "ctx_norm"))
                        for j in range(3):
                            src = cx[s][:, :] if j == 0 else cxn[s][:, j - 1, :]
                            ins = pe.transpose(b[:, j * NK:(j + 1) * NK], src, ident[0:NK, 0:NK])
                        end(ins)

                    def ctx_k(k, s):
                        b = chain_bank(pe, k)
                        after(pe, "act", (s, "ctx_t"))
                        for l, (w, j) in enumerate(((w_ck, 0), (w_k1, 0), (w_kv2, 1), (w_kvc3, 2))):
                            ins = pe.matmul(b[:, l * NK:(l + 1) * NK], w[:, 0:D], cxt[s][:, j, :], start=True, stop=True)
                        end(ins)

                    def ctx_v(k, s):
                        b = chain_bank(pe, k)
                        after(pe, "act", (s, "ctx_t"))
                        for l, (w, j, o) in enumerate(((w_cv, 0, 0), (w_v1, 0, 0), (w_kv2, 1, D), (w_kvc3, 2, D))):
                            ins = pe.matmul(b[0:NK, l * D:(l + 1) * D], cxt[s][:, j, :], w[:, o:o + D], start=True, stop=True)
                        end(ins)

                    def ln_t(k, s, m):
                        b = chain_bank(pe, k)
                        after(pe, "pool", (s, "ln_norm", m))
                        for t in range(TB):
                            ins = pe.transpose(b[:, t * P:(t + 1) * P], xn[s][:, t, :], ident[:, :])
                        end(ins)

                    def rope(k, s, w, r):
                        b = chain_bank(pe, k)
                        after(pe, "act", (s, "ln_t", 0))
                        m = (w_qkv0, w_rot)[r]
                        end(pe.matmul(b[:, :], m[:, w * D:(w + 1) * D], xt[s][:, :], start=True, stop=True))

                    def proj(k, s, a, w):
                        b = chain_bank(pe, k)
                        after(pe, "act", (s, "ln_t", LN_OF[a]))
                        m, o = QKIN[a]
                        end(pe.matmul(b[:, :], m[:, o + w * D:o + (w + 1) * D], xt[s][:, :], start=True, stop=True))

                    def v(k, s, a):
                        b = chain_bank(pe, k)
                        w = w_qkv0 if a == 0 else w_qkv3
                        for t in range(TB):
                            ins = pe.matmul(b[:, t * D:(t + 1) * D], xt[s][:, t * P:(t + 1) * P], w[:, 2 * D:3 * D], start=True, stop=True)
                        end(ins)

                    def max(k, s, a, hg, t):
                        if (hg, t) == (0, 0):
                            pe.wait_ge(qread[s], 16 * COMBOS * (a + 1))
                            if a in SELF:
                                pe.wait_ge(kread[s], 32 * (SELF.index(a) + 1))
                            elif a == 1:
                                pe.wait_ge(cread[s], 96)
                        n = MAX_AT[k]
                        if n >= 2:
                            after(pe, "dve", MAX_STEPS[n - 2])
                        b = mxb[n % 2]
                        R = MASKROW + 1
                        if a in SELF:
                            g, e, qb = 2 * hg + t // 8, t // 4 % 2, t % 4
                            ins = pe.matmul(b[:, :], qs[s][0:R, g, qb * P:(qb + 1) * P], ks[s][0:R, e, g, :], start=True, stop=(a != 0))
                            if a == 0:
                                ins = pe.matmul(b[:, :], identb[:, :], mask_q[:, qb, :], start=False, stop=True)
                        else:
                            for g in range(2):
                                ins = pe.matmul(b[:, g * 2 * NK:(g + 1) * 2 * NK], qs[s][0:R, 2 * hg + g, t * P:(t + 1) * P],
                                                ksc[s][0:R, CL[a], 2 * hg + g, :, :].rearrange("p e n -> p (e n)"), start=True, stop=True)
                        end(ins)

                    def max_t(k, s, a, hg):
                        after(pe, "dve", (s, "max_parts", a, hg))
                        m = MAXT.index(k)
                        if m:
                            after(pe, "dve", MAXT[m - 1])
                        for t in range(TB):
                            ins = pe.transpose(mtb[0:12, t * P:(t + 1) * P], mp[s][:, hg % 2, t].rearrange("p g c e -> p (g c e)"), identb[:, :])
                        end(ins)

                    def exp(k, s, a, hg, t):
                        n = EXP_AT[k]
                        if t == 0:
                            pe.wait_ge(mrows[s], 32 * (4 * a + hg + 1))
                        if n >= 2:
                            after(pe, "act", EXP_STEPS[n - 2])
                        b = exb[n % 2]
                        j, kb = t % 4, t // 4
                        g, e = 2 * hg + j // 2, j % 2
                        if a in SELF:
                            ins = pe.matmul(b[:, :], ks[s][0:ROWS, e, g, kb * P:(kb + 1) * P], qs[s][0:ROWS, g, :], start=True, stop=(a != 0))
                            if a == 0:
                                ins = pe.matmul(b[:, :], identb[:, :], mask_k[:, kb, :], start=False, stop=True)
                        else:
                            ins = pe.matmul(b[0:NK, :], ksc[s][0:ROWS, CL[a], g, e, :], qs[s][0:ROWS, g, :], start=True, stop=True)
                        end(ins)

                    def pv(k, s, a, hg, kb):
                        last = tiles(a) // 4 - 1
                        after(pe, "act", (s, "exp", a, hg, 4 * kb + 3))
                        if (hg, kb) == (0, 0):
                            after(pe, "act", (s, "v", a) if a in SELF else (s, "ctx_v"))
                        if hg % 2 == 0 and kb == 0:
                            m = PV_OUT.index((s, "pv_out", a, hg // 2))
                            if m:
                                after(pe, "act", PV_OUT[m - 1])
                        n = EXP_AT[(s, "exp", a, hg, 4 * kb)] % (4 * NSLOT)
                        K = P if a in SELF else NK
                        for j in range(4):
                            w = va[s][:, hg % 2, kb, hg // 2, j, :] if a in SELF else vac[s][:, CL[a], hg % 2, hg // 2, j, :]
                            ins = pe.matmul(pvb[32 * j:32 * j + 32, :], w, pr[0:K, n + j, :],
                                            start=(hg % 2 == 0 and kb == 0), stop=(hg % 2 == 1 and kb == last), skip_group_check=True)
                        end(ins)

                    def heads_t(k, s, a, ab):
                        b = chain_bank(pe, k)
                        after(pe, "act", (s, "pv_out", a, ab))
                        for t in range(TB):
                            ins = pe.transpose(b[:, t * P:(t + 1) * P], u[s][:, ab, t * P:(t + 1) * P], ident[:, :])
                        end(ins)

                    def attn_t(k, s, a):
                        b = chain_bank(pe, k)
                        after(pe, "dve", (s, "heads_t", a, 1))
                        for t in range(TB):
                            ins = pe.transpose(b[:, t * P:(t + 1) * P], ao[s][:, t, :], ident[:, :])
                        end(ins)

                    def attn_out(k, s, a):
                        b = chain_bank(pe, k)
                        after(pe, "act", (s, "attn_t", a))
                        if a in (0, 1, 3):
                            after(pe, "pool", (s, "gated"))
                        w = (g_o0[s], g_co[s], w_p2, g_pr[s], w_cp3)[a]
                        for t in range(TB):
                            ins = pe.matmul(b[:, t * D:(t + 1) * D], aot[s][:, t * P:(t + 1) * P], w[:, :], start=True, stop=True)
                        end(ins)

                    def l1_scores(k, s):
                        b = chain_bank(pe, k)
                        after(pe, "act", (s, "proj", 5, 0))
                        after(pe, "dve", (s, "ctx_k"))
                        for t in range(TB):
                            ins = pe.matmul(b[:, t * NK:(t + 1) * NK], qf[0][s][:, t * P:(t + 1) * P], kc[s][:, 3, :], start=True, stop=True)
                        end(ins)

                    def l1_probs_t(k, s):
                        b = chain_bank(pe, k)
                        after(pe, "dve", (s, "l1_probs"))
                        for t in range(TB):
                            ins = pe.transpose(b[0:NK, t * P:(t + 1) * P], pn[s][:, t, :], ident[:, :])
                        end(ins)

                    def l1_evidence(k, s):
                        b = chain_bank(pe, k)
                        after(pe, "act", (s, "l1_probs_t"))
                        end(pe.matmul(b[:, :], vc1[s][:, :], pt[s][:, :], start=True, stop=True))

                    def router(k, s):
                        b = chain_bank(pe, k)
                        after(pe, "act", (s, "l1_evidence"))
                        for t in range(TB):
                            o = b[:, t * E:(t + 1) * E]
                            pe.matmul(o, xt[s][:, t * P:(t + 1) * P], w_rt[:, 0, :], start=True, stop=False)
                            ins = pe.matmul(o, evt[s][:, t * P:(t + 1) * P], w_rt[:, 1, :], start=False, stop=True)
                        end(ins)

                    def hidden(k, s, w0, w1):
                        b = chain_bank(pe, k)
                        pe.matmul(b[:, :], w0, xt[s][:, :], start=True, stop=False)
                        end(pe.matmul(b[:, :], w1, evt[s][:, :], start=False, stop=True))

                    def expert_h(k, s, i):
                        hidden(k, s, *[w_e1[:, c, i // 2, (i % 2) * P:(i % 2 + 1) * P] for c in range(2)])

                    def gate_h(k, s):
                        hidden(k, s, w_g1[:, 0, :], w_g1[:, 1, :])

                    def gate(k, s):
                        b = chain_bank(pe, k)
                        after(pe, "act", (s, "gate_h"))
                        for t in range(TB):
                            o = b[:, t * D:(t + 1) * D]
                            pe.matmul(o, gh[s][:, t * P:(t + 1) * P], w_g2[:, :], start=True, stop=False)
                            ins = pe.matmul(o, ones[0:1, :], rows[0:1, R_G2, :], start=False, stop=True)
                        end(ins)

                    def expert_out(k, s, t):
                        b = chain_bank(pe, k)
                        after(pe, "act", (s, "expert_h", 2 * E - 1))
                        for e in range(E):
                            o = b[:, e * D:(e + 1) * D]
                            for c in range(2):
                                pe.matmul(o, hid[s][:, 2 * e + c, t * P:(t + 1) * P], w_e2o[:, 2 * e + c, :], start=(c == 0), stop=False)
                            ins = pe.matmul(o, ones[0:1, :], e2_row[0:1, e * D:(e + 1) * D], start=False, stop=True)
                        end(ins)

                    def mlp_h(k, s, m, c):
                        b = chain_bank(pe, k)
                        after(pe, "act", (s, "ln_t", LN_OF_MLP[m]))
                        end(pe.matmul(b[:, :], w_m1[m][:, c * P:(c + 1) * P], xt[s][:, :], start=True, stop=True))

                    def mlp_out(k, s, m):
                        b = chain_bank(pe, k)
                        after(pe, "act", (s, "mlp_h", m, FC - 1))
                        after(pe, "pool", (s, "gated"))
                        for t in range(TB):
                            for c in range(FC):
                                ins = pe.matmul(b[:, t * D:(t + 1) * D], hid[s][:, c, t * P:(t + 1) * P], g_m2[m][s][:, c, :],
                                                start=(c == 0), stop=(c == FC - 1))
                        end(ins)

                    parts = locals()
                    for step in PLAN:
                        if "pe" in STEPS[step[1]]:
                            parts[step[1]](step, step[0], *step[2:])

            nc.gpsimd.sem_clear(range(in_loop0.num, last_sem.num + 1))
            nc.all_engine_barrier(sem_only=True)


_ACT = ["x", "cond_1024", "ctx_1024"]
_MASKS = ["mask_BxS2_bf1", "mask_SxS_bk0"]


def constants():
    n = T // 2
    inv_freq = 1.0 / 10000.0 ** (np.arange(0, HD, 2, dtype=np.float32) / HD)
    freqs = np.outer(np.arange(n, dtype=np.float32), inv_freq)
    emb = np.concatenate([freqs, freqs], axis=-1)
    table = lambda f: np.ascontiguousarray(np.tile(f(emb).astype(np.float32).T, (H, 2)))
    tail = np.zeros((P, 2), np.float32)
    for part in range(3):
        for e in range(2):
            tail[MROW + 2 * part + e, e] = 1.0
    return {"c_ident": np.eye(P, dtype=np.float32), "c_cos": table(np.cos), "c_sin": table(np.sin), "c_tail": tail}


def kernel(**inputs):
    import concourse.bacc as bacc
    from concourse.bass_utils import run_bass_kernel_spmd

    nc = bacc.Bacc("TRN2", target_bir_lowering=False, num_devices=1)
    arrays = {}
    for name, a in inputs.items():
        a = np.ascontiguousarray(a)
        arrays[name] = a
    arrays.update(constants())
    io = {name: nc.dram_tensor(name, a.shape, mybir.dt.from_np(a.dtype), kind="ExternalInput").ap() for name, a in arrays.items()}
    out = nc.dram_tensor("out", [B, T, D], F32, kind="ExternalOutput").ap()
    build(nc, io, out)
    r = run_bass_kernel_spmd(nc, [arrays], core_ids=[0])
    return r.results[0]["out"]
```

```python
from contextlib import ExitStack

import numpy as np

import concourse.bass as bass
from concourse import mybir

F32 = mybir.dt.float32
BF16 = mybir.dt.bfloat16
U8 = mybir.dt.uint8
ALU = mybir.AluOpType
ACT = mybir.ActivationFunctionType
AX = mybir.AxisListType

P = 128
B, T, D = 4, 512, 128
NS = 2
H, HD = 16, 8
NK = 77
TB = T // P
G = H // 2
HG = 4
E, RH = 3, 256
FC = 4
ROPE = T // 2
COMBOS = 6
QSLOT = (0, 0, 1, 1, 2, 0)
STACK = 2 * HD * COMBOS
MASKROW = STACK
MROW = STACK + 1
ROWS = MROW + 6
BIG = 1e30
SCALE = float(HD) ** -0.5
SCALE1 = float(D) ** -0.5
CORES = ((0, 0), (1, 0), (0, 3), (1, 3))
SELF, CROSS = (0, 3), (1, 2, 4)
CL = {1: 0, 2: 1, 4: 2}
NSLOT = 3

EPS = (1e-5, 1e-5, 1e-5, 1e-5, 1e-5, 1e-6, 1e-6, 1e-6)
NMOD = 19
NLN = 9
GATES = (2, 5, 8, 15, 18)

SETUP_W = (("w_ada", 9 * D), ("w_ssq", 2 * D), ("w_sskv", 2 * D), ("w_mod", 6 * D), ("w_out", D),
           ("w_anchor", 7 * D), ("w_e2", 2 * E * D))
EARLY_W = (("cols", 32), ("mod_b", NMOD), ("e_b2", E), ("ident", P), ("tail", 2), ("w_rt", 3 * E), ("w_qkv0", 3 * D),
           ("w_o0", D), ("w_co", D), ("w_p2", D), ("w_pr3", D), ("w_cp3", D), ("w_ck", D), ("w_k1", D),
           ("w_cv", D), ("w_v1", D), ("w_kv2", 2 * D), ("w_kvc3", 2 * D))
LATE_W = (("w_cq", D), ("w_m10", FC * P), ("w_m20", FC * D), ("w_q1", D), ("w_e1", 2 * E * RH), ("w_g1", 2 * D),
          ("w_g2", D), ("w_q2", D), ("w_qkv3", 3 * D), ("w_qc3", D), ("w_m11", FC * P), ("w_m21", FC * D))
C_NW, C_GB, C_M1, C_E1, C_G1, C_Q2, C_K2, C_V2, C_QKV3, C_QC, C_KVC = 0, 3, (5, 9), 13, 19, 20, 21, 22, 23, 26, 27
R_M2, R_P2, R_PR3, R_CP3, R_OUT, R_G2, NROW = (0, 1), 2, 3, 4, 5, 6, 7

ENGINES = ("pe", "act", "dve", "pool", "sp")

STEPS = {
    "load": ("sp",), "select": ("dve",), "gate_cols": ("dve",), "ctx_stats": ("dve",), "ctx_norm": ("pool",),
    "gates": ("pe", "dve"),
    "ctx_t": ("pe", "act"), "ctx_k": ("pe", "dve"), "ctx_v": ("pe", "act"), "ctx_split": ("dve",),
    "ctx_out": ("sp",), "ctx_stack": ("sp",),
    "ln_stats": ("dve",), "ln_norm": ("pool",), "ln_t": ("pe", "act"),
    "rope": ("pe", "dve"), "proj": ("pe", "act"), "v": ("pe", "act"),
    "part1": ("act",), "parts": ("dve",), "parts_out": ("sp",), "stack": ("sp",),
    "max": ("pe", "dve"), "max_parts": ("dve",), "max_t": ("pe", "dve"), "max_rows": ("sp",),
    "exp": ("pe", "act"), "pv": ("pe",), "pv_out": ("act",),
    "heads_t": ("pe", "dve"), "attn_t": ("pe", "act"), "attn_out": ("pe", "dve"), "bias": ("pool",),
    "l1_scores": ("pe", "dve"), "l1_exp": ("act",), "l1_probs": ("dve",), "l1_probs_t": ("pe", "act"),
    "l1_evidence": ("pe", "act"), "router": ("pe", "dve"), "router_exp": ("act",),
    "router_probs": ("dve",), "expert_h": ("pe", "act"), "gate_h": ("pe", "act"),
    "gate": ("pe", "act"), "expert_out": ("pe", "dve"), "l1_add": ("dve",),
    "mlp_h": ("pe", "act"), "mlp_out": ("pe", "dve"),
    "store": ("sp",),
}
CHAIN = {k: (k, v[1]) for k, v in STEPS.items()
         if v[0] == "pe" and len(v) == 2 and k not in ("max", "exp")}
CHAIN["l1_scores"] = ("l1_exp", "act")


def tiles(a):
    return 16 if a in SELF else 4


def attention(s, a):
    n = tiles(a)
    items = [(s, "max", a, 0, t) for t in range(n)] + [(s, "max_parts", a, 0)]
    for t in range(n):
        items.append((s, "max", a, 1, t))
        if t == 1:
            items += [(s, "max_t", a, 0), (s, "max_rows", a, 0)]
    items.append((s, "max_parts", a, 1))
    for hg in range(HG):
        for k in range(n // 4):
            block = []
            for t in range(4 * k, 4 * k + 4):
                if hg + 2 < HG:
                    block.append((s, "max", a, hg + 2, t))
                block.append((s, "exp", a, hg, t))
                if t == 1 and hg + 1 < HG:
                    block += [(s, "max_t", a, hg + 1), (s, "max_rows", a, hg + 1)]
            if k == n // 4 - 1 and hg + 2 < HG:
                block.append((s, "max_parts", a, hg + 2))
            items.append(("block", block, (s, "pv", a, hg, k)))
    return items


def of(s, *steps):
    return [(s, *step) for step in steps]


def attention_end(s, a):
    return of(s, ("heads_t", a, 0), ("heads_t", a, 1), ("attn_t", a), ("attn_out", a))


def norm(s, n):
    return of(s, ("ln_stats", n), ("ln_norm", n), ("ln_t", n))


def split(s, a, w):
    return of(s, ("part1", a, w), ("parts", a, w), ("parts_out", a, w))


def self_in(s, a, n):
    if a == 0:
        q, k = (of(s, ("rope", w, 0), ("rope", w, 1)) for w in range(2))
        steps = (of(s, ("load",), ("select",)) + norm(s, n) + of(s, ("ctx_stats",)) + q + split(s, a, 0) + k
                 + of(s, ("stack", a, 0)) + split(s, a, 1)
                 + of(s, ("v", a), ("ctx_norm",), ("gate_cols",), ("ctx_t",), ("ctx_k",), ("ctx_v",), ("gates", 0), ("gates", 1),
                      ("ctx_split",), ("ctx_out",), ("ctx_stack",)))
        if s == 0:
            steps.insert(steps.index((s, "v", a)), (s, "stack", a, 1, 0))
            steps.insert(steps.index((s, "v", a)), (s, "stack", a, 1, 1))
            return steps
    else:
        steps = (norm(s, n) + of(s, ("proj", a, 0), ("bias", a), ("proj", a, 1)) + split(s, a, 0) + split(s, a, 1)
                 + of(s, ("stack", a, 0), ("v", a)))
    return steps + of(s, ("stack", a, 1, 0), ("stack", a, 1, 1))


def cross(s, a, n):
    core = attention(s, a)
    core.insert(len(core) - 1, (s, "heads_t", a, 0))
    return (norm(s, n) + (of(s, ("bias", a)) if a != 1 else []) + of(s, ("proj", a, 0)) + split(s, a, 0)
            + of(s, ("stack", a, 0)) + core + attention_end(s, a)[1:])


def mlp(s, m, n):
    return norm(s, n) + of(s, ("bias", 5 + m)) + [("bunch", of(s, *[("mlp_h", m, c) for c in range(FC)]))] + of(s, ("mlp_out", m))


def layer1(s):
    return (norm(s, 3) + of(s, ("proj", 5, 0), ("l1_scores",), ("l1_exp",), ("l1_probs",), ("l1_probs_t",), ("l1_evidence",),
                            ("router",), ("router_exp",), ("router_probs",))
            + [("bunch", of(s, ("gate_h",), *[("expert_h", i) for i in range(2 * E)]))]
            + of(s, ("gate",), *[("expert_out", t) for t in range(TB)], ("l1_add",)))


def middle(s):
    return (attention_end(s, 0) + cross(s, 1, 1) + mlp(s, 0, 2) + layer1(s) + cross(s, 2, 4) + self_in(s, 3, 5))


def last(s):
    return attention_end(s, 3) + cross(s, 4, 6) + mlp(s, 1, 7) + of(s, ("store",))


WEIGHT = {"ln_stats": 2.5, "ln_norm": 3, "ln_t": 1.5, "parts_out": 2.5, "stack": 3, "max": .6, "exp": .5, "block": 4,
          "bunch": 4, "mlp_out": 4, "heads_t": 2, "attn_t": 1.5, "attn_out": 2, "parts": 1.5, "max_t": 1, "max_rows": 2,
          "expert_out": 1, "load": 0, "select": 0, "bias": .2}


def weight(item):
    return WEIGHT.get(item[0] if item[0] in ("block", "bunch") else item[1], 1)


class Plan:

    def __init__(self):
        self.steps, self.waiting = [], None

    def product(self):
        if self.waiting:
            s, _, a, hg, k = self.waiting
            self.steps.append(self.waiting)
            if k == tiles(a) // 4 - 1 and hg % 2:
                self.steps.append((s, "pv_out", a, hg // 2))
            self.waiting = None

    def item(self, item):
        if item[0] == "block":
            for step in item[1]:
                self.steps.append(step)
            self.close(item)
        elif item[0] == "bunch":
            self.steps += item[1]
        else:
            if item[1] == "heads_t" and self.waiting and self.waiting[0] == item[0]:
                self.product()
            self.steps.append(item)

    def close(self, block):
        self.product()
        self.waiting = block[2]

    def merge(self, main, other, lead=0.0):
        other = list(other)
        total, rest = sum(map(weight, main)), sum(map(weight, other))
        spent = gone = 0.0

        def held(item):
            return item[0] not in ("block", "bunch") and item[1] == "stack" and len(item) == 5 and group <= 2 * item[4] + 1

        group = 0

        def catch_up(inside):
            nonlocal gone
            while other and gone < rest * (spent / total) + lead:
                if inside and other[0][0] in ("block", "bunch") or held(other[0]):
                    return
                gone += weight(other[0])
                self.item(other.pop(0))

        for item in main:
            catch_up(False)
            if item[0] != "block":
                self.item(item)
                spent += weight(item)
                continue
            group = item[2][3]
            for step in item[1]:
                self.steps.append(step)
                spent += weight(item) / len(item[1])
                catch_up(True)
            self.close(item)
        for item in other:
            self.item(item)


def plan():
    p = Plan()
    p.merge([], self_in(0, 0, 0))
    p.merge(attention(0, 0), self_in(1, 0, 0))
    p.merge(attention(1, 0), middle(0))
    p.merge(attention(0, 3), middle(1))
    p.merge(attention(1, 3), last(0))
    p.merge([], last(1))
    return p.steps


PLAN = plan()

ORDER = {e: {} for e in ENGINES}
for step_ in PLAN:
    for e_ in STEPS[step_[1]]:
        assert step_ not in ORDER[e_], step_
        ORDER[e_][step_] = len(ORDER[e_]) + 1


def all_of(*kinds):
    return [s for s in PLAN if s[1] in kinds]


CHAIN_STEPS = all_of(*CHAIN)
CHAIN_AT = {s: n for n, s in enumerate(CHAIN_STEPS)}
MAX_STEPS, EXP_STEPS, PV_STEPS = all_of("max"), all_of("exp"), all_of("pv")
MAX_AT = {s: n for n, s in enumerate(MAX_STEPS)}
EXP_AT = {s: n for n, s in enumerate(EXP_STEPS)}
PV_OUT = [[s for s in all_of("pv_out") if s[0] == i] for i in range(NS)]


def before_in_plan(step, *kinds):
    found = None
    for other in PLAN:
        if other == step:
            return found
        if other[1] in kinds:
            found = other


def freed_by(step):
    kind, engine = CHAIN[step[1]]
    return engine, (step[0], kind, *step[2:])


def build(nc, io, out):
    ctx = ExitStack()
    with ctx:
        def sb(name, shape, dt=F32):
            return ctx.enter_context(nc.sbuf_tensor(name, shape, dt))

        def ps(name, shape, dt=F32):
            return ctx.enter_context(nc.psum_tensor(name, shape, dt))

        def sem(name):
            return ctx.enter_context(nc.semaphore(name))

        def per(name, shape, dt=F32):
            return [sb(f"{name}{s}", shape, dt) for s in range(NS)]

        def shared(name, shape, dt=F32):
            return [sb(name, shape, dt)] * NS

        def columns(table):
            return sum(n for _, n in table)

        def column(table, name):
            at = 0
            for other, n in table:
                if other == name:
                    return at, n
                at += n

        early = sb("early", [P, columns(EARLY_W)]); late = sb("late", [P, columns(LATE_W)])

        def w(name):
            for held, table in ((early, EARLY_W), (late, LATE_W)):
                if name in [other for other, _ in table]:
                    at, n = column(table, name)
                    return held[:, at:at + n]

        cols, mod_b, e_b2, ident, tail = w("cols"), w("mod_b"), w("e_b2"), w("ident"), w("tail")
        w_rt = w("w_rt").rearrange("p (c e) -> p c e", c=3)
        w_qkv0, w_o0, w_co, w_p2, w_pr3, w_cp3 = w("w_qkv0"), w("w_o0"), w("w_co"), w("w_p2"), w("w_pr3"), w("w_cp3")
        w_ck, w_k1, w_cv, w_v1, w_kv2, w_kvc3 = w("w_ck"), w("w_k1"), w("w_cv"), w("w_v1"), w("w_kv2"), w("w_kvc3")
        w_cq, w_q1, w_g2, w_q2, w_qkv3, w_qc3 = w("w_cq"), w("w_q1"), w("w_g2"), w("w_q2"), w("w_qkv3"), w("w_qc3")
        w_m1 = [w("w_m10"), w("w_m11")]
        w_m2 = [w(name).rearrange("p (c d) -> p c d", c=FC) for name in ("w_m20", "w_m21")]
        w_e1 = w("w_e1").rearrange("p (c e r) -> p c e r", c=2, e=E)
        w_g1 = w("w_g1").rearrange("p (c d) -> p c d", c=2)
        w_rot = sb("w_rot", [P, 2 * D]); w_e2o = sb("w_e2o", [P, 2 * E, D])
        cos = sb("cos", [P, ROPE]); sin = sb("sin", [P, ROPE])
        identb = sb("identb", [P, P], BF16); ones = sb("ones", [P, P])
        mod = sb("mod", [P, NMOD, B]); cond = sb("cond", [P, 2, B]); affine = sb("affine", [P, NLN, 2, B])
        anchors = sb("anchors", [P, 7, B]); rt_all = sb("rt_all", [P, B, E])
        g2_row = sb("g2_row", [1, D]); e2_row = sb("e2_row", [1, E * D])
        bias_b = sb("bias_b", [P, 5, D])
        mask_q = sb("mask_q", [P, TB, T], BF16); mask_k = sb("mask_k", [P, TB, T], BF16)
        eps_pow = sb("eps_pow", [P, 1])

        x = per("x", [P, TB, D])
        stats = per("stats", [P, TB, 6]); mv = per("mv", [P, TB, 2]); var = per("var", [P, TB]); rstd = per("rstd", [P, TB])
        cx = per("cx", [NK, D]); cstats = per("cstats", [NK, 6]); cmv = per("cmv", [NK, 2])
        cvar = per("cvar", [NK, 2]); crstd = per("crstd", [NK, 2])
        cmask = per("cmask", [P, NK], U8); cmaskf = per("cmaskf", [P, NK]); cany = per("cany", [P, 1])
        cbias = per("cbias", [P, NK], BF16)
        aff = per("aff", [P, NLN, 2]); anc = per("anc", [P, 7]); rt_b = per("rt_b", [P, E]); gcol = per("gcol", [P, 5])
        g_o0 = per("g_o0", [P, D]); g_co = per("g_co", [P, D]); g_pr = per("g_pr", [P, D])
        g_mlp = per("g_mlp", [P, 2, D]); g_bias = per("g_bias", [P, 3, D])
        kc = per("kc", [P, 4, NK])
        ksc = per("ksc", [P, 3, G, 2, NK], BF16); vac = per("vac", [NK, 3, 2, 2, 4, 32]); vc1 = per("vc1", [NK, D])
        qs = per("qs", [P, G, T], BF16); va = per("va", [P, 2, TB, 2, 4, 32])
        mx = per("mx", [P, 2, TB, 2, 2]); mr = per("mr", [P, TB * 2, 2]); mp = per("mp", [P, 2, TB, 2, 3, 2], BF16)
        mrow = per("mrow", [12, 2, T], BF16)
        u = per("u", [P, 2, T]); rec = per("rec", [P, 2, TB, 4, 2])
        m1 = per("m1", [P, TB]); nm1 = per("nm1", [P, TB]); s1 = per("s1", [P, TB]); rs1 = per("rs1", [P, TB])
        lg = per("lg", [P, TB, E]); lm = per("lm", [P, TB]); lsub = per("lsub", [P, TB, E]); lex = per("lex", [P, TB, E])
        lsum = per("lsum", [P, TB]); lrec = per("lrec", [P, TB]); prob = per("prob", [P, TB, E])
        gt, ro = ([u[s][:, i, :].rearrange("p (t d) -> p t d", t=TB) for s in range(NS)] for i in range(2))

        xn = shared("xn", [P, TB, D]); ao = xn
        cxn = [xn[0][0:NK, 0:2, :]] * NS
        es = [xn[0][:, :, :].rearrange("p t d -> p (t d)")[:, 0:TB * NK].rearrange("p (t n) -> p t n", t=TB)] * NS
        xt = shared("xt", [P, T]); aot = xt
        ro2 = [xt[s][:, :].rearrange("p (t d) -> p t d", t=TB) for s in range(NS)]
        ks = shared("ks", [P, 2, G, T], BF16)
        hid = shared("hid", [P, 2 * E, T])
        qf, r1, r2 = ([[hid[s][:, 2 * i + w, :] for s in range(NS)] for w in range(2)] for i in range(3))
        cb = [hid[s][:, 4:6, :].rearrange("p a n -> p (a n)")[:, 0:5 * P].rearrange("p (g m) -> p g m", g=5) for s in range(NS)]
        qp = [shared(f"qp{w}", [P, 3, T], BF16) for w in range(2)]
        evt = shared("evt", [P, T])
        kcp = [evt[s][:, 0:(9 * NK + 1) // 2].bitcast(BF16)[:, 0:9 * NK].rearrange("p (a b n) -> p a b n", a=3, b=3) for s in range(NS)]
        pg = shared("pg", [P, T]); gh = pg
        pt = [pg[s][0:NK, :] for s in range(NS)]
        cxt = [pg[s][:, 0:3 * NK].rearrange("p (c n) -> p c n", c=3) for s in range(NS)]
        kcr = [pg[s][:, 3 * NK:6 * NK].rearrange("p (c n) -> p c n", c=3) for s in range(NS)]
        pr = sb("pr", [P, NSLOT * 4, T])
        scratch = pr[:, :, :].rearrange("p a n -> p (a n)")
        sw = columns(SETUP_W)

        def setup_w(name):
            at, n = column(SETUP_W, name)
            return scratch[:, at:at + n]

        w_ada, w_ssq, w_sskv, w_mod, w_out = (setup_w(n) for n in ("w_ada", "w_ssq", "w_sskv", "w_mod", "w_out"))
        w_anchor = setup_w("w_anchor").rearrange("p (c d) -> p c d", c=7)
        w_e2 = setup_w("w_e2").rearrange("p (n d) -> p n d", n=2 * E)
        w_e2t = scratch[:, sw:sw + 2 * E * P].rearrange("p (e r) -> p e r", e=2 * E)
        mask_u = scratch[:, sw + 2 * E * P:sw + 2 * E * P + T].bitcast(U8).rearrange("p (t k) -> p t k", t=TB)
        rows = hid[0][0:1, 0:2, :].rearrange("p a n -> p (a n)")[:, 0:NROW * D].rearrange("p (r d) -> p r d", r=NROW)
        bvb = hid[0][:, 2, 0:3 * P].rearrange("p (a m) -> p a m", a=3)
        cb_all = hid[0][:, 3, :].rearrange("p (b m) -> p b m", b=B)
        rt_row = hid[0][0:1, 4, 0:E]

        chain = [ps(f"chain{n}", [P, T]) for n in range(2)]
        pvb = [ps(f"pvb{s}", [P, T]) for s in range(NS)]
        mxb = [ps(f"mxb{n}", [P, T]) for n in range(2)]
        exb = [ps(f"exb{n}", [P, T]) for n in range(2)]

        q_parts = [nc.dram_tensor(f"q_parts{s}", [3, P, T], BF16).ap() for s in range(NS)]
        k_parts = [nc.dram_tensor(f"k_parts{s}", [P, COMBOS, T], BF16).ap() for s in range(NS)]
        c_parts = [nc.dram_tensor(f"c_parts{s}", [3, P, COMBOS, NK], BF16).ap() for s in range(NS)]

        loaded, loaded_mask, loaded_late = sem("loaded"), sem("loaded_mask"), sem("loaded_late")
        set_pe, set_act, set_dve = sem("set_pe"), sem("set_act"), sem("set_dve")
        in_loop0 = sem("first_loop_semaphore")
        done = {e: sem(f"{e}_done") for e in ENGINES if e != "sp"}
        pe_done, act_done, dve_done, pool_done = (done[e] for e in ENGINES[:4])
        dve_link, pool_link = sem("dve_link"), sem("pool_link")
        x_in = [sem(f"x_in{s}") for s in range(NS)]; ctx_in = [sem(f"ctx_in{s}") for s in range(NS)]
        cwrit = [sem(f"ctx_parts_written{s}") for s in range(NS)]; cread = [sem(f"ctx_stacked{s}") for s in range(NS)]
        qwrit = [sem(f"q_parts_written{s}") for s in range(NS)]; kwrit = [sem(f"k_parts_written{s}") for s in range(NS)]
        qread = [sem(f"q_stacked{s}") for s in range(NS)]; kread = [[sem(f"k_stacked{s}_{h}") for h in range(2)] for s in range(NS)]
        mrows = [sem(f"max_rows{s}") for s in range(NS)]; stored = [sem(f"stored{s}") for s in range(NS)]
        last_sem = stored[-1]

        def link(eng, s, count, ins):
            ins.then_inc(s, 1)
            count[0] += 1
            eng.wait_ge(s, count[0])

        with nc.Block() as block:
            LOADS = 16 * 7

            @block.sync
            def _(sp):
                sp.dma_start(scratch[:, 0:sw], io["setup_w"]).then_inc(loaded, 16)
                sp.dma_start(early[:, :], io["early_w"]).then_inc(loaded, 16)
                sp.dma_start(late[:, :], io["late_w"]).then_inc(loaded_late, 16)

            @block.scalar
            def _(act):
                act.dma_start(cond[:, 0, :], io["cond_t"]).then_inc(loaded, 16)
                act.dma_start(mask_u[:, :, :], io["mask_SxS_bk0"].rearrange("(a p) k -> p a k", p=P)).then_inc(loaded_mask, 16)
                act.dma_start(cos[:, :], io["c_cos"]).then_inc(loaded, 16)
                act.dma_start(sin[:, :], io["c_sin"]).then_inc(loaded, 16)
                act.dma_start(rows[0:1, :, :], io["bias_rows"].rearrange("(a r) d -> a r d", a=1)).then_inc(loaded, 16)
                act.dma_start(rt_row[0:1, :], io["L1_xcond_router_b"].rearrange("(a e) -> a e", a=1)).then_inc(loaded, 16)
                act.wait_ge(loaded, LOADS)
                act.activation(cond[:, 1, :], cond[:, 0, :], ACT.Silu).then_inc(set_act, 1)

            MODW = ([(w_ada, c, 0) for c in range(9)] + [(w_ssq, c, 1) for c in range(2)]
                    + [(w_sskv, c, 1) for c in range(2)] + [(w_mod, c, 1) for c in range(6)])

            @block.vector
            def _(dve):
                n = [0]

                def do(ins):
                    link(dve, dve_link, n, ins)

                dve.memset(ones[:, :], 1.0)
                dve.memset(eps_pow[:, :], -0.5)
                for s in range(NS):
                    dve.memset(va[s][:, :, :, :, :, :], 0.0)
                    dve.memset(vac[s][:, :, :, :, :, :], 0.0)
                    do(dve.memset(qs[s][96:128, :, :], 1.0))
                    for par in range(2):
                        dve.memset(va[s][:, par, :, :, :, 16 * par + 8:16 * par + 16], 1.0)
                        dve.memset(vac[s][:, :, par, :, :, 16 * par + 8:16 * par + 16], 1.0)
                dve.wait_ge(loaded_mask, 16)
                dve.tensor_scalar(mask_q[:, :, :], mask_u[:, :, :], 1.0, BIG, ALU.subtract, ALU.mult)
                dve.wait_ge(loaded, LOADS)
                dve.tensor_copy(identb[:, :], ident[:, :])
                for i, c in enumerate((C_V2, C_QKV3 + 2, C_KVC + 1)):
                    dve.tensor_copy(bvb[:, i, :], cols[:, c:c + 1].to_broadcast([P, P]))
                dve.tensor_copy(cb_all[:, :, :], cond[:, 0, :].rearrange("p (b a) -> p b a", a=1).to_broadcast([P, B, P])).then_inc(set_dve, 1)
                wv = w_qkv0[:, 0:2 * D].rearrange("p (h r d) -> p h r d", r=2, d=HD // 2)
                rv = w_rot[:, :].rearrange("p (h r d) -> p h r d", r=2, d=HD // 2)
                dve.tensor_scalar(rv[:, :, 0, :], wv[:, :, 1, :], -1.0, None, ALU.mult)
                dve.tensor_copy(rv[:, :, 1, :], wv[:, :, 0, :])
                for e in range(2):
                    dve.tensor_copy(ks[0][:, e, :, :].rearrange("p g n -> p (g n)"), tail[:, e:e + 1].to_broadcast([P, G * T]))
                    for s in range(NS):
                        dve.tensor_copy(ksc[s][:, :, :, e, :].rearrange("p l g n -> p (l g) n"),
                                        tail[:, e:e + 1].rearrange("p (a b) -> p a b", a=1).to_broadcast([P, 3 * G, NK]))
                dve.wait_ge(set_pe, 1)
                do(dve.tensor_tensor(mod[:, :, :], chain[0][:, 0:NMOD * B].rearrange("p (c b) -> p c b", b=B),
                                     mod_b[:, :].rearrange("p (c a) -> p c a", a=1).to_broadcast([P, NMOD, B]), ALU.add))
                dve.tensor_tensor(anchors[:, :, :], chain[0][:, NMOD * B:(NMOD + 7) * B].rearrange("p (c b) -> p c b", b=B),
                                  cols[:, C_E1:C_E1 + 7].rearrange("p (c a) -> p c a", a=1).to_broadcast([P, 7, B]), ALU.add)
                dve.tensor_copy(rt_all[:, :, :], chain[0][:, (NMOD + 7) * B:(NMOD + 7) * B + B * E].rearrange("p (b e) -> p b e", b=B))
                for n_, (sh, sc) in ((0, (0, 1)), (1, (3, 4)), (2, (6, 7)), (4, (10, 9)), (5, (13, 14)), (7, (16, 17)), (8, (12, 11))):
                    if n_ < 3:
                        do(dve.tensor_scalar(affine[:, n_, 0, :], mod[:, sc, :], 1.0, None, ALU.add))
                        dve.tensor_scalar(affine[:, n_, 0, :], affine[:, n_, 0, :], cols[:, C_NW + n_:C_NW + n_ + 1], None, ALU.mult)
                    else:
                        dve.tensor_scalar(affine[:, n_, 0, :], mod[:, sc, :], 1.0, None, ALU.add)
                    dve.tensor_copy(affine[:, n_, 1, :], mod[:, sh, :])
                for k in range(2):
                    dve.tensor_copy(affine[:, 3, k, :], cols[:, C_GB + k:C_GB + k + 1].to_broadcast([P, B]))
                    dve.memset(affine[:, 6, k, :], 1.0 - k)
                dve.wait_ge(set_pe, 2)
                dve.tensor_copy(bias_b[:, 0:4, :], chain[1][:, :].rearrange("p (a d) -> p a d", a=4))
                dve.tensor_copy(bias_b[:, 4, :], pvb[1][:, 0:D])
                dve.tensor_copy(g2_row[0:1, :], rows[0:1, R_G2, :])
                dve.wait_ge(set_pe, 3)
                dve.tensor_copy(w_e2t[:, 0:4, :], mxb[0][:, :].rearrange("p (a r) -> p a r", a=4))
                dve.tensor_copy(w_e2t[:, 4:6, :], mxb[1][:, 0:2 * P].rearrange("p (a r) -> p a r", a=2)).then_inc(set_dve, 1)
                for kb in range(TB):
                    dve.wait_ge(set_pe, 4 + kb)
                    dve.tensor_copy(mask_k[:, kb, :], chain[kb % 2][:, :].bitcast(BF16)[:, 0:T]).then_inc(set_dve, 1)
                dve.wait_ge(set_pe, 8)
                dve.tensor_copy(w_e2o[:, 0:4, :], exb[0][:, :].rearrange("p (a r) -> p a r", a=4))
                dve.tensor_copy(w_e2o[:, 4:6, :], exb[1][:, 0:2 * P].rearrange("p (a r) -> p a r", a=2))
                dve.tensor_copy(e2_row[0:1, :], pvb[0][0:1, 0:E * D])

            @block.tensor
            def _(pe):
                pe.wait_ge(loaded, LOADS)
                pe.wait_ge(set_act, 1)
                pe.wait_ge(set_dve, 1)
                for n, (wt, c, which) in enumerate(MODW):
                    pe.matmul(chain[0][:, n * B:(n + 1) * B], wt[:, c * D:(c + 1) * D], cond[:, which, :], start=True, stop=True)
                for i in range(7):
                    pe.matmul(chain[0][:, (NMOD + i) * B:(NMOD + i + 1) * B], w_anchor[:, i, :], cond[:, 0, :], start=True, stop=True)
                for b in range(B):
                    o = chain[0][:, (NMOD + 7) * B + b * E:(NMOD + 7) * B + (b + 1) * E]
                    pe.matmul(o, cb_all[:, b, :], w_rt[:, 2, :], start=True, stop=False)
                    mm = pe.matmul(o, ones[0:1, :], rt_row[0:1, :], start=False, stop=True)
                mm.then_inc(set_pe, 1)
                for n, (wt, r) in enumerate(((w_p2, R_P2), (w_pr3, R_PR3), (w_cp3, R_CP3))):
                    pe.matmul(chain[1][:, n * D:(n + 1) * D], bvb[:, n, :], wt, start=True, stop=False)
                    pe.matmul(chain[1][:, n * D:(n + 1) * D], ones[0:1, :], rows[0:1, r, :], start=False, stop=True)
                pe.matmul(chain[1][:, 3 * D:4 * D], ones[0:1, :], rows[0:1, R_M2[0], :], start=True, stop=True)
                pe.matmul(pvb[1][:, 0:D], ones[0:1, :], rows[0:1, R_M2[1], :], start=True, stop=True).then_inc(set_pe, 1)
                for n in range(2 * E):
                    mm = pe.transpose(mxb[n // 4][:, (n % 4) * P:(n % 4 + 1) * P], w_e2[:, n, :], ident[:, :])
                mm.then_inc(set_pe, 1)
                pe.wait_ge(set_dve, 2)
                for kb in range(TB):
                    if kb > 1:
                        pe.wait_ge(set_dve, 1 + kb)
                    for t in range(TB):
                        mm = pe.transpose(chain[kb % 2][:, :].bitcast(BF16)[:, t * P:(t + 1) * P],
                                          mask_q[:, t, kb * P:(kb + 1) * P], identb[:, :])
                    mm.then_inc(set_pe, 1)
                for n in range(2 * E):
                    pe.matmul(exb[n // 4][:, (n % 4) * D:(n % 4 + 1) * D], w_e2t[:, n, :], w_out[:, :], start=True, stop=True)
                for e in range(E):
                    pe.matmul(pvb[0][0:1, e * D:(e + 1) * D], e_b2[:, e:e + 1], w_out[:, :], start=True, stop=False)
                    mm = pe.matmul(pvb[0][0:1, e * D:(e + 1) * D], ones[0:1, 0:1], rows[0:1, R_OUT, :], start=False, stop=True)
                mm.then_inc(set_pe, 1)

        nc.gpsimd.sem_clear(dve_link)
        nc.all_engine_barrier(sem_only=True)

        with nc.Fori(0, B // NS) as turn:
            with nc.Block(no_gpsimd_drain=True) as block:
                def count(engine, step):
                    return ORDER[engine][step]

                def chain_bank(pe, step):
                    n = CHAIN_AT[step]
                    if n >= 2:
                        engine, taken = freed_by(CHAIN_STEPS[n - 2])
                        pe.wait_ge(done[engine], count(engine, taken))
                    return chain[n % 2]

                def bank(step):
                    return chain[CHAIN_AT[step] % 2]

                def blocks(ap, n=TB):
                    return ap.rearrange("p (t d) -> p t d", t=n)

                QKIN = {0: (w_qkv0, 0), 1: (w_cq, 0), 2: (w_q2, 0), 3: (w_qkv3, 0), 4: (w_qc3, 0), 5: (w_q1, 0)}
                QBIAS = {1: None, 2: C_Q2, 3: C_QKV3, 4: C_QC, 5: None}
                LN_OF = {0: 0, 1: 1, 2: 4, 3: 5, 4: 6, 5: 3}
                LN_OF_MLP = (2, 7)

                @block.sync
                def _(sp):
                    def load(k, s):
                        seq = turn * NS + s
                        sp.dma_start(x[s][:, :, :], io["x"][bass.ds(seq, 1)].rearrange("a (t p) d -> p (a t) d", p=P)).then_inc(x_in[s], 16)
                        sp.dma_start(cx[s][:, :], io["ctx_1024"][bass.ds(seq, 1)].rearrange("a k d -> k (a d)")).then_inc(ctx_in[s], 16)
                        sp.dma_start(cmask[s][:, :], io["mask_BxS2_bf1"][bass.ds(seq, 1)].to_broadcast([P, NK])).then_inc(ctx_in[s], 16)

                    def ctx_out(k, s):
                        sp.wait_ge(dve_done, count("dve", (s, "ctx_split")))
                        for c in range(3):
                            sp.dma_start(c_parts[s][c, :, 0:4, :].rearrange("p (a b) n -> p a b n", a=2)[:, 0], kcp[s][:, c, 0:2, :]).then_inc(cwrit[s], 16)
                            sp.dma_start(c_parts[s][c, :, 0:4, :].rearrange("p (a b) n -> p a b n", a=2)[:, 1], kcp[s][:, c, 0:2, :]).then_inc(cwrit[s], 16)
                            sp.dma_start(c_parts[s][c, :, 4:6, :], kcp[s][:, c, 0:3:2, :]).then_inc(cwrit[s], 16)

                    def ctx_stack(k, s):
                        sp.wait_ge(cwrit[s], 16 * 9)
                        for c in range(3):
                            v = c_parts[s][c].rearrange("(g e d) c n -> e (d c) g n", e=2, d=HD)
                            for e in range(2):
                                sp.dma_start(ksc[s][48 * e:48 * e + 48, c, :, e, :], v[e]).then_inc(cread[s], 16)

                    def parts_out(k, s, a, w):
                        sp.wait_ge(dve_done, count("dve", (s, "parts", a, w)))
                        if w == 0:
                            sp.dma_start(q_parts[s].rearrange("c p n -> p c n"), qp[0][s][:, :, :]).then_inc(qwrit[s], 16)
                        else:
                            kv = k_parts[s].rearrange("p c n -> p c n")
                            sp.dma_start(kv[:, 0:2, :], qp[1][s][:, 0:2, :]).then_inc(kwrit[s], 16)
                            sp.dma_start(kv[:, 2:4, :], qp[1][s][:, 0:2, :]).then_inc(kwrit[s], 16)
                            sp.dma_start(kv[:, 4:6, :], qp[1][s][:, 0:3:2, :]).then_inc(kwrit[s], 16)

                    def stack(k, s, a, w, half=0):
                        if w == 0:
                            sp.wait_ge(qwrit[s], 16 * (a + 1))
                            for c in range(COMBOS):
                                sp.dma_start(qs[s][c:STACK:COMBOS, :, :],
                                             q_parts[s][QSLOT[c]].rearrange("(g ed) n -> ed g n", g=G)).then_inc(qread[s], 16)
                        else:
                            sp.wait_ge(kwrit[s], 48 * (SELF.index(a) + 1))
                            n = CORES.index((s, a))
                            if n:
                                o, oa = CORES[n - 1]
                                sp.wait_ge(pe_done, count("pe", (o, "exp", oa, 2 * half + 1, 15)))
                            v = k_parts[s].rearrange("(g e d) c n -> e (d c) g n", e=2, d=HD)
                            for e in range(2):
                                sp.dma_start(ks[s][48 * e:48 * e + 48, e, 4 * half:4 * half + 4, :],
                                             v[e][:, 4 * half:4 * half + 4]).then_inc(kread[s][half], 16)

                    def max_rows(k, s, a, hg):
                        sp.wait_ge(dve_done, count("dve", (s, "max_t", a, hg)))
                        for g in range(2):
                            sp.dma_start(qs[s][MROW:ROWS, 2 * hg + g, :], mrow[s][6 * g:6 * g + 6, hg % 2, :]).then_inc(mrows[s], 16)

                    def store(k, s):
                        sp.wait_ge(dve_done, count("dve", (s, "mlp_out", 1)))
                        seq = turn * NS + s
                        sp.dma_start(out[bass.ds(seq, 1)].rearrange("a (t p) d -> p (a t) d", p=P), x[s][:, :, :]).then_inc(stored[s], 16)

                    parts = locals()
                    for step in PLAN:
                        if "sp" in STEPS[step[1]]:
                            parts[step[1]](step, step[0], *step[2:])
                    for s in range(NS):
                        sp.wait_ge(stored[s], 16)

                @block.gpsimd
                def _(pool):
                    n = [0]

                    def xn_free(k):
                        reader = before_in_plan(k, "ln_t", "ctx_t", "attn_t", "l1_probs_t")
                        if reader:
                            pool.wait_ge(pe_done, count("pe", reader))

                    def ctx_norm(k, s):
                        pool.wait_ge(dve_done, count("dve", (s, "ctx_stats")))
                        xn_free(k)
                        link(pool, pool_link, n, pool.tensor_tensor(crstd[s][:, :], cvar[s][:, :], eps_pow[0:NK, 0:1].to_broadcast([NK, 2]), ALU.pow))
                        for j in range(2):
                            ins = pool.tensor_scalar(cxn[s][:, j, :], cx[s][:, :], cmv[s][:, 0:1], crstd[s][:, j:j + 1], ALU.subtract, ALU.mult)
                        ins.then_inc(pool_done, 1)

                    def ln_norm(k, s, m):
                        pool.wait_ge(dve_done, count("dve", (s, "ln_stats", m)))
                        link(pool, pool_link, n, pool.tensor_tensor(rstd[s][:, :], var[s][:, :], eps_pow[:, 0:1].to_broadcast([P, TB]), ALU.pow))
                        xn_free(k)
                        for t in range(TB):
                            ins = pool.tensor_scalar(xn[s][:, t, :], x[s][:, t, :], mv[s][:, t, 0:1], rstd[s][:, t:t + 1], ALU.subtract, ALU.mult)
                        ins.then_inc(pool_done, 1)

                    def bias(k, s, m):
                        b = {2: bias_b[:, 0:1, :], 3: g_bias[s][:, 1:2, :], 4: bias_b[:, 2:3, :],
                             5: g_bias[s][:, 0:1, :], 6: g_bias[s][:, 2:3, :]}[m]
                        if m in (3, 5, 6):
                            pool.wait_ge(dve_done, count("dve", (s, "gates", 0 if m == 5 else 1)))
                        pool.wait_ge(pool_done, count("pool", (s, "ln_norm", {2: 4, 3: 5, 4: 6, 5: 2, 6: 7}[m])))
                        pool.tensor_tensor(x[s][:, :, :], x[s][:, :, :], b.to_broadcast([P, TB, D]), ALU.add).then_inc(pool_done, 1)

                    parts = locals()
                    for step in PLAN:
                        if "pool" in STEPS[step[1]]:
                            parts[step[1]](step, step[0], *step[2:])

                @block.scalar
                def _(act):
                    def ctx_t(k, s):
                        act.wait_ge(pe_done, count("pe", k))
                        c = blocks(bank(k)[:, 0:3 * NK], 3)
                        act.activation(cxt[s][:, 0, :], c[:, 0, :], ACT.Identity)
                        act.activation(cxt[s][:, 1, :], c[:, 1, :], ACT.Identity, scale=aff[s][:, 8, 0:1], bias=aff[s][:, 8, 1:2])
                        act.activation(cxt[s][:, 2, :], c[:, 2, :], ACT.Identity).then_inc(act_done, 1)

                    def heads_values(dst, src):
                        for par in range(2):
                            ins = act.activation(dst[par], src[:, :, par, :, :], ACT.Identity)
                        return ins

                    def ctx_v(k, s):
                        act.wait_ge(pe_done, count("pe", k))
                        c = bank(k)
                        for l in range(4):
                            cv = c[0:NK, l * D:(l + 1) * D]
                            if l == 1:
                                act.activation(vc1[s][:, :], cv, ACT.Identity)
                                continue
                            m = {0: 0, 2: 1, 3: 2}[l]
                            ins = heads_values([vac[s][:, m, par, :, :, 16 * par:16 * par + 8] for par in range(2)],
                                               cv.rearrange("p (h q j d) -> p h q j d", h=2, q=2, j=4))
                        ins.then_inc(act_done, 1)

                    def v(k, s, a):
                        act.wait_ge(pe_done, count("pe", k))
                        ins = heads_values([va[s][:, par, :, :, :, 16 * par:16 * par + 8].rearrange("p t h j d -> p (t h) j d") for par in range(2)],
                                           bank(k)[:, :].rearrange("p (th q j d) -> p th q j d", q=2, j=4, d=HD))
                        ins.then_inc(act_done, 1)

                    def ln_t(k, s, m):
                        act.wait_ge(pe_done, count("pe", k))
                        act.activation(xt[s][:, :], bank(k)[:, :], ACT.Identity, scale=aff[s][:, m, 0:1],
                                       bias=aff[s][:, m, 1:2]).then_inc(act_done, 1)

                    def proj(k, s, a, w):
                        act.wait_ge(pe_done, count("pe", k))
                        c = QBIAS[a]
                        kw = {} if c is None else {"bias": cols[:, c + w:c + w + 1]}
                        act.activation(qf[w][s][:, :], bank(k)[:, :], ACT.Identity, **kw).then_inc(act_done, 1)

                    def part1(k, s, a, w):
                        if a == 0:
                            act.wait_ge(dve_done, count("dve", (s, "rope", w, 1)))
                        else:
                            act.wait_ge(act_done, count("act", (s, "proj", a, w)))
                        act.activation(qp[w][s][:, 0, :], qf[w][s][:, :], ACT.Identity).then_inc(act_done, 1)

                    def exp(k, s, a, hg, t):
                        n = EXP_AT[k]
                        act.wait_ge(pe_done, count("pe", k))
                        if n >= 4 * NSLOT:
                            act.wait_ge(pe_done, count("pe", PV_STEPS[n // 4 - NSLOT]))
                        K = P if a in SELF else NK
                        act.activation(pr[0:K, n % (4 * NSLOT), :], exb[n % 2][0:K, :], ACT.Exp, scale=SCALE).then_inc(act_done, 1)

                    def pv_out(k, s, a, ab):
                        act.wait_ge(pe_done, count("pe", (s, "pv", a, 2 * ab + 1, tiles(a) // 4 - 1)))
                        act.activation(u[s][:, ab, :], pvb[s][:, :], ACT.Identity).then_inc(act_done, 1)

                    def attn_t(k, s, a):
                        act.wait_ge(pe_done, count("pe", k))
                        act.activation(aot[s][:, :], bank(k)[:, :], ACT.Identity).then_inc(act_done, 1)

                    def l1_exp(k, s):
                        act.wait_ge(dve_done, count("dve", (s, "l1_scores")))
                        c = bank((s, "l1_scores"))
                        for t in range(TB):
                            ins = act.activation(es[s][:, t, :], c[:, t * NK:(t + 1) * NK], ACT.Exp, scale=SCALE1,
                                                 bias=nm1[s][:, t:t + 1], accum_out=s1[s][:, t:t + 1])
                        ins.then_inc(act_done, 1)

                    def l1_probs_t(k, s):
                        act.wait_ge(pe_done, count("pe", k))
                        act.activation(pt[s][:, :], bank(k)[0:NK, :], ACT.Identity).then_inc(act_done, 1)

                    def l1_evidence(k, s):
                        act.wait_ge(pe_done, count("pe", k))
                        act.activation(evt[s][:, :], bank(k)[:, :], ACT.Identity).then_inc(act_done, 1)

                    def router_exp(k, s):
                        act.wait_ge(dve_done, count("dve", (s, "router")))
                        act.activation(lex[s][:, :, :], lsub[s][:, :, :], ACT.Exp).then_inc(act_done, 1)

                    def expert_h(k, s, i):
                        act.wait_ge(pe_done, count("pe", k))
                        act.activation(hid[s][:, i, :], bank(k)[:, :], ACT.Silu, bias=anc[s][:, i:i + 1]).then_inc(act_done, 1)

                    def gate_h(k, s):
                        act.wait_ge(pe_done, count("pe", k))
                        act.activation(gh[s][:, :], bank(k)[:, :], ACT.Silu, bias=anc[s][:, 6:7]).then_inc(act_done, 1)

                    def gate(k, s):
                        act.wait_ge(pe_done, count("pe", k))
                        act.activation(gt[s][:, :, :], blocks(bank(k)[:, :]), ACT.Tanh, scale=0.5).then_inc(act_done, 1)

                    def mlp_h(k, s, m, c):
                        act.wait_ge(pe_done, count("pe", k))
                        act.activation(hid[s][:, c, :], bank(k)[:, :], ACT.Gelu_apprx_tanh,
                                       bias=cols[:, C_M1[m] + c:C_M1[m] + c + 1]).then_inc(act_done, 1)

                    parts = locals()
                    for step in PLAN:
                        if "act" in STEPS[step[1]]:
                            parts[step[1]](step, step[0], *step[2:])

                @block.vector
                def _(dve):
                    n = [0]

                    def do(ins):
                        link(dve, dve_link, n, ins)

                    def select(k, s):
                        seq = turn * NS + s

                        def own(dst, src):
                            return dve.tensor_copy(dst, src.rearrange("p n a -> p (n a)"))

                        dve.tensor_copy(aff[s][:, :, :], affine[:, :, :, bass.ds(seq, 1)].rearrange("p n k a -> p n (k a)"))
                        own(anc[s][:, :], anchors[:, :, bass.ds(seq, 1)])
                        dve.tensor_copy(rt_b[s][:, :], rt_all[:, bass.ds(seq, 1), :].rearrange("p a e -> p (a e)"))
                        own(gcol[s][:, 0:3], mod[:, GATES[0]:GATES[2] + 1:3, bass.ds(seq, 1)])
                        own(gcol[s][:, 3:5], mod[:, GATES[3]:GATES[4] + 1:3, bass.ds(seq, 1)]).then_inc(dve_done, 1)

                    def gate_cols(k, s):
                        dve.wait_ge(dve_done, count("dve", (s, "select")))
                        dve.tensor_copy(cb[s][:, :, :], gcol[s][:, :].rearrange("p (g a) -> p g a", a=1).to_broadcast([P, 5, P])).then_inc(dve_done, 1)

                    def gates(k, s, l):
                        dve.wait_ge(pe_done, count("pe", k))
                        c = bank(k)
                        if l == 0:
                            dve.tensor_tensor(g_o0[s][:, :], w_o0[:, :], c[:, 0:D], ALU.mult)
                            dve.tensor_tensor(g_co[s][:, :], w_co[:, :], c[:, D:2 * D], ALU.mult)
                            dve.tensor_tensor(g_bias[s][:, 0, :], bias_b[:, 3, :], c[:, 2 * D:3 * D], ALU.mult)
                            dve.tensor_copy(g_mlp[s][:, 0, :], c[:, 2 * D:3 * D]).then_inc(dve_done, 1)
                        else:
                            dve.tensor_tensor(g_pr[s][:, :], w_pr3[:, :], c[:, 0:D], ALU.mult)
                            dve.tensor_tensor(g_bias[s][:, 1, :], bias_b[:, 1, :], c[:, 0:D], ALU.mult)
                            dve.tensor_tensor(g_bias[s][:, 2, :], bias_b[:, 4, :], c[:, D:2 * D], ALU.mult)
                            dve.tensor_copy(g_mlp[s][:, 1, :], c[:, D:2 * D]).then_inc(dve_done, 1)

                    def ctx_stats(k, s):
                        dve.wait_ge(ctx_in[s], 32)
                        do(dve.bn_stats(cstats[s][:, :], cx[s][:, :]))
                        do(dve.bn_aggr(cmv[s][:, :], cstats[s][:, :]))
                        dve.tensor_scalar(cvar[s][:, 0:1], cmv[s][:, 1:2], EPS[4], None, ALU.add)
                        do(dve.tensor_scalar(cvar[s][:, 1:2], cmv[s][:, 1:2], EPS[6], None, ALU.add))
                        do(dve.tensor_reduce(cany[s][:, :], cmask[s][:, :], AX.X, ALU.max))
                        do(dve.tensor_scalar(cmaskf[s][:, :], cmask[s][:, :], 1.0, BIG, ALU.subtract, ALU.mult))
                        do(dve.tensor_scalar(cbias[s][:, :], cmaskf[s][:, :], cany[s][:, 0:1], None, ALU.mult))
                        dve.tensor_copy(ksc[s][96:97, 0, :, :, :].rearrange("p g e n -> p (g e) n"),
                                        cbias[s][96:97, :].rearrange("p (a n) -> p a n", a=1).to_broadcast([1, 2 * G, NK])).then_inc(dve_done, 1)

                    def ctx_k(k, s):
                        dve.wait_ge(pe_done, count("pe", k))
                        c = blocks(bank(k)[:, 0:4 * NK], 4)
                        dve.tensor_scalar(kc[s][:, 0, :], c[:, 0, :], cany[s][:, 0:1], None, ALU.mult)
                        dve.tensor_copy(kc[s][:, 3, :], c[:, 1, :])
                        dve.tensor_scalar(kc[s][:, 1, :], c[:, 2, :], cols[:, C_K2:C_K2 + 1], None, ALU.add)
                        dve.tensor_scalar(kc[s][:, 2, :], c[:, 3, :], cols[:, C_KVC:C_KVC + 1], None, ALU.add).then_inc(dve_done, 1)

                    def ctx_split(k, s):
                        dve.wait_ge(dve_done, count("dve", (s, "ctx_k")))
                        if s:
                            dve.wait_ge(cwrit[s - 1], 16 * 9)
                        do(dve.tensor_copy(kcp[s][:, :, 0, :], kc[s][:, 0:3, :]))
                        do(dve.tensor_tensor(kcr[s][:, :, :], kc[s][:, 0:3, :], kcp[s][:, :, 0, :], ALU.subtract))
                        do(dve.tensor_copy(kcp[s][:, :, 1, :], kcr[s][:, :, :]))
                        dve.tensor_tensor(kcp[s][:, :, 2, :], kcr[s][:, :, :], kcp[s][:, :, 1, :], ALU.subtract).then_inc(dve_done, 1)

                    def ln_stats(k, s, m):
                        if m == 0:
                            dve.wait_ge(x_in[s], 16)
                        else:
                            prev = {1: ("attn_out", 0), 2: ("attn_out", 1), 3: ("mlp_out", 0), 4: ("l1_add",), 5: ("attn_out", 2),
                                    6: ("attn_out", 3), 7: ("attn_out", 4)}[m]
                            dve.wait_ge(dve_done, count("dve", (s, *prev)))
                        for t in range(TB):
                            ins = dve.bn_stats(stats[s][:, t, :], x[s][:, t, :])
                        do(ins)
                        for t in range(TB):
                            ins = dve.bn_aggr(mv[s][:, t, :], stats[s][:, t, :])
                        do(ins)
                        dve.tensor_scalar(var[s][:, :], mv[s][:, :, 1], EPS[m], None, ALU.add).then_inc(dve_done, 1)

                    def rope(k, s, w, r):
                        dve.wait_ge(pe_done, count("pe", k))
                        b = bank(k)[:, :].rearrange("p (h n) -> p h n", n=ROPE)
                        tab = (cos, sin)[r][:, :].rearrange("p (a n) -> p a n", a=1).to_broadcast([P, T // ROPE, ROPE])

                        def halves(ap):
                            return ap.rearrange("p (h n) -> p h n", n=ROPE)

                        if r == 0:
                            dve.tensor_tensor(halves(r1[w][s]), b, tab, ALU.mult).then_inc(dve_done, 1)
                        else:
                            do(dve.tensor_tensor(halves(r2[w][s]), b, tab, ALU.mult))
                            dve.tensor_tensor(qf[w][s][:, :], r1[w][s][:, :], r2[w][s][:, :], ALU.add).then_inc(dve_done, 1)

                    def parts(k, s, a, w):
                        dve.wait_ge(act_done, count("act", (s, "part1", a, w)))
                        q, part = qf[w][s], qp[w][s]
                        do(dve.tensor_tensor(r1[w][s][:, :], q[:, :], part[:, 0, :], ALU.subtract))
                        do(dve.tensor_copy(part[:, 1, :], r1[w][s][:, :]))
                        dve.tensor_tensor(part[:, 2, :], r1[w][s][:, :], part[:, 1, :], ALU.subtract).then_inc(dve_done, 1)

                    def max(k, s, a, hg, t):
                        dve.wait_ge(pe_done, count("pe", k))
                        b = mxb[MAX_AT[k] % 2]
                        dst = mx[s][:, hg % 2]
                        if a in SELF:
                            g, e, qb = t // 8, t // 4 % 2, t % 4
                            dve.tensor_reduce(dst[:, qb, g, e:e + 1], b[:, :], AX.X, ALU.max).then_inc(dve_done, 1)
                        else:
                            dve.tensor_reduce(dst[:, t, :, :].rearrange("p g e -> p (g e)"),
                                              b[:, 0:4 * NK].rearrange("p (h n) -> p h n", h=4), AX.X, ALU.max).then_inc(dve_done, 1)

                    def max_parts(k, s, a, hg):
                        dve.wait_ge(dve_done, count("dve", (s, "max", a, hg, tiles(a) - 1)))
                        m = mx[s][:, hg % 2].rearrange("p t g e -> p (t g) e")
                        part = mp[s][:, hg % 2].rearrange("p t g c e -> p (t g) c e")
                        do(dve.tensor_scalar(part[:, :, 0, :], m, -1.0, None, ALU.mult))
                        do(dve.scalar_tensor_tensor(mr[s][:, :, :], m, -1.0, part[:, :, 0, :], ALU.mult, ALU.subtract))
                        do(dve.tensor_copy(part[:, :, 1, :], mr[s][:, :, :]))
                        dve.tensor_tensor(part[:, :, 2, :], mr[s][:, :, :], part[:, :, 1, :], ALU.subtract).then_inc(dve_done, 1)

                    def max_t(k, s, a, hg):
                        dve.wait_ge(pe_done, count("pe", k))
                        if (a, hg) >= (0, 2):
                            dve.wait_ge(mrows[s], 32 * (4 * a + hg - 1))
                        dve.tensor_copy(mrow[s][:, hg % 2, :], bank(k)[:, :].bitcast(BF16)[0:12, 0:T]).then_inc(dve_done, 1)

                    def heads_t(k, s, a, ab):
                        dve.wait_ge(pe_done, count("pe", k))
                        c = bank(k)[:, :].rearrange("p (t j q v d) -> p t j q v d", t=TB, j=4, q=2, v=2)
                        rc = rec[s][:, ab]
                        do(dve.reciprocal(rc.rearrange("p t j q -> p (t j) q"),
                                          bank(k)[:, :].rearrange("p (tj q w) -> p tj q w", q=2, w=16)[:, :, :, 8]))
                        for par in range(2):
                            o = ao[s][:, :, 64 * ab + 32 * par:64 * ab + 32 * par + 32].rearrange("p t (j d) -> p t j d", j=4)
                            ins = dve.tensor_tensor(o, c[:, :, :, par, 0, :], rc[:, :, :, par:par + 1].to_broadcast([P, TB, 4, HD]), ALU.mult)
                        ins.then_inc(dve_done, 1)

                    def add_residual(k, s):
                        dve.tensor_tensor(x[s][:, :, :], x[s][:, :, :], blocks(bank(k)[:, :]), ALU.add).then_inc(dve_done, 1)

                    def attn_out(k, s, a):
                        dve.wait_ge(pe_done, count("pe", k))
                        dve.wait_ge(pool_done, count("pool", (s, "bias", a) if a >= 2 else (s, "ln_norm", a)))
                        add_residual(k, s)

                    def mlp_out(k, s, m):
                        dve.wait_ge(pe_done, count("pe", k))
                        dve.wait_ge(pool_done, count("pool", (s, "bias", 5 + m)))
                        do(dve.tensor_tensor(xn[s][:, :, :], blocks(bank(k)[:, :]), g_mlp[s][:, m:m + 1, :].to_broadcast([P, TB, D]), ALU.mult))
                        dve.tensor_tensor(x[s][:, :, :], x[s][:, :, :], xn[s][:, :, :], ALU.add).then_inc(dve_done, 1)

                    def l1_scores(k, s):
                        dve.wait_ge(pe_done, count("pe", k))
                        do(dve.tensor_reduce(m1[s][:, :], bank(k)[:, 0:TB * NK].rearrange("p (t n) -> p t n", t=TB), AX.X, ALU.max))
                        dve.tensor_scalar(nm1[s][:, :], m1[s][:, :], -SCALE1, None, ALU.mult).then_inc(dve_done, 1)

                    def l1_probs(k, s):
                        dve.wait_ge(act_done, count("act", (s, "l1_exp")))
                        do(dve.reciprocal(rs1[s][:, :], s1[s][:, :]))
                        dve.tensor_tensor(es[s][:, :, :], es[s][:, :, :],
                                          rs1[s][:, :].rearrange("p (t a) -> p t a", a=1).to_broadcast([P, TB, NK]), ALU.mult).then_inc(dve_done, 1)

                    def over_e(ap):
                        return ap.rearrange("p (t a) -> p t a", a=1).to_broadcast([P, TB, E])

                    def router(k, s):
                        dve.wait_ge(pe_done, count("pe", k))
                        do(dve.tensor_tensor(lg[s][:, :, :], bank(k)[:, 0:TB * E].rearrange("p (t e) -> p t e", t=TB),
                                             rt_b[s][:, :].rearrange("p (a e) -> p a e", a=1).to_broadcast([P, TB, E]), ALU.add))
                        do(dve.tensor_reduce(lm[s][:, :], lg[s][:, :, :], AX.X, ALU.max))
                        dve.tensor_tensor(lsub[s][:, :, :], lg[s][:, :, :], over_e(lm[s][:, :]), ALU.subtract).then_inc(dve_done, 1)

                    def router_probs(k, s):
                        dve.wait_ge(act_done, count("act", (s, "router_exp")))
                        do(dve.tensor_reduce(lsum[s][:, :], lex[s][:, :, :], AX.X, ALU.add))
                        do(dve.reciprocal(lrec[s][:, :], lsum[s][:, :]))
                        dve.tensor_tensor(prob[s][:, :, :], lex[s][:, :, :], over_e(lrec[s][:, :]), ALU.mult).then_inc(dve_done, 1)

                    def expert_out(k, s, t):
                        dve.wait_ge(pe_done, count("pe", k))
                        dve.wait_ge(dve_done, count("dve", (s, "router_probs")))
                        c = bank(k)
                        do(dve.tensor_scalar(ro[s][:, t, :], c[:, 0:D], prob[s][:, t, 0:1], None, ALU.mult))
                        do(dve.scalar_tensor_tensor(ro[s][:, t, :], c[:, D:2 * D], prob[s][:, t, 1:2], ro[s][:, t, :], ALU.mult, ALU.add))
                        dve.scalar_tensor_tensor(ro[s][:, t, :], c[:, 2 * D:3 * D], prob[s][:, t, 2:3], ro[s][:, t, :], ALU.mult, ALU.add).then_inc(dve_done, 1)

                    def l1_add(k, s):
                        dve.wait_ge(act_done, count("act", (s, "gate")))
                        dve.wait_ge(dve_done, count("dve", (s, "expert_out", TB - 1)))
                        dve.wait_ge(pool_done, count("pool", (s, "ln_norm", 3)))
                        do(dve.scalar_tensor_tensor(ro2[s][:, :, :], gt[s][:, :, :], 1.0, ro[s][:, :, :], ALU.add, ALU.mult))
                        dve.scalar_tensor_tensor(x[s][:, :, :], ro2[s][:, :, :], 0.5, x[s][:, :, :], ALU.mult, ALU.add).then_inc(dve_done, 1)

                    parts_ = locals()
                    for step in PLAN:
                        if "dve" in STEPS[step[1]]:
                            parts_[step[1]](step, step[0], *step[2:])

                @block.tensor
                def _(pe):
                    def gates(k, s, l):
                        b = chain_bank(pe, k)
                        pe.wait_ge(dve_done, count("dve", (s, "gate_cols")))
                        for i, g in enumerate(((0, 1, 2), (3, 4))[l]):
                            ins = pe.matmul(b[:, i * D:(i + 1) * D], cb[s][:, g, :], ident[:, :], start=True, stop=True)
                        ins.then_inc(pe_done, 1)

                    def ctx_t(k, s):
                        b = chain_bank(pe, k)
                        pe.wait_ge(pool_done, count("pool", (s, "ctx_norm")))
                        for j in range(3):
                            src = cx[s][:, :] if j == 0 else cxn[s][:, j - 1, :]
                            ins = pe.transpose(b[:, j * NK:(j + 1) * NK], src, ident[0:NK, 0:NK])
                        ins.then_inc(pe_done, 1)

                    def ctx_k(k, s):
                        b = chain_bank(pe, k)
                        pe.wait_ge(act_done, count("act", (s, "ctx_t")))
                        for l, (w, j) in enumerate(((w_ck, 0), (w_k1, 0), (w_kv2, 1), (w_kvc3, 2))):
                            ins = pe.matmul(b[:, l * NK:(l + 1) * NK], w[:, 0:D], cxt[s][:, j, :], start=True, stop=True)
                        ins.then_inc(pe_done, 1)

                    def ctx_v(k, s):
                        b = chain_bank(pe, k)
                        pe.wait_ge(act_done, count("act", (s, "ctx_t")))
                        for l, (w, j, o) in enumerate(((w_cv, 0, 0), (w_v1, 0, 0), (w_kv2, 1, D), (w_kvc3, 2, D))):
                            ins = pe.matmul(b[0:NK, l * D:(l + 1) * D], cxt[s][:, j, :], w[:, o:o + D], start=True, stop=True)
                        ins.then_inc(pe_done, 1)

                    def ln_t(k, s, m):
                        b = chain_bank(pe, k)
                        pe.wait_ge(pool_done, count("pool", (s, "ln_norm", m)))
                        for t in range(TB):
                            ins = pe.transpose(b[:, t * P:(t + 1) * P], xn[s][:, t, :], ident[:, :])
                        ins.then_inc(pe_done, 1)

                    def rope(k, s, w, r):
                        b = chain_bank(pe, k)
                        pe.wait_ge(act_done, count("act", (s, "ln_t", 0)))
                        m = (w_qkv0, w_rot)[r]
                        pe.matmul(b[:, :], m[:, w * D:(w + 1) * D], xt[s][:, :], start=True, stop=True).then_inc(pe_done, 1)

                    def proj(k, s, a, w):
                        b = chain_bank(pe, k)
                        pe.wait_ge(act_done, count("act", (s, "ln_t", LN_OF[a])))
                        m, o = QKIN[a]
                        if a == 1:
                            pe.wait_ge(loaded_late, 16)
                        pe.matmul(b[:, :], m[:, o + w * D:o + (w + 1) * D], xt[s][:, :], start=True, stop=True).then_inc(pe_done, 1)

                    def v(k, s, a):
                        b = chain_bank(pe, k)
                        w = w_qkv0 if a == 0 else w_qkv3
                        for t in range(TB):
                            ins = pe.matmul(b[:, t * D:(t + 1) * D], xt[s][:, t * P:(t + 1) * P], w[:, 2 * D:3 * D], start=True, stop=True)
                        ins.then_inc(pe_done, 1)

                    def max(k, s, a, hg, t):
                        if (hg, t) == (0, 0):
                            pe.wait_ge(qread[s], 16 * COMBOS * (a + 1))
                            if a in SELF:
                                pe.wait_ge(kread[s][0], 32 * (SELF.index(a) + 1))
                            elif a == 1:
                                pe.wait_ge(cread[s], 96)
                        if (hg, t) == (2, 0) and a in SELF:
                            pe.wait_ge(kread[s][1], 32 * (SELF.index(a) + 1))
                        n = MAX_AT[k]
                        if n >= 2:
                            pe.wait_ge(dve_done, count("dve", MAX_STEPS[n - 2]))
                        b = mxb[n % 2]
                        R = MASKROW + 1
                        if a in SELF:
                            g, e, qb = 2 * hg + t // 8, t // 4 % 2, t % 4
                            ins = pe.matmul(b[:, :], qs[s][0:R, g, qb * P:(qb + 1) * P], ks[s][0:R, e, g, :], start=True, stop=(a != 0))
                            if a == 0:
                                ins = pe.matmul(b[:, :], identb[:, :], mask_q[:, qb, :], start=False, stop=True)
                        else:
                            for g in range(2):
                                ins = pe.matmul(b[:, g * 2 * NK:(g + 1) * 2 * NK], qs[s][0:R, 2 * hg + g, t * P:(t + 1) * P],
                                                ksc[s][0:R, CL[a], 2 * hg + g, :, :].rearrange("p e n -> p (e n)"), start=True, stop=True)
                        ins.then_inc(pe_done, 1)

                    def max_t(k, s, a, hg):
                        pe.wait_ge(dve_done, count("dve", (s, "max_parts", a, hg)))
                        b = chain_bank(pe, k)[:, :].bitcast(BF16)
                        for t in range(TB):
                            ins = pe.transpose(b[0:12, t * P:(t + 1) * P], mp[s][:, hg % 2, t].rearrange("p g c e -> p (g c e)"), identb[:, :])
                        ins.then_inc(pe_done, 1)

                    def exp(k, s, a, hg, t):
                        n = EXP_AT[k]
                        if t == 0:
                            pe.wait_ge(mrows[s], 32 * (4 * a + hg + 1))
                        if n >= 2:
                            pe.wait_ge(act_done, count("act", EXP_STEPS[n - 2]))
                        b = exb[n % 2]
                        j, kb = t % 4, t // 4
                        g, e = 2 * hg + j // 2, j % 2
                        if a in SELF:
                            ins = pe.matmul(b[:, :], ks[s][0:ROWS, e, g, kb * P:(kb + 1) * P], qs[s][0:ROWS, g, :], start=True, stop=(a != 0))
                            if a == 0:
                                ins = pe.matmul(b[:, :], identb[:, :], mask_k[:, kb, :], start=False, stop=True)
                        else:
                            ins = pe.matmul(b[0:NK, :], ksc[s][0:ROWS, CL[a], g, e, :], qs[s][0:ROWS, g, :], start=True, stop=True)
                        ins.then_inc(pe_done, 1)

                    def pv(k, s, a, hg, kb):
                        last = tiles(a) // 4 - 1
                        pe.wait_ge(act_done, count("act", (s, "exp", a, hg, 4 * kb + 3)))
                        if (hg, kb) == (0, 0):
                            pe.wait_ge(act_done, count("act", (s, "v", a) if a in SELF else (s, "ctx_v")))
                        if hg % 2 == 0 and kb == 0:
                            m = PV_OUT[s].index((s, "pv_out", a, hg // 2))
                            if m:
                                pe.wait_ge(act_done, count("act", PV_OUT[s][m - 1]))
                        n = EXP_AT[(s, "exp", a, hg, 4 * kb)] % (4 * NSLOT)
                        K = P if a in SELF else NK
                        for j in range(4):
                            w = va[s][:, hg % 2, kb, hg // 2, j, :] if a in SELF else vac[s][:, CL[a], hg % 2, hg // 2, j, :]
                            ins = pe.matmul(pvb[s][32 * j:32 * j + 32, :], w, pr[0:K, n + j, :],
                                            start=(hg % 2 == 0 and kb == 0), stop=(hg % 2 == 1 and kb == last), skip_group_check=True)
                        ins.then_inc(pe_done, 1)

                    def heads_t(k, s, a, ab):
                        b = chain_bank(pe, k)
                        pe.wait_ge(act_done, count("act", (s, "pv_out", a, ab)))
                        for t in range(TB):
                            ins = pe.transpose(b[:, t * P:(t + 1) * P], u[s][:, ab, t * P:(t + 1) * P], ident[:, :])
                        ins.then_inc(pe_done, 1)

                    def attn_t(k, s, a):
                        b = chain_bank(pe, k)
                        pe.wait_ge(dve_done, count("dve", (s, "heads_t", a, 1)))
                        for t in range(TB):
                            ins = pe.transpose(b[:, t * P:(t + 1) * P], ao[s][:, t, :], ident[:, :])
                        ins.then_inc(pe_done, 1)

                    def attn_out(k, s, a):
                        b = chain_bank(pe, k)
                        pe.wait_ge(act_done, count("act", (s, "attn_t", a)))
                        if a in (0, 1, 3):
                            pe.wait_ge(dve_done, count("dve", (s, "gates", a // 3)))
                        w = (g_o0[s], g_co[s], w_p2, g_pr[s], w_cp3)[a]
                        for t in range(TB):
                            ins = pe.matmul(b[:, t * D:(t + 1) * D], aot[s][:, t * P:(t + 1) * P], w[:, :], start=True, stop=True)
                        ins.then_inc(pe_done, 1)

                    def l1_scores(k, s):
                        b = chain_bank(pe, k)
                        pe.wait_ge(act_done, count("act", (s, "proj", 5, 0)))
                        pe.wait_ge(dve_done, count("dve", (s, "ctx_k")))
                        for t in range(TB):
                            ins = pe.matmul(b[:, t * NK:(t + 1) * NK], qf[0][s][:, t * P:(t + 1) * P], kc[s][:, 3, :], start=True, stop=True)
                        ins.then_inc(pe_done, 1)

                    def l1_probs_t(k, s):
                        b = chain_bank(pe, k)
                        pe.wait_ge(dve_done, count("dve", (s, "l1_probs")))
                        for t in range(TB):
                            ins = pe.transpose(b[0:NK, t * P:(t + 1) * P], es[s][:, t, :], ident[:, :])
                        ins.then_inc(pe_done, 1)

                    def l1_evidence(k, s):
                        b = chain_bank(pe, k)
                        pe.wait_ge(act_done, count("act", (s, "l1_probs_t")))
                        pe.matmul(b[:, :], vc1[s][:, :], pt[s][:, :], start=True, stop=True).then_inc(pe_done, 1)

                    def router(k, s):
                        b = chain_bank(pe, k)
                        pe.wait_ge(act_done, count("act", (s, "l1_evidence")))
                        for t in range(TB):
                            o = b[:, t * E:(t + 1) * E]
                            pe.matmul(o, xt[s][:, t * P:(t + 1) * P], w_rt[:, 0, :], start=True, stop=False)
                            ins = pe.matmul(o, evt[s][:, t * P:(t + 1) * P], w_rt[:, 1, :], start=False, stop=True)
                        ins.then_inc(pe_done, 1)

                    def hidden(k, s, w0, w1):
                        b = chain_bank(pe, k)
                        pe.matmul(b[:, :], w0, xt[s][:, :], start=True, stop=False)
                        pe.matmul(b[:, :], w1, evt[s][:, :], start=False, stop=True).then_inc(pe_done, 1)

                    def expert_h(k, s, i):
                        hidden(k, s, *[w_e1[:, c, i // 2, (i % 2) * P:(i % 2 + 1) * P] for c in range(2)])

                    def gate_h(k, s):
                        hidden(k, s, w_g1[:, 0, :], w_g1[:, 1, :])

                    def gate(k, s):
                        b = chain_bank(pe, k)
                        pe.wait_ge(act_done, count("act", (s, "gate_h")))
                        for t in range(TB):
                            o = b[:, t * D:(t + 1) * D]
                            pe.matmul(o, gh[s][:, t * P:(t + 1) * P], w_g2[:, :], start=True, stop=False)
                            ins = pe.matmul(o, ones[0:1, :], g2_row[0:1, :], start=False, stop=True)
                        ins.then_inc(pe_done, 1)

                    def expert_out(k, s, t):
                        b = chain_bank(pe, k)
                        pe.wait_ge(act_done, count("act", (s, "expert_h", 2 * E - 1)))
                        for e in range(E):
                            o = b[:, e * D:(e + 1) * D]
                            for c in range(2):
                                pe.matmul(o, hid[s][:, 2 * e + c, t * P:(t + 1) * P], w_e2o[:, 2 * e + c, :], start=(c == 0), stop=False)
                            ins = pe.matmul(o, ones[0:1, :], e2_row[0:1, e * D:(e + 1) * D], start=False, stop=True)
                        ins.then_inc(pe_done, 1)

                    def mlp_h(k, s, m, c):
                        b = chain_bank(pe, k)
                        pe.wait_ge(act_done, count("act", (s, "ln_t", LN_OF_MLP[m])))
                        pe.matmul(b[:, :], w_m1[m][:, c * P:(c + 1) * P], xt[s][:, :], start=True, stop=True).then_inc(pe_done, 1)

                    def mlp_out(k, s, m):
                        b = chain_bank(pe, k)
                        pe.wait_ge(act_done, count("act", (s, "mlp_h", m, FC - 1)))
                        for t in range(TB):
                            for c in range(FC):
                                ins = pe.matmul(b[:, t * D:(t + 1) * D], hid[s][:, c, t * P:(t + 1) * P], w_m2[m][:, c, :],
                                                start=(c == 0), stop=(c == FC - 1))
                        ins.then_inc(pe_done, 1)

                    parts = locals()
                    for step in PLAN:
                        if "pe" in STEPS[step[1]]:
                            parts[step[1]](step, step[0], *step[2:])

            nc.gpsimd.sem_clear(range(in_loop0.num, last_sem.num + 1))
            nc.all_engine_barrier(sem_only=True)


def layout(inputs):
    a = {name: np.asarray(v) for name, v in inputs.items()}
    L0, L1, L2, L3 = (lambda name, l=l: a[f"L{l}_xcond_{name}"] for l in range(4))

    def chunks(m):
        return m.reshape(-1, P, m.shape[-1]).transpose(1, 0, 2).reshape(P, -1)

    def vector(v):
        return v.reshape(-1, P).T

    e_w1, e_w2 = L1("e_w1"), L1("e_w2")
    tail = np.zeros((P, 2), np.float32)
    for part in range(3):
        for e in range(2):
            tail[MROW + 2 * part + e, e] = 1.0
    cols = np.zeros((P, 32), np.float32)
    for c, v in ((C_NW, L0("norm1_w")), (C_NW + 1, L0("normc_w")), (C_NW + 2, L0("norm2_w")), (C_GB, L1("ln_gamma")),
                 (C_GB + 1, L1("ln_beta")), (C_M1[0], L0("mlp_b1")), (C_M1[1], L3("b_mlp1")), (C_E1, L1("e_b1")),
                 (C_G1, L1("gate_b1")), (C_Q2, L2("bq")), (C_K2, L2("bkv")), (C_QKV3, L3("b_qkv")), (C_QC, L3("b_qc")),
                 (C_KVC, L3("b_kvc"))):
        cols[:, c:c + v.size // P] = vector(v)
    parts = {
        "w_ada": L0("adaLN_W"), "w_ssq": L2("Wss_q"), "w_sskv": L2("Wss_kv"), "w_mod": L3("W_mod"), "w_out": L1("out_w"),
        "w_anchor": np.concatenate([chunks(e_w1[e, 2 * D:]) for e in range(E)] + [L1("gate_w1")[2 * D:]], axis=1),
        "w_e2": chunks(e_w2.reshape(-1, D)),
        "cols": cols, "e_b2": L1("e_b2").T, "ident": np.eye(P, dtype=np.float32), "tail": tail,
        "mod_b": vector(np.concatenate([L0("adaLN_b"), L2("bss_q"), L2("bss_kv"), L3("b_mod")])),
        "w_rt": chunks(L1("router_W")), "w_qkv0": L0("qkv_W"), "w_o0": L0("attn_out_W"), "w_co": L0("co_W"),
        "w_p2": L2("Wp"), "w_pr3": L3("W_proj"), "w_cp3": L3("W_cproj"), "w_ck": L0("ck_W"), "w_k1": L1("Wk"),
        "w_cv": L0("cv_W"), "w_v1": L1("Wv"), "w_kv2": L2("Wkv"), "w_kvc3": L3("W_kvc"),
        "w_cq": L0("cq_W"), "w_m10": L0("mlp_W1"), "w_m20": chunks(L0("mlp_W2")), "w_q1": L1("Wq"),
        "w_e1": e_w1[:, :2 * D].reshape(E, 2, P, RH).transpose(2, 1, 0, 3).reshape(P, -1),
        "w_g1": chunks(L1("gate_w1")[:2 * D]), "w_g2": L1("gate_w2"), "w_q2": L2("Wq"), "w_qkv3": L3("W_qkv"),
        "w_qc3": L3("W_qc"), "w_m11": L3("W_mlp1"), "w_m21": chunks(L3("W_mlp2")),
    }
    n = T // 2
    inv_freq = 1.0 / 10000.0 ** (np.arange(0, HD, 2, dtype=np.float32) / HD)
    freqs = np.outer(np.arange(n, dtype=np.float32), inv_freq)
    emb = np.concatenate([freqs, freqs], axis=-1)

    def rotation(f):
        return np.tile(f(emb).astype(np.float32).T, (H, 1))

    arrays = {name: a[name] for name in ("x", "ctx_1024", "mask_BxS2_bf1", "mask_SxS_bk0", "L1_xcond_router_b")}
    arrays["cond_t"] = a["cond_1024"].T
    arrays["bias_rows"] = np.stack([L0("mlp_b2"), L3("b_mlp2"), L2("bp"), L3("b_proj"), L3("b_cproj"), L1("out_b"), L1("gate_b2")])
    for name, table in (("setup_w", SETUP_W), ("early_w", EARLY_W), ("late_w", LATE_W)):
        arrays[name] = np.concatenate([parts[part] for part, _ in table], axis=1)
    arrays["c_cos"], arrays["c_sin"] = rotation(np.cos), rotation(np.sin)
    return {name: np.ascontiguousarray(v) for name, v in arrays.items()}


def kernel(**inputs):
    import concourse.bacc as bacc
    from concourse.bass_utils import run_bass_kernel_spmd

    nc = bacc.Bacc("TRN2", target_bir_lowering=False, num_devices=1)
    arrays = layout(inputs)
    io = {name: nc.dram_tensor(name, v.shape, mybir.dt.from_np(v.dtype), kind="ExternalInput").ap() for name, v in arrays.items()}
    out = nc.dram_tensor("out", [B, T, D], F32, kind="ExternalOutput").ap()
    build(nc, io, out)
    r = run_bass_kernel_spmd(nc, [arrays], core_ids=[0])
    return r.results[0]["out"]
```

```python
from contextlib import ExitStack

import numpy as np

import concourse.bass as bass
from concourse import mybir

F32 = mybir.dt.float32
BF16 = mybir.dt.bfloat16
U8 = mybir.dt.uint8
ALU = mybir.AluOpType
ACT = mybir.ActivationFunctionType
AX = mybir.AxisListType

P = 128
B, T, D = 4, 512, 128
LANES = 2
H, HD = 16, 8
NK = 77
TB = T // P
G = H // 2
HG = 4
E, RH = 3, 256
FC = 4
ROPE = T // 2
COMBOS = 6
STACK = 2 * HD * COMBOS
MASKROW = STACK
MROW = STACK + 1
ROWS = MROW + 6
BIG = 1e30
SCALE = float(HD) ** -0.5
SCALE1 = float(D) ** -0.5
SELF, CROSS = (0, 3), (1, 2, 4)
CL = {1: 0, 2: 1, 4: 2}
NSLOT = 3

EPS = (1e-5, 1e-5, 1e-5, 1e-5, 1e-5, 1e-6, 1e-6, 1e-6)
NMOD = 19
NLN = 9
GATES = (2, 5, 8, 15, 18)

SETUP_W = (("w_ada", 9 * D), ("w_ssq", 2 * D), ("w_sskv", 2 * D), ("w_mod", 6 * D), ("w_out", D),
           ("w_anchor", 7 * D), ("w_e2", 2 * E * D))
EARLY_W = (("cols", 32), ("mod_b", NMOD), ("e_b2", E), ("ident", P), ("tail", 2), ("w_rt", 3 * E), ("w_qkv0", 3 * D),
           ("w_o0", D), ("w_co", D), ("w_p2", D), ("w_pr3", D), ("w_cp3", D), ("w_ck", D), ("w_k1", D),
           ("w_cv", D), ("w_v1", D), ("w_kv2", 2 * D), ("w_kvc3", 2 * D))
LATE_W = (("w_cq", D), ("w_m10", FC * P), ("w_m20", FC * D), ("w_q1", D), ("w_e1", 2 * E * RH), ("w_g1", 2 * D),
          ("w_g2", D), ("w_q2", D), ("w_qkv3", 3 * D), ("w_qc3", D), ("w_m11", FC * P), ("w_m21", FC * D))
C_NW, C_GB, C_M1, C_E1, C_G1, C_Q2, C_K2, C_V2, C_QKV3, C_QC, C_KVC = 0, 3, (5, 9), 13, 19, 20, 21, 22, 23, 26, 27
R_P2, R_PR3, R_CP3, R_OUT, NROW = 0, 1, 2, 3, 4

ENGINES = ("pe", "act", "dve", "pool", "sp")

STEPS = {
    "mask_t": ("pe", "dve"), "bias_rows": ("pe", "dve"), "anchors_": ("pe", "dve"), "e2_t": ("pe", "dve"), "e2_out": ("pe", "dve"),
    "load": ("sp",), "gate_cols": ("dve",), "ctx_stats": ("dve",), "ctx_norm": ("pool",),
    "gates": ("pe", "dve"),
    "ctx_t": ("pe", "act"), "ctx_k": ("pe", "dve"), "ctx_v": ("pe", "act"), "ctx_split": ("dve",),
    "ctx_out": ("sp",), "ctx_stack": ("sp",),
    "ln_stats": ("dve",), "ln_rstd": ("pool",), "ln_norm": ("dve",), "ln_t": ("pe", "act"),
    "rope": ("pe", "dve"), "proj": ("pe", "act"), "v": ("pe", "act"),
    "part1": ("act",), "parts": ("dve",), "part1_out": ("sp",), "parts_out": ("sp",), "stack": ("sp",),
    "max": ("pe", "dve"), "max_parts": ("dve",), "max_t": ("pe", "dve"), "max_rows": ("sp",),
    "exp": ("pe", "act"), "pv": ("pe",), "pv_out": ("act",),
    "heads_t": ("pe", "dve"), "attn_t": ("pe", "act"), "attn_out": ("pe", "dve"), "bias": ("pool",),
    "l1_scores": ("pe", "dve"), "l1_exp": ("act",), "l1_probs": ("dve",), "l1_probs_t": ("pe", "act"),
    "l1_evidence": ("pe", "act"), "router": ("pe", "dve"), "router_exp": ("act",),
    "router_probs": ("dve",), "expert_h": ("pe", "act"), "gate_h": ("pe", "act"),
    "gate": ("pe", "act"), "expert_out": ("pe", "dve"), "l1_add": ("dve",),
    "mlp_h": ("pe", "act"), "mlp_out": ("pe", "dve"),
    "store": ("sp",),
}
CHAIN = {k: (k, v[1]) for k, v in STEPS.items()
         if v[0] == "pe" and len(v) == 2 and k not in ("max", "exp")}
CHAIN["l1_scores"] = ("l1_exp", "act")


def tiles(a):
    return 16 if a in SELF else 4


RUN_AHEAD = {16: 24, 4: 8}
DELAY = {16: 3, 4: 2}


def attention(s, a):
    n = tiles(a)
    items, maxima, on_the_way = [], [(hg, t) for hg in range(HG) for t in range(n)], []

    def rows(hg):
        on_the_way.remove(hg)
        items.extend([(s, "max_t", a, hg), (s, "max_rows", a, hg)])

    def tile(item):
        items.append(item)
        if on_the_way:
            delay[on_the_way[0]] -= 1
            if not delay[on_the_way[0]]:
                rows(on_the_way[0])

    delay = {hg: DELAY[n] for hg in range(HG)}
    for hg in range(HG):
        for t in range(n):
            if t % 4 == 0:
                items.append(("take", "tiles"))
            while maxima and maxima[0][0] * n + maxima[0][1] <= hg * n + t + RUN_AHEAD[n]:
                m = maxima.pop(0)
                inside = bool(items[-1:] == [("take", "tiles")])
                if inside:
                    items.pop()
                tile((s, "max", a, *m))
                if m[1] == n - 1:
                    items.append((s, "max_parts", a, m[0]))
                    on_the_way.append(m[0])
                if inside:
                    items.append(("take", "tiles"))
            if hg in on_the_way:
                rows(hg)
            tile((s, "exp", a, hg, t))
            if t % 4 == 3:
                items += [("product", (s, "pv", a, hg, t // 4)), ("give", "tiles")]
        if a in SELF and hg % 2:
            items.append(("give", f"keys{hg // 2}"))
    return items


def of(s, *steps):
    return [(s, *step) for step in steps]


def using(resource, items):
    return [("take", resource)] + items + [("give", resource)]


def attention_end(s, a):
    return of(s, ("heads_t", a, 0), ("heads_t", a, 1), ("attn_t", a), ("attn_out", a))


def norm(s, n):
    return of(s, ("ln_stats", n), ("ln_rstd", n), ("ln_norm", n), ("ln_t", n))


def split(s, a, w):
    return (of(s, ("part1", a, w)) + (of(s, ("part1_out", a)) if w == 0 else [])
            + of(s, ("parts", a, w), ("parts_out", a, w)))


def conditioning(s):
    return (of(s, ("ctx_norm",)) + using("gates", using("hidden", of(s, ("gate_cols",), ("ctx_t",), ("ctx_k",), ("ctx_v",), ("gates", 0), ("gates", 1)))
            + of(s, ("ctx_split",), ("ctx_out",), ("ctx_stack",))))


def stack_keys(s, a, half):
    return [("take", f"keys{half}")] + of(s, ("stack", a, 1, half))


def self_in(s, a, n):
    if a == 0:
        q, k = (of(s, ("rope", w, 0), ("rope", w, 1)) for w in range(2))
        steps = (of(s, ("load",)) + norm(s, n) + of(s, ("ctx_stats",))
                 + using("hidden", q + split(s, a, 0) + k + of(s, ("stack", a, 0)) + split(s, a, 1)))
        keys = stack_keys(s, a, 0) + stack_keys(s, a, 1)
        return steps + of(s, ("v", a)) + (keys if s == 0 else conditioning(s) + keys)
    return (norm(s, n) + of(s, ("bias", a)) + using("hidden", of(s, ("proj", a, 0), ("proj", a, 1)) + split(s, a, 0) + split(s, a, 1))
            + of(s, ("stack", a, 0), ("v", a)) + stack_keys(s, a, 0) + stack_keys(s, a, 1))


def cross(s, a, n):
    core = attention(s, a)
    core.insert(core.index((s, "exp", a, HG - 1, 0)), (s, "heads_t", a, 0))
    return (norm(s, n) + (of(s, ("bias", a)) if a != 1 else []) + using("hidden", of(s, ("proj", a, 0)) + split(s, a, 0))
            + of(s, ("stack", a, 0)) + core + attention_end(s, a)[1:])


def mlp(s, m, n):
    return norm(s, n) + of(s, ("bias", 5 + m)) + using("hidden", [("bunch", of(s, *[("mlp_h", m, c) for c in range(FC)]))]
                                                       + of(s, ("mlp_out", m)))


def layer1(s):
    return (norm(s, 3) + using("hidden", of(s, ("proj", 5, 0)) + [("bunch", of(s, ("l1_scores",), ("l1_exp",)))])
            + using("gates", of(s, ("l1_probs",), ("l1_probs_t",), ("l1_evidence",))
                    + using("hidden", [("bunch", of(s, ("gate_h",), *[("expert_h", i) for i in range(2 * E)]))]
                            + of(s, ("router",), ("router_exp",), ("gate",), ("router_probs",), *[("expert_out", t) for t in range(TB)])))
            + of(s, ("l1_add",)))


def tables():
    return using("tiles", using("gates", of(1, *[("mask_t", kb) for kb in range(TB)], ("bias_rows",), ("anchors_",),
                                            ("e2_t", 0), ("e2_t", 1), ("e2_out", 0), ("e2_out", 1), ("e2_out", 2))))


def first_attention(s):
    core = attention(s, 0)
    if s == 0:
        for n, item in enumerate(conditioning(s)):
            core.insert(3 * n + 40, item)
    return core


def sequence(s):
    return (self_in(s, 0, 0) + first_attention(s) + attention_end(s, 0) + cross(s, 1, 1) + mlp(s, 0, 2) + layer1(s)
            + cross(s, 2, 4) + self_in(s, 3, 5) + attention(s, 3) + attention_end(s, 3) + cross(s, 4, 6) + mlp(s, 1, 7)
            + of(s, ("store",)))


HOLDS = {"mask_t": (.3, .7), "bias_rows": (1.2, .5), "anchors_": (3., .2), "e2_t": (.6, .5), "e2_out": (.9, .5),
         "ln_stats": (1.4,), "ln_rstd": (1.,), "ln_norm": (1.,), "ctx_stats": (2.,), "ln_t": (.8, .7),
         "ctx_norm": (2.7,), "rope": (.9, 1.), "part1": (.5,), "parts": (1.4,), "v": (.9, .5), "ctx_t": (.2, .5),
         "ctx_k": (.8, .8), "gate_cols": (.7,), "ctx_v": (.9, .8), "gates": (.5, .8), "ctx_split": (1.6,), "max_parts": (1.1,),
         "max_t": (.2, .3), "pv": (.9,), "pv_out": (0.24,), "heads_t": (0.4, 0.8), "attn_t": (.4, .5), "attn_out": (.9, .6),
         "proj": (.9, .5), "bias": (1.2,), "mlp_h": (.9, .6), "mlp_out": (3.5, 1.3), "l1_scores": (.8, .6), "l1_exp": (1.9,),
         "l1_probs": (.6,), "l1_probs_t": (.4, .5), "l1_evidence": (.9, .5), "router": (2., .5), "router_exp": (.1,),
         "router_probs": (.5,), "gate_h": (1.7, .6), "expert_h": (2.2, 0.77), "gate": (2.7, 0.78), "expert_out": (1.6, 0.8),
         "l1_add": (1.3,), "load": (1.4,), "store": (.5,), "part1_out": (.5,), "parts_out": (0.72,), "stack": (.9,),
         "ctx_out": (1.4,), "ctx_stack": (2.7,), "max_rows": (1.1,)}
LINK, LANDED = 0.35, 1.87
FAIR, CAP = 0.0093, 0.79
AHEAD = 0.5


class Order:

    def __init__(self):
        self.steps, self.waiting = [], []
        self.free = dict.fromkeys(ENGINES, 0.)
        self.at = [dict() for _ in range(LANES)]
        self.banks = {"max": [0., 0.], "exp": [0., 0.]}

    def holds(self, item):
        kind = item[1]
        if kind in ("max", "exp"):
            a = item[2]
            return (.43 if (kind, a) == ("exp", 0) else .2, (0.6 if a in SELF else .4) if kind == "max" else 0.4426)
        return HOLDS[kind]

    def ready(self, item):
        at, kind = self.at[item[0] % LANES], item[1]
        if kind == "max":
            return max(at.get("stacked", 0.), self.banks["max"][0])
        if kind == "exp":
            return max(at.get(("rows", item[3]), 0.), self.banks["exp"][0])
        if kind in ("max_parts", "max_t", "max_rows"):
            return at.get("maxima", 0.)
        if kind == "stack":
            return at.get("written", 0.)
        return at.get("chain", 0.)

    def run(self, item):
        self.steps.append(item)
        at, kind = self.at[item[0] % LANES], item[1]
        now = self.ready(item)
        for engine, hold in zip(STEPS[kind], self.holds(item)):
            now = max(now, self.free[engine]) + hold
            self.free[engine] = now
            now += LINK
        if kind in ("max", "exp"):
            self.banks[kind] = [self.banks[kind][1], now]
        if kind in ("max", "max_parts", "max_t"):
            at["maxima"] = now
        elif kind == "max_rows":
            at["rows", item[3]] = now + LANDED
        elif kind in ("part1_out", "parts_out"):
            at["written"] = now + LANDED
        elif kind == "stack":
            at["stacked"] = now + LANDED
        elif kind == "exp":
            at["tiles"] = now
        elif kind not in ("pv", "ctx_out", "ctx_stack", "bias"):
            at["chain"] = max(now, at.get("chain", 0.))

    def product(self):
        while self.waiting:
            s, _, a, hg, k = step = self.waiting.pop()
            self.free["pe"] = max(self.free["pe"], self.at[s % LANES]["tiles"])
            self.run(step)
            if k == tiles(a) // 4 - 1 and hg % 2:
                at = self.at[s % LANES]
                at["chain"] = max(at["chain"], self.free["pe"] + LINK)
                self.run((s, "pv_out", a, hg // 2))

    def merge(self, lists):
        taken = {}

        def start(lane):
            item = lists[lane][0]
            if item[0] in ("take", "give", "product"):
                return 0.
            step = item[1][0] if item[0] == "bunch" else item
            at = max(self.free[STEPS[step[1]][0]], self.ready(step))
            behind = max(0, len(lists[lane]) - min(map(len, lists)))
            return at - min(FAIR * behind, CAP) - (0. if step[1] in ("max", "exp") else AHEAD)

        while any(lists):
            lanes = [lane for lane in range(LANES) if lists[lane] and not (lists[lane][0][0] == "take" and lists[lane][0][1] in taken)]
            if not lanes:
                raise RuntimeError("each sequence waits for the other")
            lane = min(lanes, key=start)
            item = lists[lane].pop(0)
            if item[0] == "take":
                taken[item[1]] = lane
            elif item[0] == "give":
                del taken[item[1]]
            elif item[0] == "product":
                self.product()
                self.waiting.append(item[1])
            elif item[0] == "bunch":
                for step in item[1]:
                    self.run(step)
            else:
                if item[1] == "heads_t" and self.waiting and self.waiting[0][0] == item[0]:
                    self.product()
                self.run(item)
        return self.steps


def plan():
    lists = [[item for s in range(lane, B, LANES) for item in sequence(s)] for lane in range(LANES)]
    lists[1] = tables() + lists[1]
    return Order().merge(lists)


PLAN = plan()

ORDER = {e: {} for e in ENGINES}
for step_ in PLAN:
    for e_ in STEPS[step_[1]]:
        assert step_ not in ORDER[e_], step_
        ORDER[e_][step_] = len(ORDER[e_]) + 1


def all_of(*kinds):
    return [s for s in PLAN if s[1] in kinds]


CHAIN_STEPS = all_of(*CHAIN)
CHAIN_AT = {s: n for n, s in enumerate(CHAIN_STEPS)}
MAX_STEPS, EXP_STEPS, PV_STEPS = all_of("max"), all_of("exp"), all_of("pv")
MAX_AT = {s: n for n, s in enumerate(MAX_STEPS)}
EXP_AT = {s: n for n, s in enumerate(EXP_STEPS)}
PV_OUT = [[s for s in all_of("pv_out") if s[0] % LANES == lane] for lane in range(LANES)]
CORES = [(s[0], s[2]) for s in all_of("stack") if s[3:] == (1, 0)]


def before_in_plan(step, s, *kinds):
    found = None
    for other in PLAN:
        if other == step:
            return found
        if other[1] in kinds and (s is None or s % LANES == other[0] % LANES):
            found = other


def freed_by(step):
    kind, engine = CHAIN[step[1]]
    return engine, (step[0], kind, *step[2:])


def build(nc, io, out):
    ctx = ExitStack()
    with ctx:
        def sb(name, shape, dt=F32):
            return ctx.enter_context(nc.sbuf_tensor(name, shape, dt))

        def ps(name, shape, dt=F32):
            return ctx.enter_context(nc.psum_tensor(name, shape, dt))

        def sem(name):
            return ctx.enter_context(nc.semaphore(name))

        def per(name, shape, dt=F32):
            return [sb(f"{name}{lane}", shape, dt) for lane in range(LANES)] * (B // LANES)

        def shared(name, shape, dt=F32):
            return [sb(name, shape, dt)] * B

        def columns(table):
            return sum(n for _, n in table)

        def column(table, name):
            at = 0
            for other, n in table:
                if other == name:
                    return at, n
                at += n

        early = sb("early", [P, columns(EARLY_W)]); late = sb("late", [P, columns(LATE_W)])

        def w(name):
            for held, table in ((early, EARLY_W), (late, LATE_W)):
                if name in [other for other, _ in table]:
                    at, n = column(table, name)
                    return held[:, at:at + n]

        cols, mod_b, e_b2, ident, tail = w("cols"), w("mod_b"), w("e_b2"), w("ident"), w("tail")
        w_rt = w("w_rt").rearrange("p (c e) -> p c e", c=3)
        w_qkv0, w_o0, w_co, w_p2, w_pr3, w_cp3 = w("w_qkv0"), w("w_o0"), w("w_co"), w("w_p2"), w("w_pr3"), w("w_cp3")
        w_ck, w_k1, w_cv, w_v1, w_kv2, w_kvc3 = w("w_ck"), w("w_k1"), w("w_cv"), w("w_v1"), w("w_kv2"), w("w_kvc3")
        w_cq, w_q1, w_g2, w_q2, w_qkv3, w_qc3 = w("w_cq"), w("w_q1"), w("w_g2"), w("w_q2"), w("w_qkv3"), w("w_qc3")
        w_m1 = [w("w_m10"), w("w_m11")]
        w_m2 = [w(name).rearrange("p (c d) -> p c d", c=FC) for name in ("w_m20", "w_m21")]
        w_e1 = w("w_e1").rearrange("p (c e r) -> p c e r", c=2, e=E)
        w_g1 = w("w_g1").rearrange("p (c d) -> p c d", c=2)
        w_rot = sb("w_rot", [P, 2 * D]); w_e2o = sb("w_e2o", [P, 2 * E, D])
        cos = sb("cos", [P, ROPE]); sin = sb("sin", [P, ROPE])
        identb = sb("identb", [P, P], BF16); ones = sb("ones", [P, P])
        mod = sb("mod", [P, NMOD, B]); cond = sb("cond", [P, 2, B]); affine = sb("affine", [P, NLN, 2, B])
        anchors = sb("anchors", [P, 7, B]); rt_all = sb("rt_all", [P, B, E])
        g2_row = sb("g2_row", [1, D]); e2_row = sb("e2_row", [1, E * D])
        bias_b = sb("bias_b", [P, 5, D])
        mask_q = sb("mask_q", [P, TB, T], BF16); mask_k = sb("mask_k", [P, TB, T], BF16)
        eps_pow = sb("eps_pow", [P, 1])

        x = per("x", [P, TB, D])
        stats = per("stats", [P, TB, 6]); mv = per("mv", [P, TB, 2]); var = per("var", [P, TB]); rstd = per("rstd", [P, TB])
        cx = per("cx", [NK, D]); cstats = per("cstats", [NK, 6]); cmv = per("cmv", [NK, 2])
        cvar = per("cvar", [NK, 2]); crstd = per("crstd", [NK, 2])
        cmask = per("cmask", [P, NK], U8); cmaskf = per("cmaskf", [P, NK]); cany = per("cany", [P, 1])
        cbias = per("cbias", [P, NK], BF16)
        g_o0 = per("g_o0", [P, D]); g_co = per("g_co", [P, D]); g_pr = per("g_pr", [P, D])
        g_mlp = per("g_mlp", [P, 2, D]); g_bias = per("g_bias", [P, 3, D])
        kc1 = per("kc1", [P, NK])
        ksc = per("ksc", [P, 3, G, 2, NK], BF16); vac = per("vac", [P, 3, 2, 2, 4, 32]); vc1 = per("vc1", [NK, D])
        qs = per("qs", [P, G, T], BF16); va = per("va", [P, 2, TB, 2, 4, 32])
        mx = per("mx", [P, 2, TB, 2, 2]); mr = per("mr", [P, TB * 2, 2]); mp = per("mp", [P, 2, TB, 2, 3, 2], BF16)
        mrow = per("mrow", [12, 2, T], BF16)
        u = per("u", [P, 2, T]); rec = per("rec", [P, 2, TB, 4, 2])
        m1 = per("m1", [P, TB]); nm1 = per("nm1", [P, TB]); s1 = per("s1", [P, TB]); rs1 = per("rs1", [P, TB])
        lg = per("lg", [P, TB, E]); lm = per("lm", [P, TB]); lsub = per("lsub", [P, TB, E]); lex = per("lex", [P, TB, E])
        lsum = per("lsum", [P, TB]); lrec = per("lrec", [P, TB]); prob = per("prob", [P, TB, E])
        gt, ro = ([u[s][:, i, :].rearrange("p (t d) -> p t d", t=TB) for s in range(B)] for i in range(2))

        xn = per("xn", [P, TB, D]); ao = xn
        cxn = [xn[s][0:NK, 0:2, :] for s in range(B)]
        kc = [xn[s][:, 2:4, :].rearrange("p t d -> p (t d)")[:, 0:3 * NK].rearrange("p (c n) -> p c n", c=3) for s in range(B)]
        es = [xn[s][:, :, :].rearrange("p t d -> p (t d)")[:, 0:TB * NK].rearrange("p (t n) -> p t n", t=TB) for s in range(B)]
        xt = per("xt", [P, T]); aot = xt
        ro2 = [xt[s][:, :].rearrange("p (t d) -> p t d", t=TB) for s in range(B)]
        ks = shared("ks", [P, 2, G, T], BF16)
        hid = shared("hid", [P, 2 * E, T])
        qf, r1, r2 = ([[hid[s][:, 2 * i + w, :] for s in range(B)] for w in range(2)] for i in range(3))
        cb = [hid[s][:, 4:6, :].rearrange("p a n -> p (a n)")[:, 0:5 * P].rearrange("p (g m) -> p g m", g=5) for s in range(B)]
        qp = [per("qp", [P, 3, T], BF16),
              [u[s][:, :, :].rearrange("p a n -> p (a n)")[:, 0:3 * T // 2].bitcast(BF16).rearrange("p (c n) -> p c n", c=3) for s in range(B)]]
        evt = shared("evt", [P, T])
        kcp = [evt[s][:, 0:(9 * NK + 1) // 2].bitcast(BF16)[:, 0:9 * NK].rearrange("p (a b n) -> p a b n", a=3, b=3) for s in range(B)]
        pg = shared("pg", [P, T]); gh = pg
        pt = [pg[s][0:NK, :] for s in range(B)]
        cxt = [pg[s][:, 0:3 * NK].rearrange("p (c n) -> p c n", c=3) for s in range(B)]
        kcr = [pg[s][:, 3 * NK:6 * NK].rearrange("p (c n) -> p c n", c=3) for s in range(B)]
        pr = sb("pr", [P, NSLOT * 4, T])
        scratch = pr[:, :, :].rearrange("p a n -> p (a n)")
        sw = columns(SETUP_W)

        def setup_w(name):
            at, n = column(SETUP_W, name)
            return scratch[:, at:at + n]

        w_ada, w_ssq, w_sskv, w_mod, w_out = (setup_w(n) for n in ("w_ada", "w_ssq", "w_sskv", "w_mod", "w_out"))
        w_anchor = setup_w("w_anchor").rearrange("p (c d) -> p c d", c=7)
        w_e2 = setup_w("w_e2").rearrange("p (n d) -> p n d", n=2 * E)
        w_e2t = scratch[:, sw:sw + 2 * E * P].rearrange("p (e r) -> p e r", e=2 * E)
        mask_u = scratch[:, sw + 2 * E * P:sw + 2 * E * P + T].bitcast(U8).rearrange("p (t k) -> p t k", t=TB)
        cb_all = scratch[:, sw + 2 * E * P:sw + 2 * E * P + B * P].rearrange("p (b m) -> p b m", b=B)
        bvb = scratch[:, sw + 2 * E * P + T:sw + 2 * E * P + T + 3 * P].rearrange("p (a m) -> p a m", a=3)
        rows = evt[0][0:1, :].rearrange("p (r d) -> p r d", r=NROW)
        rt_row = scratch[0:1, sw + 2 * E * P + T + 3 * P:sw + 2 * E * P + T + 3 * P + E]

        chain = [ps(f"chain{n}", [P, T]) for n in range(2)]
        pvb = [ps(f"pvb{lane}", [P, T]) for lane in range(LANES)] * (B // LANES)
        mxb = [ps(f"mxb{n}", [P, T]) for n in range(2)]
        exb = [ps(f"exb{n}", [P, T]) for n in range(2)]

        q_parts = [nc.dram_tensor(f"q_parts{lane}", [P, COMBOS, T], BF16).ap() for lane in range(LANES)] * (B // LANES)
        k_parts = [nc.dram_tensor(f"k_parts{lane}", [P, COMBOS, T], BF16).ap() for lane in range(LANES)] * (B // LANES)
        c_parts = [nc.dram_tensor(f"c_parts{lane}", [3, P, COMBOS, NK], BF16).ap() for lane in range(LANES)] * (B // LANES)

        loaded, loaded_cond, loaded_mask, loaded_late = sem("loaded"), sem("loaded_cond"), sem("loaded_mask"), sem("loaded_late")
        set_pe, set_act, set_dve = sem("set_pe"), sem("set_act"), sem("set_dve")
        done = {e: sem(f"{e}_done") for e in ENGINES if e != "sp"}
        pe_done, act_done, dve_done, pool_done = (done[e] for e in ENGINES[:4])
        dve_link, pool_link = sem("dve_link"), sem("pool_link")
        x_in = [sem(f"x_in{s}") for s in range(B)]; ctx_in = [sem(f"ctx_in{s}") for s in range(B)]
        cwrit = [sem(f"ctx_parts_written{s}") for s in range(B)]; cread = [sem(f"ctx_stacked{s}") for s in range(B)]
        qwrit = [sem(f"q_parts_written{s}") for s in range(B)]; kwrit = [sem(f"k_parts_written{s}") for s in range(B)]
        qread = [sem(f"q_stacked{s}") for s in range(B)]; kread = [[sem(f"k_stacked{s}_{h}") for h in range(2)] for s in range(B)]
        mrows = [[sem(f"max_rows{s}_{hg}") for hg in range(HG)] for s in range(B)]
        stored = [sem(f"stored{s}") for s in range(B)]

        def link(eng, s, count, ins):
            ins.then_inc(s, 1)
            count[0] += 1
            eng.wait_ge(s, count[0])

        with nc.Block() as block:
            LOADS = 16 * 8

            @block.sync
            def _(sp):
                sp.dma_start(scratch[:, 0:sw], io["setup_w"]).then_inc(loaded, 16)
                sp.dma_start(early[:, :], io["early_w"]).then_inc(loaded, 16)
                for s in range(LANES):
                    sp.dma_start(x[s][:, :, :], io["x"][s:s + 1].rearrange("a (t p) d -> p (a t) d", p=P)).then_inc(x_in[s], 16)
                sp.dma_start(bias_b[:, 3:5, :], io["mlp_bias"].rearrange("(a r) d -> a r d", a=1).to_broadcast([P, 2, D])).then_inc(loaded, 16)
                sp.dma_start(g2_row[0:1, :], io["gate_bias"]).then_inc(loaded, 16)
                sp.dma_start(rows[0:1, :, :], io["bias_rows"].rearrange("(a r) d -> a r d", a=1)).then_inc(loaded, 16)
                sp.dma_start(rt_row[0:1, :], io["L1_xcond_router_b"].rearrange("(a e) -> a e", a=1)).then_inc(loaded, 16)
                sp.dma_start(late[:, :], io["late_w"]).then_inc(loaded_late, 16)

            @block.scalar
            def _(act):
                act.dma_start(cond[:, 0, :], io["cond_t"]).then_inc(loaded_cond, 16)
                act.dma_start(mask_u[:, :, :], io["mask_SxS_bk0"].rearrange("(a p) k -> p a k", p=P)).then_inc(loaded_mask, 16)
                act.dma_start(cos[:, :], io["c_cos"]).then_inc(loaded, 16)
                act.dma_start(sin[:, :], io["c_sin"]).then_inc(loaded, 16)
                act.wait_ge(loaded_cond, 16)
                act.activation(cond[:, 1, :], cond[:, 0, :], ACT.Silu).then_inc(set_act, 1)

            MODW = ([(w_ada, c, 0) for c in range(9)] + [(w_ssq, c, 1) for c in range(2)]
                    + [(w_sskv, c, 1) for c in range(2)] + [(w_mod, c, 1) for c in range(6)])

            @block.gpsimd
            def _(pool):
                for s in range(LANES):
                    pool.memset(qs[s][96:128, :, :], 1.0)

            @block.vector
            def _(dve):
                n = [0]

                def do(ins):
                    link(dve, dve_link, n, ins)

                dve.memset(ones[:, :], 1.0)
                dve.memset(eps_pow[:, :], -0.5)
                for s in range(LANES):
                    dve.memset(va[s][:, :, :, :, :, :], 0.0)
                    do(dve.memset(vac[s][:, :, :, :, :, :], 0.0))
                    for par in range(2):
                        dve.memset(va[s][:, par, :, :, :, 16 * par + 8:16 * par + 16], 1.0)
                        dve.memset(vac[s][0:NK, :, par, :, :, 16 * par + 8:16 * par + 16], 1.0)
                dve.wait_ge(loaded_mask, 16)
                do(dve.tensor_scalar(mask_q[:, :, :], mask_u[:, :, :], 1.0, BIG, ALU.subtract, ALU.mult))
                dve.wait_ge(loaded_cond, 16)
                dve.tensor_copy(cb_all[:, :, :], cond[:, 0, :].rearrange("p (b a) -> p b a", a=1).to_broadcast([P, B, P]))
                dve.wait_ge(loaded, LOADS)
                for i, c in enumerate((C_V2, C_QKV3 + 2, C_KVC + 1)):
                    dve.tensor_copy(bvb[:, i, :], cols[:, c:c + 1].to_broadcast([P, P]))
                dve.tensor_copy(identb[:, :], ident[:, :])
                wv = w_qkv0[:, 0:2 * D].rearrange("p (h r d) -> p h r d", r=2, d=HD // 2)
                rv = w_rot[:, :].rearrange("p (h r d) -> p h r d", r=2, d=HD // 2)
                dve.tensor_scalar(rv[:, :, 0, :], wv[:, :, 1, :], -1.0, None, ALU.mult)
                dve.tensor_copy(rv[:, :, 1, :], wv[:, :, 0, :])
                for e in range(2):
                    dve.tensor_copy(ks[0][:, e, :, :].rearrange("p g n -> p (g n)"), tail[:, e:e + 1].to_broadcast([P, G * T]))
                    for s in range(LANES):
                        dve.tensor_copy(ksc[s][:, :, :, e, :].rearrange("p l g n -> p (l g) n"),
                                        tail[:, e:e + 1].rearrange("p (a b) -> p a b", a=1).to_broadcast([P, 3 * G, NK]))
                dve.wait_ge(set_pe, 1)
                do(dve.tensor_tensor(mod[:, :, :], chain[0][:, 0:NMOD * B].rearrange("p (c b) -> p c b", b=B),
                                     mod_b[:, :].rearrange("p (c a) -> p c a", a=1).to_broadcast([P, NMOD, B]), ALU.add))
                for n_, (sh, sc) in ((0, (0, 1)), (1, (3, 4)), (2, (6, 7)), (4, (10, 9)), (5, (13, 14)), (7, (16, 17)), (8, (12, 11))):
                    if n_ < 3:
                        do(dve.tensor_scalar(affine[:, n_, 0, :], mod[:, sc, :], 1.0, None, ALU.add))
                        dve.tensor_scalar(affine[:, n_, 0, :], affine[:, n_, 0, :], cols[:, C_NW + n_:C_NW + n_ + 1], None, ALU.mult)
                    else:
                        dve.tensor_scalar(affine[:, n_, 0, :], mod[:, sc, :], 1.0, None, ALU.add)
                    dve.tensor_copy(affine[:, n_, 1, :], mod[:, sh, :])
                for k in range(2):
                    dve.tensor_copy(affine[:, 3, k, :], cols[:, C_GB + k:C_GB + k + 1].to_broadcast([P, B]))
                    dve.memset(affine[:, 6, k, :], 1.0 - k)

            @block.tensor
            def _(pe):
                pe.wait_ge(loaded, LOADS)
                pe.wait_ge(set_act, 1)
                for n, (wt, c, which) in enumerate(MODW):
                    mm = pe.matmul(chain[0][:, n * B:(n + 1) * B], wt[:, c * D:(c + 1) * D], cond[:, which, :], start=True, stop=True)
                mm.then_inc(set_pe, 1)

        nc.gpsimd.sem_clear(dve_link)
        nc.all_engine_barrier(sem_only=True)

        with nc.Block(no_gpsimd_drain=True) as block:
            def count(engine, step):
                return ORDER[engine][step]

            def chain_bank(pe, step):
                n = CHAIN_AT[step]
                if n >= 2:
                    engine, taken = freed_by(CHAIN_STEPS[n - 2])
                    pe.wait_ge(done[engine], count(engine, taken))
                return chain[n % 2]

            def bank(step):
                return chain[CHAIN_AT[step] % 2]

            def blocks(ap, n=TB):
                return ap.rearrange("p (t d) -> p t d", t=n)

            QKIN = {0: (w_qkv0, 0), 1: (w_cq, 0), 2: (w_q2, 0), 3: (w_qkv3, 0), 4: (w_qc3, 0), 5: (w_q1, 0)}
            QBIAS = {1: None, 2: C_Q2, 3: C_QKV3, 4: C_QC, 5: None}
            LN_OF = {0: 0, 1: 1, 2: 4, 3: 5, 4: 6, 5: 3}
            LN_OF_MLP = (2, 7)

            @block.sync
            def _(sp):
                def load(k, s):
                    if s >= LANES:
                        sp.wait_ge(stored[s - LANES], 16)
                        sp.dma_start(x[s][:, :, :], io["x"][s:s + 1].rearrange("a (t p) d -> p (a t) d", p=P)).then_inc(x_in[s], 16)
                    sp.dma_start(cx[s][:, :], io["ctx_1024"][s:s + 1].rearrange("a k d -> k (a d)")).then_inc(ctx_in[s], 16)
                    sp.dma_start(cmask[s][:, :], io["mask_BxS2_bf1"][s:s + 1].to_broadcast([P, NK])).then_inc(ctx_in[s], 16)

                def ctx_out(k, s):
                    sp.wait_ge(dve_done, count("dve", (s, "ctx_split")))
                    o = c_parts[s].rearrange("l p c n -> p l c n")
                    sp.dma_start(o[:, :, 0:3, :], kcp[s][:, :, :, :]).then_inc(cwrit[s], 16)
                    sp.dma_start(o[:, :, 3:5, :], kcp[s][:, :, 0:2, :]).then_inc(cwrit[s], 16)
                    sp.dma_start(o[:, :, 5, :], kcp[s][:, :, 0, :]).then_inc(cwrit[s], 16)

                def ctx_stack(k, s):
                    sp.wait_ge(cwrit[s], 48)
                    for l in range(3):
                        v = c_parts[s][l].rearrange("(g e d) c n -> e (d c) g n", e=2, d=HD)
                        for e in range(2):
                            sp.dma_start(ksc[s][48 * e:48 * e + 48, l, :, e, :], v[e]).then_inc(cread[s], 16)

                def part1_out(k, s, a):
                    sp.wait_ge(act_done, count("act", (s, "part1", a, 0)))
                    sp.dma_start(q_parts[s][:, 0:3, :], qp[0][s][:, 0:1, :].to_broadcast([P, 3, T])).then_inc(qwrit[s], 16)

                def parts_out(k, s, a, w):
                    sp.wait_ge(dve_done, count("dve", (s, "parts", a, w)))
                    if w == 0:
                        sp.dma_start(q_parts[s][:, 3:5, :], qp[0][s][:, 1:2, :].to_broadcast([P, 2, T])).then_inc(qwrit[s], 16)
                        sp.dma_start(q_parts[s][:, 5, :], qp[0][s][:, 2, :]).then_inc(qwrit[s], 16)
                    else:
                        sp.dma_start(k_parts[s][:, 0:3, :], qp[1][s][:, :, :]).then_inc(kwrit[s], 16)
                        sp.dma_start(k_parts[s][:, 3:5, :], qp[1][s][:, 0:2, :]).then_inc(kwrit[s], 16)
                        sp.dma_start(k_parts[s][:, 5, :], qp[1][s][:, 0, :]).then_inc(kwrit[s], 16)

                def stack(k, s, a, w, half=0):
                    if w == 0:
                        sp.wait_ge(qwrit[s], 48 * (a + 1))
                        sp.dma_start(qs[s][0:STACK, :, :],
                                     q_parts[s].rearrange("(g ed) c n -> (ed c) g n", g=G)).then_inc(qread[s], 16)
                    else:
                        sp.wait_ge(kwrit[s], 48 * (SELF.index(a) + 1))
                        n = CORES.index((s, a))
                        if n:
                            o, oa = CORES[n - 1]
                            sp.wait_ge(pe_done, count("pe", (o, "exp", oa, 2 * half + 1, 15)))
                        v = k_parts[s].rearrange("(g e d) c n -> e (d c) g n", e=2, d=HD)
                        for e in range(2):
                            sp.dma_start(ks[s][48 * e:48 * e + 48, e, 4 * half:4 * half + 4, :],
                                         v[e][:, 4 * half:4 * half + 4]).then_inc(kread[s][half], 16)

                def max_rows(k, s, a, hg):
                    sp.wait_ge(dve_done, count("dve", (s, "max_t", a, hg)))
                    for g in range(2):
                        sp.dma_start(qs[s][MROW:ROWS, 2 * hg + g, :], mrow[s][6 * g:6 * g + 6, hg % 2, :]).then_inc(mrows[s][hg], 16)

                def store(k, s):
                    sp.wait_ge(dve_done, count("dve", (s, "mlp_out", 1)))
                    sp.dma_start(out[s:s + 1].rearrange("a (t p) d -> p (a t) d", p=P), x[s][:, :, :]).then_inc(stored[s], 16)

                parts = locals()
                for step in PLAN:
                    if "sp" in STEPS[step[1]]:
                        parts[step[1]](step, step[0], *step[2:])
                for s in range(B):
                    sp.wait_ge(stored[s], 16)

            @block.gpsimd
            def _(pool):
                n = [0]

                def ctx_norm(k, s):
                    pool.wait_ge(dve_done, count("dve", (s, "ctx_stats")))
                    pool.wait_ge(pe_done, count("pe", (s, "ln_t", 0)))
                    link(pool, pool_link, n, pool.tensor_tensor(crstd[s][:, :], cvar[s][:, :], eps_pow[0:NK, 0:1].to_broadcast([NK, 2]), ALU.pow))
                    for j in range(2):
                        ins = pool.tensor_scalar(cxn[s][:, j, :], cx[s][:, :], cmv[s][:, 0:1], crstd[s][:, j:j + 1], ALU.subtract, ALU.mult)
                    ins.then_inc(pool_done, 1)

                def ln_rstd(k, s, m):
                    pool.wait_ge(dve_done, count("dve", (s, "ln_stats", m)))
                    pool.tensor_tensor(rstd[s][:, :], var[s][:, :], eps_pow[:, 0:1].to_broadcast([P, TB]), ALU.pow).then_inc(pool_done, 1)

                def bias(k, s, m):
                    b = {2: bias_b[:, 0:1, :], 3: g_bias[s][:, 1:2, :], 4: bias_b[:, 2:3, :],
                         5: g_bias[s][:, 0:1, :], 6: g_bias[s][:, 2:3, :]}[m]
                    if m in (3, 5, 6):
                        pool.wait_ge(dve_done, count("dve", (s, "gates", 0 if m == 5 else 1)))
                    pool.wait_ge(dve_done, count("dve", (s, "ln_norm", {2: 4, 3: 5, 4: 6, 5: 2, 6: 7}[m])))
                    pool.tensor_tensor(x[s][:, :, :], x[s][:, :, :], b.to_broadcast([P, TB, D]), ALU.add).then_inc(pool_done, 1)

                parts = locals()
                for step in PLAN:
                    if "pool" in STEPS[step[1]]:
                        parts[step[1]](step, step[0], *step[2:])

            @block.scalar
            def _(act):
                def ctx_t(k, s):
                    act.wait_ge(pe_done, count("pe", k))
                    c = blocks(bank(k)[:, 0:3 * NK], 3)
                    act.activation(cxt[s][:, 0, :], c[:, 0, :], ACT.Identity)
                    act.activation(cxt[s][:, 1, :], c[:, 1, :], ACT.Identity, scale=affine[:, 8, 0, s:s + 1], bias=affine[:, 8, 1, s:s + 1])
                    act.activation(cxt[s][:, 2, :], c[:, 2, :], ACT.Identity).then_inc(act_done, 1)

                def heads_values(dst, src):
                    for par in range(2):
                        ins = act.activation(dst[par], src[:, :, par, :, :], ACT.Identity)
                    return ins

                def ctx_v(k, s):
                    act.wait_ge(pe_done, count("pe", k))
                    c = bank(k)
                    for l in range(4):
                        cv = c[0:NK, l * D:(l + 1) * D]
                        if l == 1:
                            act.activation(vc1[s][:, :], cv, ACT.Identity)
                            continue
                        m = {0: 0, 2: 1, 3: 2}[l]
                        ins = heads_values([vac[s][0:NK, m, par, :, :, 16 * par:16 * par + 8] for par in range(2)],
                                           cv.rearrange("p (h q j d) -> p h q j d", h=2, q=2, j=4))
                    ins.then_inc(act_done, 1)

                def v(k, s, a):
                    act.wait_ge(pe_done, count("pe", k))
                    ins = heads_values([va[s][:, par, :, :, :, 16 * par:16 * par + 8].rearrange("p t h j d -> p (t h) j d") for par in range(2)],
                                       bank(k)[:, :].rearrange("p (th q j d) -> p th q j d", q=2, j=4, d=HD))
                    ins.then_inc(act_done, 1)

                def ln_t(k, s, m):
                    act.wait_ge(pe_done, count("pe", k))
                    act.activation(xt[s][:, :], bank(k)[:, :], ACT.Identity, scale=affine[:, m, 0, s:s + 1],
                                   bias=affine[:, m, 1, s:s + 1]).then_inc(act_done, 1)

                def hid_free(k):
                    reader = before_in_plan(k, None, "parts")
                    if reader:
                        act.wait_ge(dve_done, count("dve", reader))

                def proj(k, s, a, w):
                    if w == 0:
                        hid_free(k)
                    act.wait_ge(pe_done, count("pe", k))
                    c = QBIAS[a]
                    kw = {} if c is None else {"bias": cols[:, c + w:c + w + 1]}
                    act.activation(qf[w][s][:, :], bank(k)[:, :], ACT.Identity, **kw).then_inc(act_done, 1)

                def part1(k, s, a, w):
                    if a == 0:
                        act.wait_ge(dve_done, count("dve", (s, "rope", w, 1)))
                    else:
                        act.wait_ge(act_done, count("act", (s, "proj", a, w)))
                    act.activation(qp[w][s][:, 0, :], qf[w][s][:, :], ACT.Identity).then_inc(act_done, 1)

                def exp(k, s, a, hg, t):
                    n = EXP_AT[k]
                    act.wait_ge(pe_done, count("pe", k))
                    if n >= 4 * NSLOT:
                        act.wait_ge(pe_done, count("pe", PV_STEPS[n // 4 - NSLOT]))
                    K = P if a in SELF else NK
                    act.activation(pr[0:K, n % (4 * NSLOT), :], exb[n % 2][0:K, :], ACT.Exp, scale=SCALE).then_inc(act_done, 1)

                def pv_out(k, s, a, ab):
                    act.wait_ge(pe_done, count("pe", (s, "pv", a, 2 * ab + 1, tiles(a) // 4 - 1)))
                    act.activation(u[s][:, ab, :], pvb[s][:, :], ACT.Identity).then_inc(act_done, 1)

                def attn_t(k, s, a):
                    act.wait_ge(pe_done, count("pe", k))
                    act.activation(aot[s][:, :], bank(k)[:, :], ACT.Identity).then_inc(act_done, 1)

                def l1_exp(k, s):
                    act.wait_ge(dve_done, count("dve", (s, "l1_scores")))
                    c = bank((s, "l1_scores"))
                    for t in range(TB):
                        ins = act.activation(es[s][:, t, :], c[:, t * NK:(t + 1) * NK], ACT.Exp, scale=SCALE1,
                                             bias=nm1[s][:, t:t + 1], accum_out=s1[s][:, t:t + 1])
                    ins.then_inc(act_done, 1)

                def l1_probs_t(k, s):
                    act.wait_ge(pe_done, count("pe", k))
                    act.activation(pt[s][:, :], bank(k)[0:NK, :], ACT.Identity).then_inc(act_done, 1)

                def l1_evidence(k, s):
                    for o in range(B):
                        if PLAN.index((o, "ctx_out")) < PLAN.index(k):
                            act.wait_ge(cwrit[o], 48)
                    act.wait_ge(pe_done, count("pe", k))
                    act.activation(evt[s][:, :], bank(k)[:, :], ACT.Identity).then_inc(act_done, 1)

                def router_exp(k, s):
                    act.wait_ge(dve_done, count("dve", (s, "router")))
                    act.activation(lex[s][:, :, :], lsub[s][:, :, :], ACT.Exp).then_inc(act_done, 1)

                def expert_h(k, s, i):
                    act.wait_ge(pe_done, count("pe", k))
                    act.activation(hid[s][:, i, :], bank(k)[:, :], ACT.Silu, bias=anchors[:, i, s:s + 1]).then_inc(act_done, 1)

                def gate_h(k, s):
                    hid_free(k)
                    act.wait_ge(pe_done, count("pe", k))
                    act.activation(gh[s][:, :], bank(k)[:, :], ACT.Silu, bias=anchors[:, 6, s:s + 1]).then_inc(act_done, 1)

                def gate(k, s):
                    act.wait_ge(pe_done, count("pe", k))
                    act.activation(gt[s][:, :, :], blocks(bank(k)[:, :]), ACT.Tanh, scale=0.5).then_inc(act_done, 1)

                def mlp_h(k, s, m, c):
                    if c == 0:
                        hid_free(k)
                    act.wait_ge(pe_done, count("pe", k))
                    act.activation(hid[s][:, c, :], bank(k)[:, :], ACT.Gelu_apprx_tanh,
                                   bias=cols[:, C_M1[m] + c:C_M1[m] + c + 1]).then_inc(act_done, 1)

                parts = locals()
                for step in PLAN:
                    if "act" in STEPS[step[1]]:
                        parts[step[1]](step, step[0], *step[2:])

            @block.vector
            def _(dve):
                n = [0]

                def do(ins):
                    link(dve, dve_link, n, ins)

                def gate_cols(k, s):
                    reader = before_in_plan(k, None, "mlp_out", "expert_out")
                    if reader:
                        dve.wait_ge(pe_done, count("pe", reader))
                    dve.tensor_copy(cb[s][:, 0:3, :], mod[:, GATES[0]:GATES[2] + 1:3, s:s + 1].to_broadcast([P, 3, P]))
                    dve.tensor_copy(cb[s][:, 3:5, :], mod[:, GATES[3]:GATES[4] + 1:3, s:s + 1].to_broadcast([P, 2, P])).then_inc(dve_done, 1)

                def gates(k, s, l):
                    dve.wait_ge(pe_done, count("pe", k))
                    c = bank(k)
                    if l == 0:
                        dve.tensor_tensor(g_o0[s][:, :], w_o0[:, :], c[:, 0:D], ALU.mult)
                        dve.tensor_tensor(g_co[s][:, :], w_co[:, :], c[:, D:2 * D], ALU.mult)
                        dve.tensor_tensor(g_bias[s][:, 0, :], bias_b[:, 3, :], c[:, 2 * D:3 * D], ALU.mult)
                        dve.tensor_copy(g_mlp[s][:, 0, :], c[:, 2 * D:3 * D]).then_inc(dve_done, 1)
                    else:
                        dve.tensor_tensor(g_pr[s][:, :], w_pr3[:, :], c[:, 0:D], ALU.mult)
                        dve.tensor_tensor(g_bias[s][:, 1, :], bias_b[:, 1, :], c[:, 0:D], ALU.mult)
                        dve.tensor_tensor(g_bias[s][:, 2, :], bias_b[:, 4, :], c[:, D:2 * D], ALU.mult)
                        dve.tensor_copy(g_mlp[s][:, 1, :], c[:, D:2 * D]).then_inc(dve_done, 1)

                def mask_t(k, s, kb):
                    dve.wait_ge(pe_done, count("pe", k))
                    dve.tensor_copy(mask_k[:, kb, :], bank(k)[:, :].bitcast(BF16)[:, 0:T]).then_inc(dve_done, 1)

                def bias_rows(k, s):
                    dve.wait_ge(pe_done, count("pe", k))
                    dve.tensor_copy(bias_b[:, 0:3, :], blocks(bank(k)[:, 0:3 * D], 3)).then_inc(dve_done, 1)

                def anchors_(k, s):
                    dve.wait_ge(pe_done, count("pe", k))
                    dve.tensor_tensor(anchors[:, :, :], bank(k)[:, 0:7 * B].rearrange("p (c b) -> p c b", b=B),
                                      cols[:, C_E1:C_E1 + 7].rearrange("p (c a) -> p c a", a=1).to_broadcast([P, 7, B]), ALU.add)
                    dve.tensor_copy(rt_all[:, :, :], bank(k)[:, 7 * B:7 * B + B * E].rearrange("p (b e) -> p b e", b=B)).then_inc(dve_done, 1)

                def e2_t(k, s, i):
                    dve.wait_ge(pe_done, count("pe", k))
                    m = (4, 2)[i]
                    dve.tensor_copy(w_e2t[:, 4 * i:4 * i + m, :], blocks(bank(k)[:, 0:m * P], m)).then_inc(dve_done, 1)

                def e2_out(k, s, i):
                    dve.wait_ge(pe_done, count("pe", k))
                    if i < 2:
                        m = (4, 2)[i]
                        dve.tensor_copy(w_e2o[:, 4 * i:4 * i + m, :], blocks(bank(k)[:, 0:m * D], m)).then_inc(dve_done, 1)
                    else:
                        dve.tensor_copy(e2_row[0:1, :], bank(k)[0:1, 0:E * D]).then_inc(dve_done, 1)

                def ctx_stats(k, s):
                    dve.wait_ge(ctx_in[s], 32)
                    do(dve.bn_stats(cstats[s][:, :], cx[s][:, :]))
                    do(dve.bn_aggr(cmv[s][:, :], cstats[s][:, :]))
                    dve.tensor_scalar(cvar[s][:, 0:1], cmv[s][:, 1:2], EPS[4], None, ALU.add)
                    do(dve.tensor_scalar(cvar[s][:, 1:2], cmv[s][:, 1:2], EPS[6], None, ALU.add))
                    do(dve.tensor_reduce(cany[s][:, :], cmask[s][:, :], AX.X, ALU.max))
                    do(dve.tensor_scalar(cmaskf[s][:, :], cmask[s][:, :], 1.0, BIG, ALU.subtract, ALU.mult))
                    do(dve.tensor_scalar(cbias[s][:, :], cmaskf[s][:, :], cany[s][:, 0:1], None, ALU.mult))
                    dve.tensor_copy(ksc[s][96:97, 0, :, :, :].rearrange("p g e n -> p (g e) n"),
                                    cbias[s][96:97, :].rearrange("p (a n) -> p a n", a=1).to_broadcast([1, 2 * G, NK])).then_inc(dve_done, 1)

                def ctx_k(k, s):
                    dve.wait_ge(pe_done, count("pe", k))
                    c = blocks(bank(k)[:, 0:4 * NK], 4)
                    dve.tensor_scalar(kc[s][:, 0, :], c[:, 0, :], cany[s][:, 0:1], None, ALU.mult)
                    dve.tensor_copy(kc1[s][:, :], c[:, 1, :])
                    dve.tensor_scalar(kc[s][:, 1, :], c[:, 2, :], cols[:, C_K2:C_K2 + 1], None, ALU.add)
                    dve.tensor_scalar(kc[s][:, 2, :], c[:, 3, :], cols[:, C_KVC:C_KVC + 1], None, ALU.add).then_inc(dve_done, 1)

                def ctx_split(k, s):
                    dve.wait_ge(dve_done, count("dve", (s, "ctx_k")))
                    written = before_in_plan(k, None, "ctx_out")
                    if written:
                        dve.wait_ge(cwrit[written[0]], 48)
                    do(dve.tensor_copy(kcp[s][:, :, 0, :], kc[s][:, 0:3, :]))
                    do(dve.tensor_tensor(kcr[s][:, :, :], kc[s][:, 0:3, :], kcp[s][:, :, 0, :], ALU.subtract))
                    do(dve.tensor_copy(kcp[s][:, :, 1, :], kcr[s][:, :, :]))
                    dve.tensor_tensor(kcp[s][:, :, 2, :], kcr[s][:, :, :], kcp[s][:, :, 1, :], ALU.subtract).then_inc(dve_done, 1)

                def ln_stats(k, s, m):
                    if m == 0:
                        dve.wait_ge(x_in[s], 16)
                    else:
                        prev = {1: ("attn_out", 0), 2: ("attn_out", 1), 3: ("mlp_out", 0), 4: ("l1_add",), 5: ("attn_out", 2),
                                6: ("attn_out", 3), 7: ("attn_out", 4)}[m]
                        dve.wait_ge(dve_done, count("dve", (s, *prev)))
                    for t in range(TB):
                        ins = dve.bn_stats(stats[s][:, t, :], x[s][:, t, :])
                    do(ins)
                    for t in range(TB):
                        ins = dve.bn_aggr(mv[s][:, t, :], stats[s][:, t, :])
                    do(ins)
                    dve.tensor_scalar(var[s][:, :], mv[s][:, :, 1], EPS[m], None, ALU.add).then_inc(dve_done, 1)

                def ln_norm(k, s, m):
                    dve.wait_ge(pool_done, count("pool", (s, "ln_rstd", m)))
                    reader = before_in_plan(k, s, "ln_t", "ctx_t", "attn_t", "l1_probs_t")
                    if reader:
                        dve.wait_ge(pe_done, count("pe", reader))
                    for t in range(TB):
                        ins = dve.tensor_scalar(xn[s][:, t, :], x[s][:, t, :], mv[s][:, t, 0:1], rstd[s][:, t:t + 1], ALU.subtract, ALU.mult)
                    ins.then_inc(dve_done, 1)

                def rope(k, s, w, r):
                    dve.wait_ge(pe_done, count("pe", k))
                    b = bank(k)[:, :].rearrange("p (h n) -> p h n", n=ROPE)
                    tab = (cos, sin)[r][:, :].rearrange("p (a n) -> p a n", a=1).to_broadcast([P, T // ROPE, ROPE])

                    def halves(ap):
                        return ap.rearrange("p (h n) -> p h n", n=ROPE)

                    if r == 0:
                        dve.tensor_tensor(halves(r1[w][s]), b, tab, ALU.mult).then_inc(dve_done, 1)
                    else:
                        do(dve.tensor_tensor(halves(r2[w][s]), b, tab, ALU.mult))
                        dve.tensor_tensor(qf[w][s][:, :], r1[w][s][:, :], r2[w][s][:, :], ALU.add).then_inc(dve_done, 1)

                def parts(k, s, a, w):
                    dve.wait_ge(act_done, count("act", (s, "part1", a, w)))
                    q, part = qf[w][s], qp[w][s]
                    do(dve.tensor_tensor(r1[w][s][:, :], q[:, :], part[:, 0, :], ALU.subtract))
                    do(dve.tensor_copy(part[:, 1, :], r1[w][s][:, :]))
                    dve.tensor_tensor(part[:, 2, :], r1[w][s][:, :], part[:, 1, :], ALU.subtract).then_inc(dve_done, 1)

                def max(k, s, a, hg, t):
                    dve.wait_ge(pe_done, count("pe", k))
                    b = mxb[MAX_AT[k] % 2]
                    dst = mx[s][:, hg % 2]
                    if a in SELF:
                        g, e, qb = t // 8, t // 4 % 2, t % 4
                        if a == 0:
                            dve.tensor_tensor_reduce(b[:, :], b[:, :], mask_q[:, qb, :], 1.0, -3e38, ALU.add, ALU.max,
                                                     dst[:, qb, g, e:e + 1]).then_inc(dve_done, 1)
                        else:
                            dve.tensor_reduce(dst[:, qb, g, e:e + 1], b[:, :], AX.X, ALU.max).then_inc(dve_done, 1)
                    else:
                        dve.tensor_reduce(dst[:, t, :, :].rearrange("p g e -> p (g e)"),
                                          b[:, 0:4 * NK].rearrange("p (h n) -> p h n", h=4), AX.X, ALU.max).then_inc(dve_done, 1)

                def max_parts(k, s, a, hg):
                    dve.wait_ge(dve_done, count("dve", (s, "max", a, hg, tiles(a) - 1)))
                    m = mx[s][:, hg % 2].rearrange("p t g e -> p (t g) e")
                    part = mp[s][:, hg % 2].rearrange("p t g c e -> p (t g) c e")
                    do(dve.tensor_scalar(part[:, :, 0, :], m, -1.0, None, ALU.mult))
                    do(dve.scalar_tensor_tensor(mr[s][:, :, :], m, -1.0, part[:, :, 0, :], ALU.mult, ALU.subtract))
                    do(dve.tensor_copy(part[:, :, 1, :], mr[s][:, :, :]))
                    dve.tensor_tensor(part[:, :, 2, :], mr[s][:, :, :], part[:, :, 1, :], ALU.subtract).then_inc(dve_done, 1)

                def max_t(k, s, a, hg):
                    dve.wait_ge(pe_done, count("pe", k))
                    if hg >= 2:
                        dve.wait_ge(mrows[s][hg - 2], 32 * (a + 1))
                    elif a:
                        dve.wait_ge(mrows[s][hg + 2], 32 * a)
                    dve.tensor_copy(mrow[s][:, hg % 2, :], bank(k)[:, :].bitcast(BF16)[0:12, 0:T]).then_inc(dve_done, 1)

                def heads_t(k, s, a, ab):
                    dve.wait_ge(pe_done, count("pe", k))
                    c = bank(k)[:, :].rearrange("p (t j q v d) -> p t j q v d", t=TB, j=4, q=2, v=2)
                    rc = rec[s][:, ab]
                    do(dve.reciprocal(rc.rearrange("p t j q -> p (t j) q"),
                                      bank(k)[:, :].rearrange("p (tj q w) -> p tj q w", q=2, w=16)[:, :, :, 8]))
                    for par in range(2):
                        o = ao[s][:, :, 64 * ab + 32 * par:64 * ab + 32 * par + 32].rearrange("p t (j d) -> p t j d", j=4)
                        ins = dve.tensor_tensor(o, c[:, :, :, par, 0, :], rc[:, :, :, par:par + 1].to_broadcast([P, TB, 4, HD]), ALU.mult)
                    ins.then_inc(dve_done, 1)

                def add_residual(k, s):
                    dve.tensor_tensor(x[s][:, :, :], x[s][:, :, :], blocks(bank(k)[:, :]), ALU.add).then_inc(dve_done, 1)

                def attn_out(k, s, a):
                    dve.wait_ge(pe_done, count("pe", k))
                    if a >= 2:
                        dve.wait_ge(pool_done, count("pool", (s, "bias", a)))
                    add_residual(k, s)

                def mlp_out(k, s, m):
                    dve.wait_ge(pe_done, count("pe", k))
                    dve.wait_ge(pool_done, count("pool", (s, "bias", 5 + m)))
                    do(dve.tensor_tensor(xn[s][:, :, :], blocks(bank(k)[:, :]), g_mlp[s][:, m:m + 1, :].to_broadcast([P, TB, D]), ALU.mult))
                    dve.tensor_tensor(x[s][:, :, :], x[s][:, :, :], xn[s][:, :, :], ALU.add).then_inc(dve_done, 1)

                def l1_scores(k, s):
                    dve.wait_ge(pe_done, count("pe", k))
                    do(dve.tensor_reduce(m1[s][:, :], bank(k)[:, 0:TB * NK].rearrange("p (t n) -> p t n", t=TB), AX.X, ALU.max))
                    dve.tensor_scalar(nm1[s][:, :], m1[s][:, :], -SCALE1, None, ALU.mult).then_inc(dve_done, 1)

                def l1_probs(k, s):
                    dve.wait_ge(act_done, count("act", (s, "l1_exp")))
                    do(dve.reciprocal(rs1[s][:, :], s1[s][:, :]))
                    dve.tensor_tensor(es[s][:, :, :], es[s][:, :, :],
                                      rs1[s][:, :].rearrange("p (t a) -> p t a", a=1).to_broadcast([P, TB, NK]), ALU.mult).then_inc(dve_done, 1)

                def over_e(ap):
                    return ap.rearrange("p (t a) -> p t a", a=1).to_broadcast([P, TB, E])

                def router(k, s):
                    dve.wait_ge(pe_done, count("pe", k))
                    do(dve.tensor_tensor(lg[s][:, :, :], bank(k)[:, 0:TB * E].rearrange("p (t e) -> p t e", t=TB),
                                         rt_all[:, s:s + 1, :].to_broadcast([P, TB, E]), ALU.add))
                    do(dve.tensor_reduce(lm[s][:, :], lg[s][:, :, :], AX.X, ALU.max))
                    dve.tensor_tensor(lsub[s][:, :, :], lg[s][:, :, :], over_e(lm[s][:, :]), ALU.subtract).then_inc(dve_done, 1)

                def router_probs(k, s):
                    dve.wait_ge(act_done, count("act", (s, "router_exp")))
                    do(dve.tensor_reduce(lsum[s][:, :], lex[s][:, :, :], AX.X, ALU.add))
                    do(dve.reciprocal(lrec[s][:, :], lsum[s][:, :]))
                    dve.tensor_tensor(prob[s][:, :, :], lex[s][:, :, :], over_e(lrec[s][:, :]), ALU.mult).then_inc(dve_done, 1)

                def expert_out(k, s, t):
                    dve.wait_ge(pe_done, count("pe", k))
                    dve.wait_ge(dve_done, count("dve", (s, "router_probs")))
                    c = bank(k)
                    do(dve.tensor_scalar(ro[s][:, t, :], c[:, 0:D], prob[s][:, t, 0:1], None, ALU.mult))
                    do(dve.scalar_tensor_tensor(ro[s][:, t, :], c[:, D:2 * D], prob[s][:, t, 1:2], ro[s][:, t, :], ALU.mult, ALU.add))
                    dve.scalar_tensor_tensor(ro[s][:, t, :], c[:, 2 * D:3 * D], prob[s][:, t, 2:3], ro[s][:, t, :], ALU.mult, ALU.add).then_inc(dve_done, 1)

                def l1_add(k, s):
                    dve.wait_ge(act_done, count("act", (s, "gate")))
                    dve.wait_ge(dve_done, count("dve", (s, "expert_out", TB - 1)))
                    do(dve.scalar_tensor_tensor(ro2[s][:, :, :], gt[s][:, :, :], 1.0, ro[s][:, :, :], ALU.add, ALU.mult))
                    dve.scalar_tensor_tensor(x[s][:, :, :], ro2[s][:, :, :], 0.5, x[s][:, :, :], ALU.mult, ALU.add).then_inc(dve_done, 1)

                parts_ = locals()
                for step in PLAN:
                    if "dve" in STEPS[step[1]]:
                        parts_[step[1]](step, step[0], *step[2:])

            @block.tensor
            def _(pe):
                def mask_t(k, s, kb):
                    b = chain_bank(pe, k)[:, :].bitcast(BF16)
                    for t in range(TB):
                        ins = pe.transpose(b[:, t * P:(t + 1) * P], mask_q[:, t, kb * P:(kb + 1) * P], identb[:, :])
                    ins.then_inc(pe_done, 1)

                def bias_rows(k, s):
                    b = chain_bank(pe, k)
                    for n, (wt, r) in enumerate(((w_p2, R_P2), (w_pr3, R_PR3), (w_cp3, R_CP3))):
                        pe.matmul(b[:, n * D:(n + 1) * D], bvb[:, n, :], wt, start=True, stop=False)
                        ins = pe.matmul(b[:, n * D:(n + 1) * D], ones[0:1, :], rows[0:1, r, :], start=False, stop=True)
                    ins.then_inc(pe_done, 1)

                def anchors_(k, s):
                    b = chain_bank(pe, k)
                    for i in range(7):
                        pe.matmul(b[:, i * B:(i + 1) * B], w_anchor[:, i, :], cond[:, 0, :], start=True, stop=True)
                    for n in range(B):
                        o = b[:, 7 * B + n * E:7 * B + (n + 1) * E]
                        pe.matmul(o, cb_all[:, n, :], w_rt[:, 2, :], start=True, stop=False)
                        ins = pe.matmul(o, ones[0:1, :], rt_row[0:1, :], start=False, stop=True)
                    ins.then_inc(pe_done, 1)

                def e2_t(k, s, i):
                    b = chain_bank(pe, k)
                    for n in range((4, 2)[i]):
                        ins = pe.transpose(b[:, n * P:(n + 1) * P], w_e2[:, 4 * i + n, :], ident[:, :])
                    ins.then_inc(pe_done, 1)

                def e2_out(k, s, i):
                    b = chain_bank(pe, k)
                    if i < 2:
                        pe.wait_ge(dve_done, count("dve", (s, "e2_t", i)))
                        for n in range((4, 2)[i]):
                            ins = pe.matmul(b[:, n * D:(n + 1) * D], w_e2t[:, 4 * i + n, :], w_out[:, :], start=True, stop=True)
                    else:
                        for e in range(E):
                            pe.matmul(b[0:1, e * D:(e + 1) * D], e_b2[:, e:e + 1], w_out[:, :], start=True, stop=False)
                            ins = pe.matmul(b[0:1, e * D:(e + 1) * D], ones[0:1, 0:1], rows[0:1, R_OUT, :], start=False, stop=True)
                    ins.then_inc(pe_done, 1)

                def gates(k, s, l):
                    b = chain_bank(pe, k)
                    pe.wait_ge(dve_done, count("dve", (s, "gate_cols")))
                    for i, g in enumerate(((0, 1, 2), (3, 4))[l]):
                        ins = pe.matmul(b[:, i * D:(i + 1) * D], cb[s][:, g, :], ident[:, :], start=True, stop=True)
                    ins.then_inc(pe_done, 1)

                def ctx_t(k, s):
                    b = chain_bank(pe, k)
                    pe.wait_ge(pool_done, count("pool", (s, "ctx_norm")))
                    for j in range(3):
                        src = cx[s][:, :] if j == 0 else cxn[s][:, j - 1, :]
                        ins = pe.transpose(b[:, j * NK:(j + 1) * NK], src, ident[0:NK, 0:NK])
                    ins.then_inc(pe_done, 1)

                def ctx_k(k, s):
                    b = chain_bank(pe, k)
                    pe.wait_ge(act_done, count("act", (s, "ctx_t")))
                    for l, (w, j) in enumerate(((w_ck, 0), (w_k1, 0), (w_kv2, 1), (w_kvc3, 2))):
                        ins = pe.matmul(b[:, l * NK:(l + 1) * NK], w[:, 0:D], cxt[s][:, j, :], start=True, stop=True)
                    ins.then_inc(pe_done, 1)

                def ctx_v(k, s):
                    b = chain_bank(pe, k)
                    pe.wait_ge(act_done, count("act", (s, "ctx_t")))
                    for l, (w, j, o) in enumerate(((w_cv, 0, 0), (w_v1, 0, 0), (w_kv2, 1, D), (w_kvc3, 2, D))):
                        ins = pe.matmul(b[0:NK, l * D:(l + 1) * D], cxt[s][:, j, :], w[:, o:o + D], start=True, stop=True)
                    ins.then_inc(pe_done, 1)

                def ln_t(k, s, m):
                    b = chain_bank(pe, k)
                    pe.wait_ge(dve_done, count("dve", (s, "ln_norm", m)))
                    for t in range(TB):
                        ins = pe.transpose(b[:, t * P:(t + 1) * P], xn[s][:, t, :], ident[:, :])
                    ins.then_inc(pe_done, 1)

                def rope(k, s, w, r):
                    b = chain_bank(pe, k)
                    pe.wait_ge(act_done, count("act", (s, "ln_t", 0)))
                    m = (w_qkv0, w_rot)[r]
                    pe.matmul(b[:, :], m[:, w * D:(w + 1) * D], xt[s][:, :], start=True, stop=True).then_inc(pe_done, 1)

                def proj(k, s, a, w):
                    b = chain_bank(pe, k)
                    pe.wait_ge(act_done, count("act", (s, "ln_t", LN_OF[a])))
                    m, o = QKIN[a]
                    if a == 1:
                        pe.wait_ge(loaded_late, 16)
                    pe.matmul(b[:, :], m[:, o + w * D:o + (w + 1) * D], xt[s][:, :], start=True, stop=True).then_inc(pe_done, 1)

                def v(k, s, a):
                    b = chain_bank(pe, k)
                    w = w_qkv0 if a == 0 else w_qkv3
                    for t in range(TB):
                        ins = pe.matmul(b[:, t * D:(t + 1) * D], xt[s][:, t * P:(t + 1) * P], w[:, 2 * D:3 * D], start=True, stop=True)
                    ins.then_inc(pe_done, 1)

                def max(k, s, a, hg, t):
                    if (hg, t) == (0, 0):
                        pe.wait_ge(qread[s], 16 * (a + 1))
                        if a in SELF:
                            pe.wait_ge(kread[s][0], 32 * (SELF.index(a) + 1))
                        elif a == 1:
                            pe.wait_ge(cread[s], 96)
                    if (hg, t) == (2, 0) and a in SELF:
                        pe.wait_ge(kread[s][1], 32 * (SELF.index(a) + 1))
                    n = MAX_AT[k]
                    if n >= 2:
                        pe.wait_ge(dve_done, count("dve", MAX_STEPS[n - 2]))
                    b = mxb[n % 2]
                    R = MASKROW + 1
                    if a in SELF:
                        g, e, qb = 2 * hg + t // 8, t // 4 % 2, t % 4
                        ins = pe.matmul(b[:, :], qs[s][0:R, g, qb * P:(qb + 1) * P], ks[s][0:R, e, g, :], start=True, stop=True)
                    else:
                        for g in range(2):
                            ins = pe.matmul(b[:, g * 2 * NK:(g + 1) * 2 * NK], qs[s][0:R, 2 * hg + g, t * P:(t + 1) * P],
                                            ksc[s][0:R, CL[a], 2 * hg + g, :, :].rearrange("p e n -> p (e n)"), start=True, stop=True)
                    ins.then_inc(pe_done, 1)

                def max_t(k, s, a, hg):
                    pe.wait_ge(dve_done, count("dve", (s, "max_parts", a, hg)))
                    b = chain_bank(pe, k)[:, :].bitcast(BF16)
                    for t in range(TB):
                        ins = pe.transpose(b[0:12, t * P:(t + 1) * P], mp[s][:, hg % 2, t].rearrange("p g c e -> p (g c e)"), identb[:, :])
                    ins.then_inc(pe_done, 1)

                def exp(k, s, a, hg, t):
                    n = EXP_AT[k]
                    if k == EXP_STEPS[0]:
                        pe.wait_ge(dve_done, count("dve", (1, "mask_t", TB - 1)))
                    if t == 0:
                        pe.wait_ge(mrows[s][hg], 32 * (a + 1))
                    if n >= 2:
                        pe.wait_ge(act_done, count("act", EXP_STEPS[n - 2]))
                    b = exb[n % 2]
                    j, kb = t % 4, t // 4
                    g, e = 2 * hg + j // 2, j % 2
                    if a in SELF:
                        ins = pe.matmul(b[:, :], ks[s][0:ROWS, e, g, kb * P:(kb + 1) * P], qs[s][0:ROWS, g, :], start=True, stop=(a != 0))
                        if a == 0:
                            ins = pe.matmul(b[:, :], identb[:, :], mask_k[:, kb, :], start=False, stop=True)
                    else:
                        ins = pe.matmul(b[0:NK, :], ksc[s][0:ROWS, CL[a], g, e, :], qs[s][0:ROWS, g, :], start=True, stop=True)
                    ins.then_inc(pe_done, 1)

                def pv(k, s, a, hg, kb):
                    last = tiles(a) // 4 - 1
                    pe.wait_ge(act_done, count("act", (s, "exp", a, hg, 4 * kb + 3)))
                    if (hg, kb) == (0, 0):
                        pe.wait_ge(act_done, count("act", (s, "v", a) if a in SELF else (s, "ctx_v")))
                    if hg % 2 == 0 and kb == 0:
                        m = PV_OUT[s % LANES].index((s, "pv_out", a, hg // 2))
                        if m:
                            pe.wait_ge(act_done, count("act", PV_OUT[s % LANES][m - 1]))
                    n = EXP_AT[(s, "exp", a, hg, 4 * kb)] % (4 * NSLOT)
                    for j in range(4):
                        w = va[s][:, hg % 2, kb, hg // 2, j, :] if a in SELF else vac[s][:, CL[a], hg % 2, hg // 2, j, :]
                        ins = pe.matmul(pvb[s][32 * j:32 * j + 32, :], w, pr[:, n + j, :],
                                        start=(hg % 2 == 0 and kb == 0), stop=(hg % 2 == 1 and kb == last), skip_group_check=True)
                    ins.then_inc(pe_done, 1)

                def heads_t(k, s, a, ab):
                    b = chain_bank(pe, k)
                    pe.wait_ge(act_done, count("act", (s, "pv_out", a, ab)))
                    for t in range(TB):
                        ins = pe.transpose(b[:, t * P:(t + 1) * P], u[s][:, ab, t * P:(t + 1) * P], ident[:, :])
                    ins.then_inc(pe_done, 1)

                def attn_t(k, s, a):
                    b = chain_bank(pe, k)
                    pe.wait_ge(dve_done, count("dve", (s, "heads_t", a, 1)))
                    for t in range(TB):
                        ins = pe.transpose(b[:, t * P:(t + 1) * P], ao[s][:, t, :], ident[:, :])
                    ins.then_inc(pe_done, 1)

                def attn_out(k, s, a):
                    b = chain_bank(pe, k)
                    pe.wait_ge(act_done, count("act", (s, "attn_t", a)))
                    if a in (0, 1, 3):
                        pe.wait_ge(dve_done, count("dve", (s, "gates", a // 3)))
                    w = (g_o0[s], g_co[s], w_p2, g_pr[s], w_cp3)[a]
                    for t in range(TB):
                        ins = pe.matmul(b[:, t * D:(t + 1) * D], aot[s][:, t * P:(t + 1) * P], w[:, :], start=True, stop=True)
                    ins.then_inc(pe_done, 1)

                def l1_scores(k, s):
                    b = chain_bank(pe, k)
                    pe.wait_ge(act_done, count("act", (s, "proj", 5, 0)))
                    pe.wait_ge(dve_done, count("dve", (s, "ctx_k")))
                    for t in range(TB):
                        ins = pe.matmul(b[:, t * NK:(t + 1) * NK], qf[0][s][:, t * P:(t + 1) * P], kc1[s][:, :], start=True, stop=True)
                    ins.then_inc(pe_done, 1)

                def l1_probs_t(k, s):
                    b = chain_bank(pe, k)
                    pe.wait_ge(dve_done, count("dve", (s, "l1_probs")))
                    for t in range(TB):
                        ins = pe.transpose(b[0:NK, t * P:(t + 1) * P], es[s][:, t, :], ident[:, :])
                    ins.then_inc(pe_done, 1)

                def l1_evidence(k, s):
                    b = chain_bank(pe, k)
                    pe.wait_ge(act_done, count("act", (s, "l1_probs_t")))
                    pe.matmul(b[:, :], vc1[s][:, :], pt[s][:, :], start=True, stop=True).then_inc(pe_done, 1)

                def router(k, s):
                    b = chain_bank(pe, k)
                    pe.wait_ge(act_done, count("act", (s, "l1_evidence")))
                    for t in range(TB):
                        o = b[:, t * E:(t + 1) * E]
                        pe.matmul(o, xt[s][:, t * P:(t + 1) * P], w_rt[:, 0, :], start=True, stop=False)
                        ins = pe.matmul(o, evt[s][:, t * P:(t + 1) * P], w_rt[:, 1, :], start=False, stop=True)
                    ins.then_inc(pe_done, 1)

                def hidden(k, s, w0, w1):
                    b = chain_bank(pe, k)
                    pe.matmul(b[:, :], w0, xt[s][:, :], start=True, stop=False)
                    pe.matmul(b[:, :], w1, evt[s][:, :], start=False, stop=True).then_inc(pe_done, 1)

                def expert_h(k, s, i):
                    hidden(k, s, *[w_e1[:, c, i // 2, (i % 2) * P:(i % 2 + 1) * P] for c in range(2)])

                def gate_h(k, s):
                    pe.wait_ge(act_done, count("act", (s, "l1_evidence")))
                    hidden(k, s, w_g1[:, 0, :], w_g1[:, 1, :])

                def gate(k, s):
                    b = chain_bank(pe, k)
                    pe.wait_ge(act_done, count("act", (s, "gate_h")))
                    for t in range(TB):
                        o = b[:, t * D:(t + 1) * D]
                        pe.matmul(o, gh[s][:, t * P:(t + 1) * P], w_g2[:, :], start=True, stop=False)
                        ins = pe.matmul(o, ones[0:1, :], g2_row[0:1, :], start=False, stop=True)
                    ins.then_inc(pe_done, 1)

                def expert_out(k, s, t):
                    b = chain_bank(pe, k)
                    pe.wait_ge(act_done, count("act", (s, "expert_h", 2 * E - 1)))
                    for e in range(E):
                        o = b[:, e * D:(e + 1) * D]
                        for c in range(2):
                            pe.matmul(o, hid[s][:, 2 * e + c, t * P:(t + 1) * P], w_e2o[:, 2 * e + c, :], start=(c == 0), stop=False)
                        ins = pe.matmul(o, ones[0:1, :], e2_row[0:1, e * D:(e + 1) * D], start=False, stop=True)
                    ins.then_inc(pe_done, 1)

                def mlp_h(k, s, m, c):
                    b = chain_bank(pe, k)
                    pe.wait_ge(act_done, count("act", (s, "ln_t", LN_OF_MLP[m])))
                    pe.matmul(b[:, :], w_m1[m][:, c * P:(c + 1) * P], xt[s][:, :], start=True, stop=True).then_inc(pe_done, 1)

                def mlp_out(k, s, m):
                    b = chain_bank(pe, k)
                    pe.wait_ge(act_done, count("act", (s, "mlp_h", m, FC - 1)))
                    for t in range(TB):
                        for c in range(FC):
                            ins = pe.matmul(b[:, t * D:(t + 1) * D], hid[s][:, c, t * P:(t + 1) * P], w_m2[m][:, c, :],
                                            start=(c == 0), stop=(c == FC - 1))
                    ins.then_inc(pe_done, 1)

                parts = locals()
                for step in PLAN:
                    if "pe" in STEPS[step[1]]:
                        parts[step[1]](step, step[0], *step[2:])


def layout(inputs):
    a = {name: np.asarray(v) for name, v in inputs.items()}
    L0, L1, L2, L3 = (lambda name, l=l: a[f"L{l}_xcond_{name}"] for l in range(4))

    def chunks(m):
        return m.reshape(-1, P, m.shape[-1]).transpose(1, 0, 2).reshape(P, -1)

    def vector(v):
        return v.reshape(-1, P).T

    e_w1, e_w2 = L1("e_w1"), L1("e_w2")
    tail = np.zeros((P, 2), np.float32)
    for part in range(3):
        for e in range(2):
            tail[MROW + 2 * part + e, e] = 1.0
    cols = np.zeros((P, 32), np.float32)
    for c, v in ((C_NW, L0("norm1_w")), (C_NW + 1, L0("normc_w")), (C_NW + 2, L0("norm2_w")), (C_GB, L1("ln_gamma")),
                 (C_GB + 1, L1("ln_beta")), (C_M1[0], L0("mlp_b1")), (C_M1[1], L3("b_mlp1")), (C_E1, L1("e_b1")),
                 (C_G1, L1("gate_b1")), (C_Q2, L2("bq")), (C_K2, L2("bkv")), (C_QKV3, L3("b_qkv")), (C_QC, L3("b_qc")),
                 (C_KVC, L3("b_kvc"))):
        cols[:, c:c + v.size // P] = vector(v)
    parts = {
        "w_ada": L0("adaLN_W"), "w_ssq": L2("Wss_q"), "w_sskv": L2("Wss_kv"), "w_mod": L3("W_mod"), "w_out": L1("out_w"),
        "w_anchor": np.concatenate([chunks(e_w1[e, 2 * D:]) for e in range(E)] + [L1("gate_w1")[2 * D:]], axis=1),
        "w_e2": chunks(e_w2.reshape(-1, D)),
        "cols": cols, "e_b2": L1("e_b2").T, "ident": np.eye(P, dtype=np.float32), "tail": tail,
        "mod_b": vector(np.concatenate([L0("adaLN_b"), L2("bss_q"), L2("bss_kv"), L3("b_mod")])),
        "w_rt": chunks(L1("router_W")), "w_qkv0": L0("qkv_W"), "w_o0": L0("attn_out_W"), "w_co": L0("co_W"),
        "w_p2": L2("Wp"), "w_pr3": L3("W_proj"), "w_cp3": L3("W_cproj"), "w_ck": L0("ck_W"), "w_k1": L1("Wk"),
        "w_cv": L0("cv_W"), "w_v1": L1("Wv"), "w_kv2": L2("Wkv"), "w_kvc3": L3("W_kvc"),
        "w_cq": L0("cq_W"), "w_m10": L0("mlp_W1"), "w_m20": chunks(L0("mlp_W2")), "w_q1": L1("Wq"),
        "w_e1": e_w1[:, :2 * D].reshape(E, 2, P, RH).transpose(2, 1, 0, 3).reshape(P, -1),
        "w_g1": chunks(L1("gate_w1")[:2 * D]), "w_g2": L1("gate_w2"), "w_q2": L2("Wq"), "w_qkv3": L3("W_qkv"),
        "w_qc3": L3("W_qc"), "w_m11": L3("W_mlp1"), "w_m21": chunks(L3("W_mlp2")),
    }
    n = T // 2
    inv_freq = 1.0 / 10000.0 ** (np.arange(0, HD, 2, dtype=np.float32) / HD)
    freqs = np.outer(np.arange(n, dtype=np.float32), inv_freq)
    emb = np.concatenate([freqs, freqs], axis=-1)

    def rotation(f):
        return np.tile(f(emb).astype(np.float32).T, (H, 1))

    arrays = {name: a[name] for name in ("x", "ctx_1024", "mask_BxS2_bf1", "mask_SxS_bk0", "L1_xcond_router_b")}
    arrays["cond_t"] = a["cond_1024"].T
    arrays["bias_rows"] = np.stack([L2("bp"), L3("b_proj"), L3("b_cproj"), L1("out_b")])
    arrays["mlp_bias"] = np.stack([L0("mlp_b2"), L3("b_mlp2")])
    arrays["gate_bias"] = L1("gate_b2")[None]
    for name, table in (("setup_w", SETUP_W), ("early_w", EARLY_W), ("late_w", LATE_W)):
        arrays[name] = np.concatenate([parts[part] for part, _ in table], axis=1)
    arrays["c_cos"], arrays["c_sin"] = rotation(np.cos), rotation(np.sin)
    return {name: np.ascontiguousarray(v) for name, v in arrays.items()}


def kernel(**inputs):
    import concourse.bacc as bacc
    from concourse.bass_utils import run_bass_kernel_spmd

    nc = bacc.Bacc("TRN2", target_bir_lowering=False, num_devices=1)
    arrays = layout(inputs)
    io = {name: nc.dram_tensor(name, v.shape, mybir.dt.from_np(v.dtype), kind="ExternalInput").ap() for name, v in arrays.items()}
    out = nc.dram_tensor("out", [B, T, D], F32, kind="ExternalOutput").ap()
    build(nc, io, out)
    r = run_bass_kernel_spmd(nc, [arrays], core_ids=[0])
    return r.results[0]["out"]
```
